# Optimizing a Trainium2 kernel written in Bass

```python
import numpy as np
import jax
import jax.numpy as jnp

def _softmax(x, axis=-1):
    return jax.nn.softmax(x, axis=axis)

def _gelu(x):
    return jax.nn.gelu(x, approximate=True)

def _silu(x):
    return jax.nn.silu(x)

def _sigmoid(x):
    return jax.nn.sigmoid(x)

def _layernorm(x, axis=-1, eps=1e-05):
    m = jnp.mean(x, axis=axis, keepdims=True)
    v = jnp.var(x, axis=axis, keepdims=True)
    return (x - m) / jnp.sqrt(v + eps)

def _scatter_add(tgt, idx, src, axis=0):
    return tgt.at[idx].add(src)

def _segment_sum(src, seg, n):
    return jax.ops.segment_sum(src, seg, n)
kernel_name = 'mk_gnn_preln_d4_gnn_r32_aec227'

def setup_inputs(seed: int=0):
    np.random.seed(seed)
    _w = jnp.asarray

    def _rec_inputs():
        import jax
        import jax.numpy as jnp
        _gk = jax.random.key(seed)
        x = -0.000202 + 1 * jax.random.normal(jax.random.fold_in(_gk, 1), (3125, 64), jnp.float32)
        _s = jax.random.randint(jax.random.fold_in(_gk, 2), (50000,), 0, 3125, jnp.int32)
        _d = jax.random.randint(jax.random.fold_in(_gk, 3), (50000,), 0, 3125, jnp.int32)
        _loop = jnp.arange(3125, dtype=jnp.int32)
        src = jnp.concatenate([_s, _d, _loop])
        dst = jnp.concatenate([_d, _s, _loop])
        _o = jnp.argsort(dst, stable=True)
        src = src[_o]
        dst = dst[_o]
        edge_attr_8 = 0.000254156 + 0.999948 * jax.random.normal(jax.random.fold_in(_gk, 12), (103125, 8), jnp.float32)
        edge_type_16 = jax.random.randint(jax.random.fold_in(_gk, 14), (103125,), 0, 16, jnp.int32)
        return (x, src, dst, edge_attr_8, edge_type_16)
    x, src, dst, edge_attr_8, edge_type_16 = _rec_inputs()

    def _L0_gnn_setup():
        import jax, jax.numpy as jnp
        import numpy as np
        N = 3125
        E = 50000
        DIN = 64
        DOUT = 64
        EPS = 1e-12

        def _sage_conv(x, src, dst, Wl, bl, Wr):
            agg = jax.ops.segment_sum(x[src], dst, num_segments=N)
            return agg @ Wl.T + bl + x @ Wr.T
        key = jax.random.key(seed)
        ks = jax.random.split(key, 10)
        x = jax.random.normal(ks[0], (N, DIN), dtype=jnp.float32)
        edge_index = jax.random.randint(ks[1], (2, E), 0, N, dtype=jnp.int32)
        edge_feature = jax.random.normal(ks[2], (E, 8), dtype=jnp.float32)
        s_in = 1.0 / np.sqrt(DIN)
        s_out = 1.0 / np.sqrt(DOUT)
        W1l = jax.random.uniform(ks[3], (DOUT, DIN), jnp.float32, -s_in, s_in)
        b1l = jax.random.uniform(ks[4], (DOUT,), jnp.float32, -s_in, s_in)
        W1r = jax.random.uniform(ks[5], (DOUT, DIN), jnp.float32, -s_in, s_in)
        W2l = jax.random.uniform(ks[6], (DOUT, DOUT), jnp.float32, -s_out, s_out)
        b2l = jax.random.uniform(ks[7], (DOUT,), jnp.float32, -s_out, s_out)
        W2r = jax.random.uniform(ks[8], (DOUT, DOUT), jnp.float32, -s_out, s_out)
        return {'x': x, 'edge_index': edge_index, 'edge_feature': edge_feature, 'W1l': W1l, 'b1l': b1l, 'W1r': W1r, 'W2l': W2l, 'b2l': b2l, 'W2r': W2r}
    _L0_gnn_all = _L0_gnn_setup()
    _L0_gnn_in = {k: v for k, v in _L0_gnn_all.items() if k in ('W1l', 'b1l', 'W1r', 'W2l', 'b2l', 'W2r')}
    del _L0_gnn_all

    def _L1_gnn_setup():
        import jax, jax.numpy as jnp
        import numpy as np
        N_NODES = 50000
        N_EDGES = 25000
        D_IN = 64
        D_OUT = 64
        NUM_RELS = 16
        key = jax.random.key(seed)
        k1, k2, k3, k4, k5 = jax.random.split(key, 5)
        feat = jax.random.normal(k1, (N_NODES, D_IN), dtype=jnp.float32)
        weight = jax.random.normal(k2, (NUM_RELS, D_IN, D_OUT), dtype=jnp.float32) * 0.05
        src = jax.random.randint(k3, (N_EDGES,), 0, N_NODES, dtype=jnp.int32)
        dst = jax.random.randint(k4, (N_EDGES,), 0, N_NODES, dtype=jnp.int32)
        etypes = jax.random.randint(k5, (N_EDGES,), 0, NUM_RELS, dtype=jnp.int32)
        return {'feat': feat, 'weight': weight, 'src': src, 'dst': dst, 'etypes': etypes}
    _L1_gnn_all = _L1_gnn_setup()
    _L1_gnn_in = {k: v for k, v in _L1_gnn_all.items() if k in ('weight',)}
    del _L1_gnn_all

    def _L2_gnn_setup():
        import jax, jax.numpy as jnp
        import numpy as np
        N_NODES = 50000
        N_EDGES = 25000
        D = 64
        NEG_SLOPE = 0.2

        def _gat_conv(x, src, dst, W, a_src, a_dst, b, n_nodes):
            h = x @ W
            alpha_s = h @ a_src
            alpha_d = h @ a_dst
            e = alpha_s[src] + alpha_d[dst]
            e = jnp.where(e > 0, e, NEG_SLOPE * e)
            m = jax.ops.segment_max(e, dst, num_segments=n_nodes)
            m = jnp.where(jnp.isfinite(m), m, 0.0)
            ex = jnp.exp(e - m[dst])
            s = jax.ops.segment_sum(ex, dst, num_segments=n_nodes)
            alpha = ex / (s[dst] + 1e-16)
            out = jax.ops.segment_sum(alpha[:, None] * h[src], dst, num_segments=n_nodes)
            return out + b

        def _add_self_loops(edge_index, n_nodes):
            loop = jnp.arange(n_nodes, dtype=edge_index.dtype)
            src = jnp.concatenate([edge_index[0], loop])
            dst = jnp.concatenate([edge_index[1], loop])
            return (src, dst)
        key = jax.random.key(seed)
        ks = jax.random.split(key, 16)
        x = jax.random.normal(ks[0], (N_NODES, D), dtype=jnp.float32)
        edge_index = jax.random.randint(ks[1], (2, N_EDGES), 0, N_NODES, dtype=jnp.int32)
        sc = 1.0 / np.sqrt(D)

        def lin(k):
            return jax.random.uniform(k, (D, D), jnp.float32, -sc, sc)

        def att(k):
            return jax.random.uniform(k, (D,), jnp.float32, -sc, sc)
        return {'x': x, 'edge_index': edge_index, 'W1': lin(ks[2]), 'a1s': att(ks[3]), 'a1d': att(ks[4]), 'b1': jnp.zeros((D,), jnp.float32), 'W2': lin(ks[5]), 'a2s': att(ks[6]), 'a2d': att(ks[7]), 'b2': jnp.zeros((D,), jnp.float32), 'W3': lin(ks[8]), 'a3s': att(ks[9]), 'a3d': att(ks[10]), 'b3': jnp.zeros((D,), jnp.float32)}
    _L2_gnn_all = _L2_gnn_setup()
    _L2_gnn_in = {k: v for k, v in _L2_gnn_all.items() if k in ('W1', 'a1s', 'a1d', 'b1', 'W2', 'a2s', 'a2d', 'b2', 'W3', 'a3s', 'a3d', 'b3')}
    del _L2_gnn_all

    def _L3_gnn_setup():
        import jax, jax.numpy as jnp
        import numpy as np
        N_NODES = 3125
        IN_DIM = 64
        HID = 64
        N_EDGES = 50000
        EPS = 1e-05
        SLOPE = 0.01

        def _glorot(key, shape):
            fan_in, fan_out = (shape[1], shape[0])
            lim = jnp.sqrt(6.0 / (fan_in + fan_out))
            return jax.random.uniform(key, shape, jnp.float32, -lim, lim)

        def _sage_mean(h, src, dst, W_self, W_neigh, b):
            msg_sum = jax.ops.segment_sum(h[src], dst, num_segments=N_NODES)
            deg = jax.ops.segment_sum(jnp.ones_like(dst, jnp.float32), dst, num_segments=N_NODES)
            h_neigh = msg_sum / jnp.maximum(deg, 1.0)[:, None]
            return h @ W_self.T + h_neigh @ W_neigh.T + b

        def _bn(h, gamma, beta):
            mu = jnp.mean(h, axis=0)
            var = jnp.mean(jnp.square(h - mu), axis=0)
            return (h - mu) * jax.lax.rsqrt(var + EPS) * gamma + beta
        key = jax.random.key(seed)
        ks = jax.random.split(key, 8)
        x = jax.random.normal(ks[0], (N_NODES, IN_DIM), jnp.float32)
        src = jax.random.randint(ks[1], (N_EDGES,), 0, N_NODES, jnp.int32)
        dst = jax.random.randint(ks[2], (N_EDGES,), 0, N_NODES, jnp.int32)
        edge_index = jnp.stack([src, dst])
        return {'x': x, 'edge_index': edge_index, 'W_self1': _glorot(ks[3], (HID, IN_DIM)), 'W_neigh1': _glorot(ks[4], (HID, IN_DIM)), 'b1': jnp.zeros((HID,), jnp.float32), 'gamma1': jnp.ones((HID,), jnp.float32), 'beta1': jnp.zeros((HID,), jnp.float32), 'W_self2': _glorot(ks[5], (HID, HID)), 'W_neigh2': _glorot(ks[6], (HID, HID)), 'b2': jnp.zeros((HID,), jnp.float32), 'gamma2': jnp.ones((HID,), jnp.float32), 'beta2': jnp.zeros((HID,), jnp.float32)}
    _L3_gnn_all = _L3_gnn_setup()
    _L3_gnn_in = {k: v for k, v in _L3_gnn_all.items() if k in ('W_self1', 'W_neigh1', 'b1', 'gamma1', 'beta1', 'W_self2', 'W_neigh2', 'b2', 'gamma2', 'beta2')}
    del _L3_gnn_all
    return {'x': x, 'src': src, 'dst': dst, 'edge_attr_8': edge_attr_8, 'edge_type_16': edge_type_16, 'L0_gnn_W1l': _L0_gnn_in['W1l'], 'L0_gnn_b1l': _L0_gnn_in['b1l'], 'L0_gnn_W1r': _L0_gnn_in['W1r'], 'L0_gnn_W2l': _L0_gnn_in['W2l'], 'L0_gnn_b2l': _L0_gnn_in['b2l'], 'L0_gnn_W2r': _L0_gnn_in['W2r'], 'L1_gnn_weight': _L1_gnn_in['weight'], 'L2_gnn_W1': _L2_gnn_in['W1'], 'L2_gnn_a1s': _L2_gnn_in['a1s'], 'L2_gnn_a1d': _L2_gnn_in['a1d'], 'L2_gnn_b1': _L2_gnn_in['b1'], 'L2_gnn_W2': _L2_gnn_in['W2'], 'L2_gnn_a2s': _L2_gnn_in['a2s'], 'L2_gnn_a2d': _L2_gnn_in['a2d'], 'L2_gnn_b2': _L2_gnn_in['b2'], 'L2_gnn_W3': _L2_gnn_in['W3'], 'L2_gnn_a3s': _L2_gnn_in['a3s'], 'L2_gnn_a3d': _L2_gnn_in['a3d'], 'L2_gnn_b3': _L2_gnn_in['b3'], 'L3_gnn_W_self1': _L3_gnn_in['W_self1'], 'L3_gnn_W_neigh1': _L3_gnn_in['W_neigh1'], 'L3_gnn_b1': _L3_gnn_in['b1'], 'L3_gnn_gamma1': _L3_gnn_in['gamma1'], 'L3_gnn_beta1': _L3_gnn_in['beta1'], 'L3_gnn_W_self2': _L3_gnn_in['W_self2'], 'L3_gnn_W_neigh2': _L3_gnn_in['W_neigh2'], 'L3_gnn_b2': _L3_gnn_in['b2'], 'L3_gnn_gamma2': _L3_gnn_in['gamma2'], 'L3_gnn_beta2': _L3_gnn_in['beta2']}

def reference(x, src, dst, edge_attr_8, edge_type_16, L0_gnn_W1l, L0_gnn_b1l, L0_gnn_W1r, L0_gnn_W2l, L0_gnn_b2l, L0_gnn_W2r, L1_gnn_weight, L2_gnn_W1, L2_gnn_a1s, L2_gnn_a1d, L2_gnn_b1, L2_gnn_W2, L2_gnn_a2s, L2_gnn_a2d, L2_gnn_b2, L2_gnn_W3, L2_gnn_a3s, L2_gnn_a3d, L2_gnn_b3, L3_gnn_W_self1, L3_gnn_W_neigh1, L3_gnn_b1, L3_gnn_gamma1, L3_gnn_beta1, L3_gnn_W_self2, L3_gnn_W_neigh2, L3_gnn_b2, L3_gnn_gamma2, L3_gnn_beta2):
    import jax
    import jax.numpy as jnp

    def _L0_gnn_ref(x, edge_index, edge_feature, W1l, b1l, W1r, W2l, b2l, W2r):
        import jax, jax.numpy as jnp
        import numpy as np
        N = 3125
        E = 50000
        DIN = 64
        DOUT = 64
        EPS = 1e-12

        def _sage_conv(x, src, dst, Wl, bl, Wr):
            agg = jax.ops.segment_sum(x[src], dst, num_segments=N)
            return agg @ Wl.T + bl + x @ Wr.T
        src, dst = (edge_index[0], edge_index[1])
        h = _sage_conv(x, src, dst, W1l, b1l, W1r)
        h = jax.nn.relu(h)
        nrm = jnp.linalg.norm(h, axis=-1, keepdims=True)
        h = h / jnp.maximum(nrm, EPS)
        out = _sage_conv(h, src, dst, W2l, b2l, W2r)
        return out

    def _L1_gnn_ref(feat, weight, src, dst, etypes):
        import jax, jax.numpy as jnp
        import numpy as np
        N_NODES = 50000
        N_EDGES = 25000
        D_IN = 64
        D_OUT = 64
        NUM_RELS = 16
        num_rels = weight.shape[0]
        h_src = feat[src]
        msg = jnp.zeros((h_src.shape[0], weight.shape[2]), dtype=feat.dtype)
        for r in range(num_rels):
            mask = etypes == r
            msg = msg + h_src * mask[:, None].astype(feat.dtype) @ weight[r]
        out = jax.ops.segment_sum(msg, dst, num_segments=feat.shape[0])
        return out

    def _L2_gnn_ref(x, edge_index, W1, a1s, a1d, b1, W2, a2s, a2d, b2, W3, a3s, a3d, b3):
        import jax, jax.numpy as jnp
        import numpy as np
        N_NODES = 50000
        N_EDGES = 25000
        D = 64
        NEG_SLOPE = 0.2

        def _gat_conv(x, src, dst, W, a_src, a_dst, b, n_nodes):
            h = x @ W
            alpha_s = h @ a_src
            alpha_d = h @ a_dst
            e = alpha_s[src] + alpha_d[dst]
            e = jnp.where(e > 0, e, NEG_SLOPE * e)
            m = jax.ops.segment_max(e, dst, num_segments=n_nodes)
            m = jnp.where(jnp.isfinite(m), m, 0.0)
            ex = jnp.exp(e - m[dst])
            s = jax.ops.segment_sum(ex, dst, num_segments=n_nodes)
            alpha = ex / (s[dst] + 1e-16)
            out = jax.ops.segment_sum(alpha[:, None] * h[src], dst, num_segments=n_nodes)
            return out + b

        def _add_self_loops(edge_index, n_nodes):
            loop = jnp.arange(n_nodes, dtype=edge_index.dtype)
            src = jnp.concatenate([edge_index[0], loop])
            dst = jnp.concatenate([edge_index[1], loop])
            return (src, dst)
        n = x.shape[0]
        src, dst = _add_self_loops(edge_index, n)
        h = _gat_conv(x, src, dst, W1, a1s, a1d, b1, n)
        h = jax.nn.relu(h)
        h = _gat_conv(h, src, dst, W2, a2s, a2d, b2, n)
        h = jax.nn.relu(h)
        return _gat_conv(h, src, dst, W3, a3s, a3d, b3, n)

    def _L3_gnn_ref(x, edge_index, W_self1, W_neigh1, b1, gamma1, beta1, W_self2, W_neigh2, b2, gamma2, beta2):
        import jax, jax.numpy as jnp
        import numpy as np
        N_NODES = 3125
        IN_DIM = 64
        HID = 64
        N_EDGES = 50000
        EPS = 1e-05
        SLOPE = 0.01

        def _glorot(key, shape):
            fan_in, fan_out = (shape[1], shape[0])
            lim = jnp.sqrt(6.0 / (fan_in + fan_out))
            return jax.random.uniform(key, shape, jnp.float32, -lim, lim)

        def _sage_mean(h, src, dst, W_self, W_neigh, b):
            msg_sum = jax.ops.segment_sum(h[src], dst, num_segments=N_NODES)
            deg = jax.ops.segment_sum(jnp.ones_like(dst, jnp.float32), dst, num_segments=N_NODES)
            h_neigh = msg_sum / jnp.maximum(deg, 1.0)[:, None]
            return h @ W_self.T + h_neigh @ W_neigh.T + b

        def _bn(h, gamma, beta):
            mu = jnp.mean(h, axis=0)
            var = jnp.mean(jnp.square(h - mu), axis=0)
            return (h - mu) * jax.lax.rsqrt(var + EPS) * gamma + beta
        src, dst = (edge_index[0], edge_index[1])
        h = _sage_mean(x, src, dst, W_self1, W_neigh1, b1)
        h = jax.nn.leaky_relu(_bn(h, gamma1, beta1), SLOPE)
        h = _sage_mean(h, src, dst, W_self2, W_neigh2, b2)
        h = jax.nn.leaky_relu(_bn(h, gamma2, beta2), SLOPE)
        return h
    edge_index = jnp.stack([src, dst])
    h = jnp.maximum(_layernorm(x, axis=-1), 0.0)
    x = x + _L0_gnn_ref(h, edge_index, edge_attr_8, L0_gnn_W1l, L0_gnn_b1l, L0_gnn_W1r, L0_gnn_W2l, L0_gnn_b2l, L0_gnn_W2r)
    h = jnp.maximum(_layernorm(x, axis=-1), 0.0)
    x = x + _L1_gnn_ref(h, L1_gnn_weight, src, dst, edge_type_16)
    h = jnp.maximum(_layernorm(x, axis=-1), 0.0)
    x = x + _L2_gnn_ref(h, edge_index, L2_gnn_W1, L2_gnn_a1s, L2_gnn_a1d, L2_gnn_b1, L2_gnn_W2, L2_gnn_a2s, L2_gnn_a2d, L2_gnn_b2, L2_gnn_W3, L2_gnn_a3s, L2_gnn_a3d, L2_gnn_b3)
    h = jnp.maximum(_layernorm(x, axis=-1), 0.0)
    x = x + _L3_gnn_ref(h, edge_index, L3_gnn_W_self1, L3_gnn_W_neigh1, L3_gnn_b1, L3_gnn_gamma1, L3_gnn_beta1, L3_gnn_W_self2, L3_gnn_W_neigh2, L3_gnn_b2, L3_gnn_gamma2, L3_gnn_beta2)
    return x

_drawn_inputs = setup_inputs


def setup_inputs(seed=0):
    import zlib

    import numpy as np

    out = dict(_drawn_inputs(seed))
    spreads = {'L2_gnn_b1': (0.0, 0.8),
     'L2_gnn_b2': (0.0, 0.757),
     'L2_gnn_b3': (0.0, 0.282),
     'L3_gnn_b1': (0.0, 2.0),
     'L3_gnn_gamma1': (1.0, 0.6),
     'L3_gnn_beta1': (0.0, 0.548),
     'L3_gnn_b2': (0.0, 2.0),
     'L3_gnn_gamma2': (1.0, 0.6),
     'L3_gnn_beta2': (0.0, 0.449)}
    factors = {'L0_gnn_b1l': 5.374,
     'L2_gnn_W1': 5.837,
     'L2_gnn_a1s': 8.0,
     'L2_gnn_a1d': 64.0,
     'L2_gnn_W2': 4.089,
     'L2_gnn_a2s': 8.0,
     'L2_gnn_a2d': 8.0,
     'L2_gnn_W3': 2.906,
     'L2_gnn_a3s': 8.0,
     'L2_gnn_a3d': 8.0}
    for name, (base, spread) in spreads.items():
        noise = np.random.default_rng([zlib.crc32(name.encode()), seed]).standard_normal(out[name].shape)
        drawn = base * np.exp(spread * noise) if base else spread * noise
        out[name] = jnp.asarray(drawn.astype(out[name].dtype))
    for name, factor in factors.items():
        out[name] = (out[name] * factor).astype(out[name].dtype)
    return out
```

```python
import concourse.bass as bass
from concourse import mybir
from contextlib import ExitStack

FP32 = mybir.dt.float32
FP16 = mybir.dt.float16
BF16 = mybir.dt.bfloat16
I32 = mybir.dt.int32
U32 = mybir.dt.uint32
ALU = mybir.AluOpType
ACT = mybir.ActivationFunctionType
AX = mybir.AxisListType

N = 3125
D = 64
E = 103125
P = 125
NT = N // P
NC = 5
TC = NT // NC
CW = N // NC
ET = 128
GT = 4
GE = ET * GT
G = -(-E // GE)
W = 20
AW = N + W
R = 16
PAD_DST = 1 << 20
MAGIC = 12582912.0
LO_SCALE = 2048.0
LN_EPS = 1e-5

MATS = ["L0_W1l", "L0_W1r", "L0_W2l", "L0_W2r", "G_W1", "G_W2", "G_W3", "S_self1", "S_neigh1", "S_self2", "S_neigh2"]
VECS = ["L0_b1", "L0_b2", "G_as1", "G_as2", "G_as3", "G_ad1", "G_ad2", "G_ad3", "G_b1", "G_b2", "G_b3",
        "S_b1", "S_gamma1", "S_beta1", "S_b2", "S_gamma2", "S_beta2"]
STOP = "L3"


class Chain:

    def __init__(self, eng, sem):
        self.eng, self.sem, self.count = eng, sem, 0

    def __call__(self, ins):
        ins.then_inc(self.sem, 1)
        self.count += 1
        self.eng.wait_ge(self.sem, self.count)
        return ins


def gnn(nc, x_in, dst_groups, src_tiles, dst_tiles, type_tiles, mats_in, vecs_in, rel_in, out):
    ctx = ExitStack()
    with ctx:
        names = set()

        def sem(name):
            assert name not in names, name
            names.add(name)
            return ctx.enter_context(nc.semaphore(name))

        def sb(name, shape, dt, scope=None):
            return (scope or ctx).enter_context(nc.sbuf_tensor(name, shape, dt))

        adj = sb("adj", [P, NT, AW], FP16)
        x_sb = sb("x_sb", [P, NT, D], FP32)
        mats = sb("mats", [128, len(MATS), D], FP32)
        vecs = sb("vecs", [P, len(VECS), D], FP32)
        ident = sb("ident", [128, 128], FP32)
        ones = sb("ones", [128, 128], FP32)
        deg = sb("deg", [P, NT], FP32)
        stat = sb("stat", [P, 4, NT], FP32)
        psum = ctx.enter_context(nc.psum_tensor("psum", [128, 8, 512], FP32))

        def mat(name, rows=D):
            return mats[0:rows, MATS.index(name), :]

        def vec(name):
            return vecs[:, VECS.index(name), :]

        def over_tiles(ap2, n=NT):
            return ap2.unsqueeze(1).to_broadcast([P, n, D])

        def over_features(ap2, n=NT, d=D):
            return ap2.unsqueeze(2).to_broadcast([P, n, d])

        edge_scope = ExitStack()
        base_row = sb("base_row", [1, 2 * 128], I32, edge_scope)
        basef_row = sb("basef_row", [1, 2 * 128], FP32, edge_scope)
        d_tab = sb("d_tab", [128, G * GT], FP32, edge_scope)
        gather_idx = sb("gather_idx", [128, G * GT], U32, edge_scope)
        npass = sb("npass", [128, 1], I32, edge_scope)
        pass_off = sb("pass_off", [128, 1], FP32, edge_scope)

        build_scope = ExitStack()
        lo_tab = sb("lo_tab", [128, G * GT], FP32, build_scope)
        hi_tab = sb("hi_tab", [128, G * GT], FP32, build_scope)
        c_tab = sb("c_tab", [128, G * GT], FP32, build_scope)
        iota_i = sb("iota_i", [128, W * NT], I32, build_scope)
        iota_h = sb("iota_h", [128, W * NT], FP16, build_scope)

        prep_scope = ExitStack()
        dg_i = sb("dg_i", [128, 2, GE], I32, prep_scope)
        dg = dg_i[:, :, :].bitcast(FP32)
        dv = sb("dv", [128, 2, GE], FP32, prep_scope)
        ti = sb("ti", [128, 3, G * GT], I32, prep_scope)
        tf = ti[:, :, :].bitcast(FP32)
        gstat = sb("gstat", [128, 4, 2], FP32, prep_scope)
        diag = sb("diag", [128, 2, 128], FP32, prep_scope)

        s_dg, s_ti, s_x, s_mats, s_mats2, s_vecs = (sem(n) for n in (
            "dst_groups_in", "edge_tiles_in", "x_in_done", "mats_in_done", "mats_twice_done", "vecs_in_done"))
        s_zeroed = sem("adj_zeroed")
        s_iota, s_ident, s_ident2 = sem("iota_ready"), sem("ident_zeroed"), sem("ident_ready")
        s_chain, s_diag, s_basebc, s_span, s_spanall = (sem(n) for n in (
            "prep_chain", "diag_ready", "base_broadcast", "span_ready", "span_over_partitions"))

        block = nc.Block()
        with block as block:
            @block.sync
            def _(sp):
                sp.dma_start(dg_i[:, :, :], dst_groups).then_inc(s_dg, 16)
                sp.dma_start(ti[:, 1, :], dst_tiles).then_inc(s_ti, 16)
                sp.dma_start(ti[:, 0, :], src_tiles).then_inc(s_ti, 16)
                sp.dma_start(ti[:, 2, :], type_tiles).then_inc(s_ti, 16)
                sp.dma_start(x_sb[:, :, :], x_in).then_inc(s_x, 16)
                sp.dma_start(mats[0:D, :, :], mats_in).then_inc(s_mats, 16)
                sp.dma_start(mats[D:2 * D, :, :], mats_in).then_inc(s_mats2, 16)
                sp.dma_start(vecs[:, :, :], vecs_in.to_broadcast([P, len(VECS) * D])).then_inc(s_vecs, 16)
                for s in (s_mats, s_mats2, s_vecs, s_x):
                    sp.wait_ge(s, 16)

            @block.gpsimd
            def _(pool):
                pool.iota(iota_i[:, :], pattern=[[1, W * NT]], base=0, channel_multiplier=0).then_inc(s_iota, 1)
                pool.memset(ident[:, :], 0.0).then_inc(s_ident, 1)
                pool.memset(ones[:, :], 1.0).then_inc(s_ident2, 1)
                pool.memset(adj[:, NT // 2:NT, :], 0.0).then_inc(s_zeroed, 1)
                pool.wait_ge(s_zeroed, 1)
                pool.wait_ge(s_ident, 1)
                pool.affine_select(out=ident[:, :], in_=ident[:, :], compare_op=ALU.not_equal, fill=1.0, base=0,
                                   pattern=[[-1, 128]], channel_multiplier=1).then_inc(s_ident2, 1)
                pool.wait_ge(s_span, 1)
                pool.partition_all_reduce(gstat[:, 3, 1:2], gstat[:, 3, 0:1], 128,
                                          bass.bass_isa.ReduceOp.max).then_inc(s_spanall, 1)

            @block.tensor
            def _(pe):
                pe.wait_ge(s_ident2, 2)
                pe.wait_ge(s_diag, 2)
                pe.matmul(psum[:, 0, 0:256], ones[:, :], diag[:, :, :], start=True, stop=True).then_inc(s_basebc, 1)

            @block.vector
            def _(dve):
                link = Chain(dve, s_chain)
                v = nc.vector
                link(v.memset(adj[:, 0:NT // 2, :], 0.0))
                link(v.memset(pass_off[:, :], 0.0))
                dve.wait_ge(s_iota, 1)
                link(v.tensor_copy(iota_h[:, :], iota_i[:, :]))
                dve.wait_ge(s_dg, 16)
                link(v.tensor_copy(dg[:, :, :], dg_i[:, :, :]))
                link(v.tensor_reduce(gstat[:, 0, :], dg[:, :, :], AX.X, ALU.min))
                dve.wait_ge(s_ident2, 2)
                for k in range(2):
                    v.tensor_scalar(diag[:, k, :], ident[:, :], gstat[:, 0, k:k + 1], None, ALU.mult).then_inc(s_diag, 1)
                link(v.scalar_tensor_tensor(dv[:, :, :], dg[:, :, :], float(N), dg[:, :, :], ALU.is_lt, ALU.mult))
                link(v.tensor_reduce(gstat[:, 1, :], dv[:, :, :], AX.X, ALU.max))
                link(v.tensor_tensor(gstat[:, 2, :], gstat[:, 1, :], gstat[:, 0, :], ALU.subtract))
                v.tensor_reduce(gstat[:, 3, 0:1], gstat[:, 2, :], AX.X, ALU.max).then_inc(s_span, 1)
                dve.wait_ge(s_ti, 48)
                link(v.tensor_copy(tf[:, :, :], ti[:, :, :]))
                link(v.scalar_tensor_tensor(gather_idx[:, :], tf[:, 0, :], float(R), tf[:, 2, :], ALU.mult, ALU.add))
                link(v.tensor_scalar(hi_tab[:, :], tf[:, 0, :], 1.0 / P, 0.5 / P - 0.5, ALU.mult, ALU.add))
                link(v.tensor_scalar(hi_tab[:, :], hi_tab[:, :], MAGIC, -MAGIC, ALU.add, ALU.add))
                link(v.scalar_tensor_tensor(lo_tab[:, :], hi_tab[:, :], -float(P), tf[:, 0, :], ALU.mult, ALU.add))
                link(v.tensor_scalar(hi_tab[:, :], hi_tab[:, :], float(W), None, ALU.mult))
                dve.wait_ge(s_basebc, 1)
                link(v.tensor_copy(basef_row[:, :], psum[0:1, 0, 0:256]))
                link(v.tensor_tensor(d_tab[:, :].rearrange("p (g t) -> p g t", t=GT),
                                     tf[:, 1, :].rearrange("p (g t) -> p g t", t=GT),
                                     psum[:, 0, 0:G].unsqueeze(2).to_broadcast([128, G, GT]), ALU.subtract))
                dve.wait_ge(s_spanall, 1)
                link(v.tensor_scalar(gstat[:, 2, 0:1], gstat[:, 3, 1:2], 1.0 / W, 0.5 / W - 0.5, ALU.mult, ALU.add))
                link(v.tensor_scalar(gstat[:, 2, 1:2], gstat[:, 2, 0:1], MAGIC, -MAGIC, ALU.add, ALU.add))
                link(v.tensor_scalar(npass[:, :], gstat[:, 2, 1:2], 1.0, None, ALU.add))
        prep_scope.close()

        src_hot = sb("src_hot", [128, 2, GT, 128], BF16, build_scope)
        col_hot = sb("col_hot", [128, 2, GT, W * NT], BF16, build_scope)
        cv = sb("cv", [128, 2, G * GT], FP32, build_scope)
        s_bchain, s_hot, s_outer, s_added = (sem(n) for n in ("build_chain", "one_hots_ready", "outer_done", "window_added"))

        passes = nc.values_load(npass[0:1, 0:1], min_val=1, max_val=N // W + 1)
        with nc.Fori(0, passes):
            with nc.Block() as block:
                @block.vector
                def _(dve):
                    v = nc.vector
                    link = Chain(dve, s_bchain)
                    dw = cv[:, 0, :]
                    inside = cv[:, 1, :]
                    link(v.tensor_scalar(dw, d_tab[:, :], pass_off[:, 0:1], None, ALU.subtract))
                    link(v.tensor_scalar(inside, dw, 0.0, None, ALU.is_ge))
                    link(v.scalar_tensor_tensor(inside, dw, float(W), inside, ALU.is_lt, ALU.mult))
                    link(v.scalar_tensor_tensor(c_tab[:, :], dw, 1.0, hi_tab[:, :], ALU.add, ALU.add))
                    link(v.tensor_tensor(c_tab[:, :], c_tab[:, :], inside, ALU.mult))
                    link(v.tensor_scalar(c_tab[:, :], c_tab[:, :], -1.0, None, ALU.add))
                    link(v.tensor_scalar(base_row[:, :], basef_row[:, :], pass_off[0:1, 0:1], float(N), ALU.add, ALU.min))

                    def one_hots(g, half):
                        for t in range(GT):
                            e = g * GT + t
                            v.tensor_scalar(col_hot[:, half, t, :], iota_h[:, :], c_tab[:, bass.ds(e, 1)], None, ALU.is_equal)
                            last = v.tensor_scalar(src_hot[:, half, t, :], iota_h[:, 0:128], lo_tab[:, bass.ds(e, 1)], None,
                                                   ALU.is_equal)
                        last.then_inc(s_hot, 1)

                    def add_window(g, half):
                        base = dve.value_load(base_row[0:1, bass.ds(g, 1)], min_val=0, max_val=N)
                        dve.wait_ge(s_outer, g + 1)
                        win = adj[:, :, bass.ds(base, W)]
                        v.tensor_tensor(win, win, psum[0:P, half, 0:W * NT].rearrange("p (t w) -> p t w", w=W),
                                        ALU.add).then_inc(s_added, 1)
                        dve.wait_ge(s_added, g + 1)

                    one_hots(0, 0)
                    one_hots(1, 1)
                    add_window(0, 0)
                    with dve.Fori(1, G // 2) as i:
                        g = 2 * i
                        dve.wait_ge(s_outer, g - 1)
                        one_hots(g, 0)
                        add_window(g - 1, 1)
                        one_hots(g + 1, 1)
                        add_window(g, 0)
                    add_window(G - 1, 1)
                    v.tensor_scalar(pass_off[:, :], pass_off[:, :], float(W), None, ALU.add).then_inc(s_bchain, 1)
                    dve.wait_ge(s_bchain, link.count + 1)

                @block.tensor
                def _(pe):
                    def group(g, half):
                        pe.wait_ge(s_hot, g + 1)
                        for t in range(GT):
                            last = pe.matmul(psum[0:P, half, 0:W * NT], src_hot[:, half, t, 0:P], col_hot[:, half, t, :],
                                             start=(t == 0), stop=(t == GT - 1))
                        last.then_inc(s_outer, 1)

                    group(0, 0)
                    group(1, 1)
                    with pe.Fori(1, G // 2) as i:
                        g = 2 * i
                        pe.wait_ge(s_added, g - 1)
                        group(g, 0)
                        pe.wait_ge(s_added, g)
                        group(g + 1, 1)
            nc.all_engine_barrier(sems_to_clear=None)
            for s in (s_bchain, s_hot, s_outer, s_added):
                nc.sync.sem_clear(s)
            nc.all_engine_barrier()
        build_scope.close()

        def layer_norm_relu(tag, h, tmp, loops=None):
            s_c, s_var, s_std = sem(tag + "_ln_chain"), sem(tag + "_ln_var"), sem(tag + "_ln_std")
            with nc.Block() as block:
                if loops is not None:
                    s_loops = sem(tag + "_self_loops")

                    @block.gpsimd
                    def _(pool):
                        flat = adj[:, :, :].rearrange("p t n -> p (t n)")
                        with pool.Fori(0, NT) as t:
                            own = flat[:, bass.ds(t * (AW + P), P)]
                            pool.tensor_tensor(own, own, ident[0:P, 0:P], loops).then_inc(s_loops, 1)
                        pool.wait_ge(s_loops, NT)

                @block.vector
                def _(dve):
                    v = nc.vector
                    link = Chain(dve, s_c)
                    link(v.tensor_reduce(stat[:, 0, :], x_sb[:, :, :], AX.X, ALU.add))
                    link(v.tensor_scalar(stat[:, 0, :], stat[:, 0, :], 1.0 / D, None, ALU.mult))
                    link(v.tensor_tensor(tmp, x_sb[:, :, :], over_features(stat[:, 0, :]), ALU.subtract))
                    link(v.tensor_tensor(h, tmp, tmp, ALU.mult))
                    link(v.tensor_reduce(stat[:, 1, :], h, AX.X, ALU.add))
                    v.tensor_scalar(stat[:, 1, :], stat[:, 1, :], 1.0 / D, LN_EPS, ALU.mult, ALU.add).then_inc(s_var, 1)
                    dve.wait_ge(s_std, 1)
                    link(v.reciprocal(stat[:, 3, :], stat[:, 2, :]))
                    link(v.scalar_tensor_tensor(h, tmp, 0.0, over_features(stat[:, 3, :]), ALU.max, ALU.mult))

                @block.scalar
                def _(act):
                    act.wait_ge(s_var, 1)
                    act.activation(stat[:, 2, :], stat[:, 1, :], ACT.Sqrt).then_inc(s_std, 1)

        def sage_layer(tag, h, hT, agg, parts, lows, z, bias, w_agg, w_self, mean):
            s_split, s_t, s_tc, s_agg, s_aggc, s_z, s_zc, s_c = (sem(f"{tag}_{n}") for n in (
                "parts_ready", "transposed", "transpose_copied", "aggregated", "aggregate_copied", "projected",
                "projection_read", "sage_chain"))
            blocks = lambda half: psum[:, 2 * half:2 * half + 2, :].rearrange("p a b -> p (a b)")\
                .rearrange("p (t q) -> p t q", q=128)
            with nc.Block() as block:
                @block.vector
                def _(dve):
                    v = nc.vector
                    link = Chain(dve, s_c)
                    if lows is None:
                        v.tensor_copy(parts[:, :, 0:D], h).then_inc(s_c, 1)
                        v.tensor_scalar(z, h, LO_SCALE, None, ALU.mult).then_inc(s_c, 1)
                        link.count = 2
                        dve.wait_ge(s_c, 2)
                        v.scalar_tensor_tensor(parts[:, :, D:2 * D], parts[:, :, 0:D], -LO_SCALE, z,
                                               ALU.mult, ALU.add).then_inc(s_split, 1)
                    else:
                        link(v.tensor_copy(parts[:, :, 0:D], h))
                        link(v.tensor_tensor(z, h, parts[:, :, 0:D], ALU.subtract))
                        link(v.tensor_copy(parts[:, :, D:2 * D], z))
                        v.tensor_tensor(lows, z, parts[:, :, D:2 * D], ALU.subtract).then_inc(s_split, 1)
                    dve.wait_ge(s_split, 1)
                    for c in range(NC):
                        dve.wait_ge(s_z, c + 1)
                        zc = z[:, c * TC:(c + 1) * TC, :]
                        pa = psum[0:P, 4, 0:TC * D].rearrange("p (t d) -> p t d", d=D)
                        ps = psum[0:P, 5, 0:TC * D].rearrange("p (t d) -> p t d", d=D)
                        if mean:
                            link(v.tensor_tensor(zc, pa, over_features(deg[:, c * TC:(c + 1) * TC], TC), ALU.mult))
                            link(v.tensor_tensor(zc, zc, ps, ALU.add))
                            v.tensor_tensor(zc, zc, over_tiles(bias, TC), ALU.add).then_inc(s_zc, 1)
                        else:
                            v.tensor_tensor(zc, pa, over_tiles(bias, TC), ALU.add).then_inc(s_zc, 1)
                    dve.wait_ge(s_zc, NC)

                @block.scalar
                def _(act):
                    for c in range(NC):
                        act.wait_ge(s_agg, c + 1)
                        if c >= 2:
                            act.wait_ge(s_z, c - 1)
                        act.activation(agg[:, c % 2, :].rearrange("p (t q) -> p t q", q=P),
                                       blocks(c % 2)[:, 0:TC, 0:P], ACT.Copy).then_inc(s_aggc, 1)
                        act.wait_ge(s_t, c + 1)
                        act.activation(hT[:, c % 2, :].rearrange("p (t q) -> p t q", q=P),
                                       blocks(3)[0:D, 0:TC, 0:P], ACT.Copy).then_inc(s_tc, 1)

                @block.tensor
                def _(pe):
                    pe.wait_ge(s_split, 1)

                    def spmm(c):
                        if c >= 2:
                            pe.wait_ge(s_aggc, c - 1)
                        o = blocks(c % 2)

                        def step(k, first, final):
                            wide = adj[:, bass.ds(k, 1), c * CW:c * CW + 4 * P].rearrange("p a (t q) -> p (a t) q", q=P)
                            rest = adj[:, bass.ds(k, 1), c * CW + 4 * P:(c + 1) * CW].rearrange("p a q -> p (a q)")
                            hi = parts[:, bass.ds(k, 1), :].rearrange("p a d -> p (a d)")
                            for r, o_all, o_low in ((wide, o[:, 0:4, 0:P], o[0:D, 0:4, 0:P]), (rest, o[:, 4, 0:P], o[0:D, 4, 0:P])):
                                tail = final and lows is None
                                last = pe.matmul(o_all, hi, r, start=first, stop=tail, skip_group_check=True)
                                if lows is not None:
                                    lo = lows[:, bass.ds(k, 1), :].rearrange("p a d -> p (a d)")
                                    last = pe.matmul(o_low, lo, r, start=False, stop=final, skip_group_check=True)
                            return last

                        step(0, True, False)
                        with pe.Fori(1, NT - 1) as k:
                            step(k, False, False)
                        step(NT - 1, False, True).then_inc(s_agg, 1)

                    def transposes(c):
                        if c >= 1:
                            pe.wait_ge(s_tc, c)
                        for t in range(TC):
                            last = pe.transpose(blocks(3)[0:D, t, 0:P], h[:, c * TC + t, :], ident[0:P, 0:P])
                        last.then_inc(s_t, 1)

                    def project(c):
                        pe.wait_ge(s_aggc, c + 1)
                        pe.wait_ge(s_tc, c + 1)
                        if c >= 1:
                            pe.wait_ge(s_zc, c)
                        for t in range(TC):
                            node = slice(t * P, (t + 1) * P)
                            cols = slice(t * D, (t + 1) * D)
                            pe.matmul(psum[0:P, 4, cols], agg[:, c % 2, node], w_agg, start=True, stop=mean)
                            last = pe.matmul(psum[0:P, 5 if mean else 4, cols], hT[:, c % 2, node], w_self,
                                             start=mean, stop=True)
                        last.then_inc(s_z, 1)

                    for c in range(NC + 1):
                        if c < NC:
                            spmm(c)
                            transposes(c)
                        if c >= 1:
                            project(c - 1)

        s_wscale = sem("weights_scaled")
        with nc.Block() as block:
            @block.scalar
            def _(act):
                for name in ("L0_W1l", "L0_W2l", "S_neigh1"):
                    w = mats[D:2 * D, MATS.index(name), :]
                    act.activation(w, w, ACT.Copy, scale=1.0 / LO_SCALE).then_inc(s_wscale, 1)
                act.wait_ge(s_wscale, 3)

        with ExitStack() as scope:
            h = sb("l0_h", [P, NT, D], FP32, scope)
            z = sb("l0_z", [P, NT, D], FP32, scope)
            hT = sb("l0_hT", [D, 2, CW], FP32, scope)
            agg = sb("l0_agg", [128, 2, CW], FP32, scope)
            parts = sb("l0_parts", [P, NT, 2 * D], FP16, scope)
            layer_norm_relu("l0", h[:, :, :], z[:, :, :])
            sage_layer("l0a", h[:, :, :], hT, agg, parts, None, z[:, :, :], vec("L0_b1"), mat("L0_W1l", 128),
                       mat("L0_W1r"), False)
            s_c, s_ss, s_nrm = sem("l0_norm_chain"), sem("l0_sum_squares"), sem("l0_norm")
            with nc.Block() as block:
                @block.vector
                def _(dve):
                    v = nc.vector
                    link = Chain(dve, s_c)
                    link(v.tensor_scalar(z[:, :, :], z[:, :, :], 0.0, None, ALU.max))
                    link(v.tensor_tensor(h[:, :, :], z[:, :, :], z[:, :, :], ALU.mult))
                    v.tensor_reduce(stat[:, 0, :], h[:, :, :], AX.X, ALU.add).then_inc(s_ss, 1)
                    dve.wait_ge(s_nrm, 1)
                    link(v.tensor_scalar(stat[:, 1, :], stat[:, 1, :], 1e-12, None, ALU.max))
                    link(v.reciprocal(stat[:, 2, :], stat[:, 1, :]))
                    link(v.tensor_tensor(h[:, :, :], z[:, :, :], over_features(stat[:, 2, :]), ALU.mult))

                @block.scalar
                def _(act):
                    act.wait_ge(s_ss, 1)
                    act.activation(stat[:, 1, :], stat[:, 0, :], ACT.Sqrt).then_inc(s_nrm, 1)
            sage_layer("l0b", h[:, :, :], hT, agg, parts, None, z[:, :, :], vec("L0_b2"), mat("L0_W2l", 128),
                       mat("L0_W2r"), False)
            add_residual(nc, sem("l0_residual"), x_sb, z)
        if STOP == "L0":
            edge_scope.close()
            return store(nc, sem, out, x_sb)

        table = nc.dram_tensor("relation_table", [N * R, D], FP32, kind="Internal").ap()
        with ExitStack() as scope:
            h = sb("l1_h", [P, NT, D], FP32, scope)
            hT = sb("l1_hT", [D, 2, CW], FP32, scope)
            rel = sb("rel", [D, R * D], FP32, scope)
            rows = sb("table_rows", [P, 3, R * D], FP32, scope)
            s_rel = sem("rel_in")
            layer_norm_relu("l1", h[:, :, :], rows[:, :, :].rearrange("p a b -> p (a b)")[:, 0:NT * D]
                            .rearrange("p (t d) -> p t d", d=D))
            s_t, s_tc, s_y = (sem("l1_" + n) for n in ("transposed", "transpose_copied", "table_rows_ready"))
            s_yc = [sem(f"l1_table_rows_copied{k}") for k in range(2)]
            s_store = [sem(f"l1_table_stored{k}") for k in range(3)]
            with nc.Block() as block:
                @block.sync
                def _(sp):
                    sp.dma_start(rel[:, :], rel_in).then_inc(s_rel, 16)
                    for t in range(NT):
                        for s in s_yc:
                            sp.wait_ge(s, t + 1)
                        sp.dma_start(table[t * P * R:(t + 1) * P * R, :].rearrange("(p r) d -> p (r d)", r=R),
                                     rows[:, t % 3, :]).then_inc(s_store[t % 3], 16)
                    for k in range(3):
                        sp.wait_ge(s_store[k], 16 * len(range(k, NT, 3)))

                @block.tensor
                def _(pe):
                    def transposes(c):
                        if c >= 1:
                            pe.wait_ge(s_tc, c)
                        for t in range(TC):
                            last = pe.transpose(psum[0:D, t // 4, (t % 4) * 128:(t % 4) * 128 + P], h[:, c * TC + t, :],
                                                ident[0:P, 0:P])
                        last.then_inc(s_t, 1)

                    transposes(0)
                    pe.wait_ge(s_rel, 16)
                    for t in range(NT):
                        c, u = divmod(t, TC)
                        if u == 0:
                            if c + 1 < NC:
                                transposes(c + 1)
                            pe.wait_ge(s_tc, c + 1)
                        if t >= 3:
                            for s in s_yc:
                                pe.wait_ge(s, t - 2)
                        for k in range(2):
                            pe.matmul(psum[0:P, 2 + 2 * (t % 3) + k, :], hT[:, c % 2, u * P:(u + 1) * P],
                                      rel[:, k * 512:(k + 1) * 512], start=True, stop=True).then_inc(s_y, 1)

                def copy_rows(eng, copy, k):
                    for t in range(NT):
                        eng.wait_ge(s_y, 2 * t + k + 1)
                        if t >= 3:
                            eng.wait_ge(s_store[t % 3], 16 * (t // 3))
                        copy(rows[:, t % 3, k * 512:(k + 1) * 512], psum[0:P, 2 + 2 * (t % 3) + k, :]).then_inc(s_yc[k], 1)
                        if k == 0 and t % TC == 0 and t // TC + 1 < NC:
                            copy_transposes(eng, t // TC + 1)

                def copy_transposes(act, c):
                    act.wait_ge(s_t, c + 1)
                    if c >= 2:
                        act.wait_ge(s_y, 2 * TC * (c - 1))
                    act.activation(hT[:, c % 2, :].rearrange("p (t q) -> p t q", q=P),
                                   psum[0:D, 0:2, :].rearrange("p a b -> p (a b)")
                                   .rearrange("p (t q) -> p t q", q=128)[:, 0:TC, 0:P], ACT.Copy).then_inc(s_tc, 1)

                @block.scalar
                def _(act):
                    copy_transposes(act, 0)
                    copy_rows(act, lambda o, i: act.activation(o, i, ACT.Copy), 0)

                @block.vector
                def _(dve):
                    copy_rows(dve, lambda o, i: nc.vector.tensor_copy(o, i), 1)

        with ExitStack() as scope:
            aggT = sb("l1_aggT", [D + 1, AW], FP32, scope)
            idx = sb("l1_idx", [128, 2, GT], U32, scope)
            got = sb("l1_gathered", [128, 2, GT, D + 1], FP32, scope)
            dst_hot = sb("l1_dst_hot", [128, 2, GT, W], FP32, scope)
            wi = sb("l1_window_iota_i", [128, W], I32, scope)
            wf = sb("l1_window_iota", [128, W], FP32, scope)
            s_iw, s_ic = sem("l1_iota"), sem("l1_init_chain")
            with nc.Block() as block:
                @block.gpsimd
                def _(pool):
                    pool.iota(wi[:, :], pattern=[[1, W]], base=0, channel_multiplier=0).then_inc(s_iw, 1)

                @block.vector
                def _(dve):
                    v = nc.vector
                    link = Chain(dve, s_ic)
                    link(v.memset(aggT[:, :], 0.0))
                    link(v.memset(got[:, :, :, D:D + 1], 1.0))
                    link(v.memset(pass_off[:, :], 0.0))
                    dve.wait_ge(s_iw, 1)
                    link(v.tensor_copy(wf[:, :], wi[:, :]))
            s_gc, s_ix, s_hot, s_sum, s_added = (sem("l1_" + n) for n in ("pass_chain", "indices_ready", "dst_hot_ready",
                                                                         "summed", "window_added"))
            s_tick = sem("l1_wait_carrier")
            s_got = [sem(f"l1_gathered{k}") for k in range(2)]
            with nc.Fori(0, passes):
                with nc.Block() as block:
                    @block.gpsimd
                    def _(pool):
                        def group(g, half):
                            pool.tensor_copy(idx[:, half, :], gather_idx[:, bass.ds(g * GT, GT)]).then_inc(s_ix, 1)
                            pool.wait_ge(s_ix, g + 1)
                            pool.sem_inc(s_tick, 1)
                            for t in range(GT):
                                pool.indirect_dma_start(
                                    out=got[:, half, t, 0:D], out_offset=None, in_=table[:, :],
                                    in_offset=bass.IndirectOffsetOnAxis(ap=idx[:, half, t:t + 1], axis=0),
                                ).then_inc(s_got[half], 16)

                        group(0, 0)
                        group(1, 1)
                        with pool.Fori(1, G // 2) as i:
                            pool.wait_ge(s_sum, 2 * i - 1)
                            pool.sem_inc(s_tick, 1)
                            group(2 * i, 0)
                            pool.wait_ge(s_sum, 2 * i)
                            pool.sem_inc(s_tick, 1)
                            group(2 * i + 1, 1)

                    @block.tensor
                    def _(pe):
                        def group(i, half):
                            pe.wait_ge(s_got[half], 16 * GT * (i + 1))
                            pe.wait_ge(s_hot, 2 * i + half + 1)
                            for t in range(GT):
                                last = pe.matmul(psum[0:D + 1, half, 0:W], got[:, half, t, :], dst_hot[:, half, t, :],
                                                 start=(t == 0), stop=(t == GT - 1))
                            last.then_inc(s_sum, 1)

                        group(0, 0)
                        group(0, 1)
                        with pe.Fori(1, G // 2) as i:
                            pe.wait_ge(s_added, 2 * i - 1)
                            group(i, 0)
                            pe.wait_ge(s_added, 2 * i)
                            group(i, 1)

                    @block.vector
                    def _(dve):
                        v = nc.vector
                        link = Chain(dve, s_gc)
                        link(v.tensor_scalar(base_row[:, :], basef_row[:, :], pass_off[0:1, 0:1], float(N), ALU.add, ALU.min))

                        def hot(g, half):
                            v.tensor_tensor(dst_hot[:, half, :, :], wf[:, :].unsqueeze(1).to_broadcast([128, GT, W]),
                                            d_tab[:, bass.ds(g * GT, GT)].unsqueeze(2).to_broadcast([128, GT, W]),
                                            ALU.is_equal).then_inc(s_hot, 1)

                        def add_window(g, half):
                            base = dve.value_load(base_row[0:1, bass.ds(g, 1)], min_val=0, max_val=N)
                            dve.wait_ge(s_sum, g + 1)
                            win = aggT[:, bass.ds(base, W)]
                            v.tensor_tensor(win, win, psum[0:D + 1, half, 0:W], ALU.add).then_inc(s_added, 1)
                            dve.wait_ge(s_added, g + 1)

                        hot(0, 0)
                        hot(1, 1)
                        add_window(0, 0)
                        with dve.Fori(1, G // 2) as i:
                            g = 2 * i
                            hot(g, 0)
                            add_window(g - 1, 1)
                            hot(g + 1, 1)
                            add_window(g, 0)
                        add_window(G - 1, 1)
                        link(v.tensor_scalar(pass_off[:, :], pass_off[:, :], float(W), None, ALU.add))
                        link(v.tensor_scalar(wf[:, :], wf[:, :], float(W), None, ALU.add))
                nc.all_engine_barrier()
                for s in (s_gc, s_ix, s_hot, s_sum, s_added, s_tick, *s_got):
                    nc.sync.sem_clear(s)
                nc.all_engine_barrier()
            s_t, s_x, s_dc = sem("l1_agg_transposed"), sem("l1_x_added"), sem("l1_degree_chain")
            with nc.Block() as block:
                @block.tensor
                def _(pe):
                    for c in range(NC):
                        if c >= 2:
                            pe.wait_ge(s_x, c - 1)
                        for t in range(TC):
                            node = c * CW + t * P
                            last = pe.transpose(psum[0:P, c % 2, t * (D + 1):(t + 1) * (D + 1)], aggT[:, node:node + P],
                                                ident[0:D + 1, 0:D + 1])
                        last.then_inc(s_t, 1)

                @block.vector
                def _(dve):
                    v = nc.vector
                    link = Chain(dve, s_dc)
                    for c in range(NC):
                        dve.wait_ge(s_t, c + 1)
                        tiles = slice(c * TC, (c + 1) * TC)
                        part = psum[0:P, c % 2, 0:TC * (D + 1)].rearrange("p (t d) -> p t d", d=D + 1)
                        link(v.tensor_scalar(deg[:, tiles], part[:, :, D], 1.0, None, ALU.max))
                        v.tensor_tensor(x_sb[:, tiles, :], x_sb[:, tiles, :], part[:, :, 0:D], ALU.add).then_inc(s_x, 1)
                    link(v.reciprocal(deg[:, :], deg[:, :]))
                    dve.wait_ge(s_x, NC)
        edge_scope.close()
        if STOP == "L1":
            return store(nc, sem, out, x_sb)

        with ExitStack() as scope:
            RING = TC
            o_all = sb("gat_o", [P, NT, D + 1], FP32, scope)
            hx = sb("gat_hx", [P, NT, D + 1], FP32, scope)
            ring = sb("gat_ring", [P, RING, CW], FP32, scope)
            rrow = sb("gat_rows", [P, 2, 2, CW], FP32, scope)
            shuttle = sb("gat_shuttle", [P, TC, P], FP32, scope)
            diag = shuttle
            oT = shuttle[0:D + 1, :, :].rearrange("p t q -> p (t q)")
            hcur = sb("gat_hcur", [P, RING, D + 1], FP32, scope)
            node = sb("gat_node", [P, 8, NT], FP32, scope)
            ext = sb("gat_ext", [P, 8], FP32, scope)
            h_in = o_all[:, :, 0:D]
            tmp = ring[:, :, :].rearrange("p a b -> p (a b)")[:, 0:NT * D].rearrange("p (t d) -> p t d", d=D)
            layer_norm_relu("l2", h_in, tmp, ALU.add)
            gat_sems = {}

            def gat_sem(name):
                if name not in gat_sems:
                    gat_sems[name] = sem(name)
                return gat_sems[name]

            for layer in range(3):
                if layer > 0:
                    for s in gat_sems.values():
                        nc.sync.sem_clear(s)
                    nc.all_engine_barrier()
                gat_layer(nc, gat_sem, dict(
                    adj=adj, psum=psum, ident=ident, ones=ones, o_all=o_all, hx=hx, ring=ring, rrow=rrow, oT=oT, hcur=hcur,
                    node=node, ext=ext, diag=diag, w=mat(f"G_W{layer + 1}"), a_src=vec(f"G_as{layer + 1}"),
                    a_dst=vec(f"G_ad{layer + 1}"), bias=vec(f"G_b{layer + 1}"), tmp=tmp, over_tiles=over_tiles,
                    over_features=over_features, relu=(layer < 2)))
            add_residual(nc, sem("l2_residual"), x_sb, o_all, D)
        if STOP == "L2":
            return store(nc, sem, out, x_sb)

        with ExitStack() as scope:
            h = sb("l3_h", [P, NT, D], FP32, scope)
            z = sb("l3_z", [P, NT, D], FP32, scope)
            hT = sb("l3_hT", [D, 2, CW], FP32, scope)
            agg = sb("l3_agg", [128, 2, CW], FP32, scope)
            bn = sb("l3_bn", [P, 3, D], FP32, scope)

            def batch_norm_lrelu(tag, gamma, beta):
                s_c, s_sum, s_sq, s_sumsq, s_var, s_std = (sem(f"{tag}_{n}") for n in (
                    "bn_chain", "bn_sum", "bn_squares", "bn_sum_squares", "bn_var", "bn_std"))
                with nc.Block() as block:
                    @block.tensor
                    def _(pe):
                        for t in range(NT):
                            last = pe.matmul(psum[0:P, 0, 0:D], ones[0:P, 0:P], z[:, t, :], start=(t == 0), stop=(t == NT - 1))
                        last.then_inc(s_sum, 1)
                        pe.wait_ge(s_sq, 1)
                        for t in range(NT):
                            last = pe.matmul(psum[0:P, 1, 0:D], ones[0:P, 0:P], h[:, t, :], start=(t == 0), stop=(t == NT - 1))
                        last.then_inc(s_sumsq, 1)

                    @block.scalar
                    def _(act):
                        act.wait_ge(s_var, 1)
                        act.activation(bn[:, 2, :], bn[:, 1, :], ACT.Sqrt).then_inc(s_std, 1)

                    @block.vector
                    def _(dve):
                        v = nc.vector
                        link = Chain(dve, s_c)
                        dve.wait_ge(s_sum, 1)
                        link(v.tensor_scalar(bn[:, 0, :], psum[0:P, 0, 0:D], 1.0 / N, None, ALU.mult))
                        link(v.tensor_tensor(z[:, :, :], z[:, :, :], over_tiles(bn[:, 0, :]), ALU.subtract))
                        v.tensor_tensor(h[:, :, :], z[:, :, :], z[:, :, :], ALU.mult).then_inc(s_sq, 1)
                        dve.wait_ge(s_sumsq, 1)
                        v.tensor_scalar(bn[:, 1, :], psum[0:P, 1, 0:D], 1.0 / N, LN_EPS, ALU.mult, ALU.add).then_inc(s_var, 1)
                        dve.wait_ge(s_std, 1)
                        link(v.reciprocal(bn[:, 0, :], bn[:, 2, :]))
                        link(v.tensor_tensor(z[:, :, :], z[:, :, :], over_tiles(bn[:, 0, :]), ALU.mult))
                        link(v.tensor_tensor(z[:, :, :], z[:, :, :], over_tiles(gamma), ALU.mult))
                        link(v.tensor_tensor(z[:, :, :], z[:, :, :], over_tiles(beta), ALU.add))
                        link(v.scalar_tensor_tensor(h[:, :, :], z[:, :, :], 0.01, z[:, :, :], ALU.mult, ALU.max))

            with ExitStack() as half_scope:
                parts = sb("l3_parts", [P, NT, 2 * D], FP16, half_scope)
                layer_norm_relu("l3", h[:, :, :], z[:, :, :], ALU.subtract)
                sage_layer("l3a", h[:, :, :], hT, agg, parts, None, z[:, :, :], vec("S_b1"), mat("S_neigh1", 128),
                           mat("S_self1"), True)
            batch_norm_lrelu("l3a", vec("S_gamma1"), vec("S_beta1"))
            with ExitStack() as half_scope:
                parts = sb("l3_parts3", [P, NT, 2 * D], BF16, half_scope)
                lows = sb("l3_lows", [P, NT, D], BF16, half_scope)
                sage_layer("l3b", h[:, :, :], hT, agg, parts, lows[:, :, :], z[:, :, :], vec("S_b2"), mat("S_neigh2", 128),
                           mat("S_self2"), True)
            batch_norm_lrelu("l3b", vec("S_gamma2"), vec("S_beta2"))
            add_residual(nc, sem("l3_residual"), x_sb, h)
        store(nc, sem, out, x_sb)


def gat_layer(nc, sem, b):
    adj, psum, ident, ones, o_all, hx, ring, rrow, oT, hcur, node, ext = (b[k] for k in (
        "adj", "psum", "ident", "ones", "o_all", "hx", "ring", "rrow", "oT", "hcur", "node", "ext"))
    diag = b["diag"]
    a_s, a_d, a_unit, k_s, m_max, m_log, r1, r2 = (node[:, k, :] for k in range(8))
    h_in = o_all[:, :, 0:D]
    tag = "gat_"
    hT = rrow[0:D, 0, :, :]
    blocks = lambda bank: psum[:, bank:bank + 2, :].rearrange("p a b -> p (a b)").rearrange("p (t q) -> p t q", q=128)
    tiled = lambda row: row.rearrange("p (t q) -> p t q", q=P)
    RING = TC

    s_t, s_tc, s_h, s_hc, s_c, s_ext, s_ext2 = (sem(tag + n) for n in (
        "transposed", "transpose_copied", "h_ready", "h_copied", "node_chain", "extremes", "extremes_all"))
    with nc.Block() as block:
        @block.tensor
        def _(pe):
            def transposes(c):
                if c >= 2:
                    pe.wait_ge(s_tc, c - 1)
                for t in range(TC):
                    last = pe.transpose(blocks(2 * (c % 2))[0:D, t, 0:P], h_in[:, c * TC + t, :], ident[0:P, 0:P])
                last.then_inc(s_t, 1)

            transposes(0)
            for c in range(NC):
                if c + 1 < NC:
                    transposes(c + 1)
                pe.wait_ge(s_tc, c + 1)
                if c >= 2:
                    pe.wait_ge(s_hc, c - 1)
                for t in range(TC):
                    last = pe.matmul(psum[0:P, 4 + c % 2, t * D:(t + 1) * D], hT[:, c % 2, t * P:(t + 1) * P], b["w"],
                                     start=True, stop=True)
                last.then_inc(s_h, 1)

        @block.scalar
        def _(act):
            for c in range(NC):
                act.wait_ge(s_t, c + 1)
                if c >= 2:
                    act.wait_ge(s_h, c - 1)
                act.activation(tiled(hT[:, c % 2, :]), blocks(2 * (c % 2))[0:D, 0:TC, 0:P], ACT.Copy).then_inc(s_tc, 1)

        @block.gpsimd
        def _(pool):
            pool.wait_ge(s_ext, 1)
            pool.partition_all_reduce(ext[0:P, 2:4], ext[0:P, 0:2], P, bass.bass_isa.ReduceOp.max).then_inc(s_ext2, 1)

        @block.vector
        def _(dve):
            v = nc.vector
            link = Chain(dve, s_c)
            link(v.memset(hx[:, :, D:D + 1], 1.0))
            for c in range(NC):
                dve.wait_ge(s_h, c + 1)
                v.tensor_copy(hx[:, c * TC:(c + 1) * TC, 0:D],
                              psum[0:P, 4 + c % 2, 0:TC * D].rearrange("p (t d) -> p t d", d=D)).then_inc(s_hc, 1)
            dve.wait_ge(s_hc, NC)
            link(v.tensor_tensor(b["tmp"], hx[:, :, 0:D], b["over_tiles"](b["a_src"]), ALU.mult))
            link(v.tensor_reduce(a_s, b["tmp"], AX.X, ALU.add))
            link(v.tensor_reduce(ext[:, 0:1], a_s, AX.X, ALU.max))
            link(v.tensor_scalar(k_s, a_s, -1.0, None, ALU.mult))
            v.tensor_reduce(ext[:, 1:2], k_s, AX.X, ALU.max).then_inc(s_ext, 1)
            link(v.tensor_tensor(b["tmp"], hx[:, :, 0:D], b["over_tiles"](b["a_dst"]), ALU.mult))
            link(v.tensor_reduce(a_d, b["tmp"], AX.X, ALU.add))
            dve.wait_ge(s_ext2, 1)
            link(v.tensor_tensor(ext[:, 4:5], ext[:, 2:3], ext[:, 3:4], ALU.add))
            link(v.tensor_scalar(ext[:, 4:5], ext[:, 4:5], 1e-30, 2.0, ALU.max, ALU.mult))
            link(v.reciprocal(ext[:, 5:6], ext[:, 4:5]))
            link(v.tensor_scalar(a_unit, a_s, ext[:, 3:4], ext[:, 5:6], ALU.add, ALU.mult))
            link(v.tensor_scalar(a_unit, a_unit, 0.5, None, ALU.add))
            link(v.tensor_scalar(k_s, a_s, -0.8, None, ALU.mult))

    s_m, s_mt, s_mr, s_mc = (sem(tag + n) for n in ("max_step", "max_transposed", "max_reduced", "max_chain"))
    with nc.Block() as block:
        @block.vector
        def _(dve):
            v = nc.vector
            for c in range(NC):
                v.tensor_scalar(ring[:, c, :], adj[:, 0, c * CW:(c + 1) * CW], a_unit[:, 0:1], None, ALU.min).then_inc(s_m, 1)
            with dve.Fori(1, NT) as k:
                for c in range(NC):
                    dve.wait_ge(s_m, NC * (k - 1) + c + 1)
                    v.scalar_tensor_tensor(ring[:, c, :], adj[:, bass.ds(k, 1), c * CW:(c + 1) * CW]
                                           .rearrange("p a q -> p (a q)"), a_unit[:, bass.ds(k, 1)], ring[:, c, :],
                                           ALU.min, ALU.max).then_inc(s_m, 1)
            for c in range(NC):
                dve.wait_ge(s_mt, c + 1)
                v.tensor_reduce(m_max[:, c * TC:(c + 1) * TC], blocks(2 * (c % 2))[0:P, 0:TC, 0:P], AX.X,
                                ALU.max).then_inc(s_mr, 1)
            dve.wait_ge(s_mr, NC)
            link = Chain(dve, s_mc)
            link(v.tensor_scalar(m_max, m_max, -0.5, ext[:, 4:5], ALU.add, ALU.mult))
            link(v.scalar_tensor_tensor(r2, m_max, ext[:, 3:4], a_d, ALU.subtract, ALU.add))
            link(v.scalar_tensor_tensor(m_log, r2, 0.2, r2, ALU.mult, ALU.max))
            link(v.tensor_tensor(r1, a_d, m_log, ALU.subtract))
            link(v.scalar_tensor_tensor(r2, a_d, 0.2, m_log, ALU.mult, ALU.subtract))

        @block.tensor
        def _(pe):
            for c in range(NC):
                pe.wait_ge(s_m, NC * (NT - 1) + c + 1)
                if c >= 2:
                    pe.wait_ge(s_mr, c - 1)
                for t in range(TC):
                    last = pe.transpose(blocks(2 * (c % 2))[0:P, t, 0:P], ring[:, c, t * P:(t + 1) * P], ident[0:P, 0:P])
                last.then_inc(s_mt, 1)

    s_dg, s_rp, s_rr, s_pre, s_exp, s_w, s_mm, s_hcur, s_oT, s_ot, s_oc = (sem(tag + n) for n in (
        "diag_ready", "rows_in_psum", "rows_ready", "exponent_ready", "exp_ready", "weight_ready", "product_done", "hcur_ready",
        "sums_copied", "sums_transposed", "sums_stored"))
    s_tick = sem(tag + "wait_carrier")
    with nc.Block() as block:
        @block.vector
        def _(dve):
            v = nc.vector

            def exponent(c, k, s):
                n = c * NT + k
                if not (c == 0 and isinstance(k, int)):
                    dve.wait_ge(s_mm, n - RING + 1)
                v.scalar_tensor_tensor(ring[:, s, :], rrow[:, c % 2, 1, :], k_s[:, bass.ds(k, 1)], rrow[:, c % 2, 0, :],
                                       ALU.add, ALU.max).then_inc(s_pre, 1)

            def weight(c, k, s):
                n = c * NT + k
                dve.wait_ge(s_exp, n + 1)
                v.scalar_tensor_tensor(ring[:, s, :], ring[:, s, :], 2.0, adj[:, bass.ds(k, 1), c * CW:(c + 1) * CW]
                                       .rearrange("p a q -> p (a q)"), ALU.min, ALU.mult).then_inc(s_w, 1)

            for c in range(NC):
                dve.wait_ge(s_rr, 2 * (c + 1))
                for s in range(RING):
                    exponent(c, s, s)
                    if s >= 2:
                        weight(c, s - 2, s - 2)
                    elif c > 0:
                        weight(c - 1, NT - 2 + s, RING - 2 + s)
                with dve.Fori(1, NT // RING) as i:
                    for s in range(RING):
                        exponent(c, i * RING + s, s)
                        weight(c, i * RING + s - 2, (s - 2) % RING)
            weight(NC - 1, NT - 2, RING - 2)
            weight(NC - 1, NT - 1, RING - 1)

        @block.gpsimd
        def _(pool):
            def copy(c, k, s):
                n = c * NT + k
                if not (c == 0 and isinstance(k, int)):
                    pool.wait_ge(s_mm, n - RING + 1)
                    pool.sem_inc(s_tick, 1)
                pool.tensor_copy(hcur[:, s, :], hx[:, bass.ds(k, 1), :].rearrange("p a d -> p (a d)")).then_inc(s_hcur, 1)

            for c in range(NC):
                for s in range(RING):
                    copy(c, s, s)
                with pool.Fori(1, NT // RING) as i:
                    for s in range(RING):
                        copy(c, i * RING + s, s)

        @block.scalar
        def _(act):
            def rows(c):
                for k, r in enumerate((r1, r2)):
                    if c > 0 or k > 0:
                        act.wait_ge(s_rp, 2 * c + k)
                    for t in range(TC):
                        act.activation(diag[:, t, :], ident[0:P, 0:P], ACT.Copy, scale=r[:, c * TC + t:c * TC + t + 1])\
                           .then_inc(s_dg, 1)
                    act.wait_ge(s_rp, 2 * c + k + 1)
                    if c >= 2:
                        act.wait_ge(s_pre, (c - 1) * NT)
                    act.activation(tiled(rrow[:, c % 2, k, :]), blocks(4)[0:P, 0:TC, 0:P], ACT.Copy).then_inc(s_rr, 1)

            def exp(c, k, s):
                act.wait_ge(s_pre, c * NT + k + 1)
                act.activation(ring[:, s, :], ring[:, s, :], ACT.Exp, bias=a_s[:, bass.ds(k, 1)]).then_inc(s_exp, 1)

            def sums(c):
                act.wait_ge(s_mm, (c + 1) * NT)
                if c > 0:
                    act.wait_ge(s_ot, c)
                act.activation(tiled(oT[:, :]), blocks(2 * (c % 2))[0:D + 1, 0:TC, 0:P], ACT.Copy).then_inc(s_oT, 1)
                act.wait_ge(s_ot, c + 1)
                act.activation(o_all[:, c * TC:(c + 1) * TC, :],
                               psum[0:P, 6, 0:TC * (D + 1)].rearrange("p (t d) -> p t d", d=D + 1), ACT.Copy).then_inc(s_oc, 1)

            rows(0)
            for c in range(NC):
                for s in range(RING):
                    exp(c, s, s)
                if c + 1 < NC:
                    rows(c + 1)
                if c > 0:
                    sums(c - 1)
                with act.Fori(1, NT // RING) as i:
                    for s in range(RING):
                        exp(c, i * RING + s, s)
            sums(NC - 1)

        @block.tensor
        def _(pe):
            def rows(c):
                for k in range(2):
                    if c > 0 or k > 0:
                        pe.wait_ge(s_rr, 2 * c + k)
                    pe.wait_ge(s_dg, (2 * c + k + 1) * TC)
                    for t in range(TC):
                        last = pe.matmul(blocks(4)[0:P, t, 0:P], ones[0:P, 0:P], diag[:, t, :], start=True, stop=True)
                    last.then_inc(s_rp, 1)

            def product(c, k, s, first, final):
                n = c * NT + k
                pe.wait_ge(s_w, n + 1)
                pe.wait_ge(s_hcur, n + 1)
                o = blocks(2 * (c % 2))
                pe.matmul(o[0:D + 1, 0:4, 0:P], hcur[:, s, :], tiled(ring[:, s, 0:4 * P]), start=first, stop=final,
                          skip_group_check=True)
                pe.matmul(o[0:D + 1, 4, 0:P], hcur[:, s, :], ring[:, s, 4 * P:], start=first, stop=final,
                          skip_group_check=True).then_inc(s_mm, 1)

            def transposes(c):
                pe.wait_ge(s_oT, c + 1)
                if c > 0:
                    pe.wait_ge(s_oc, c)
                for t in range(TC):
                    last = pe.transpose(psum[0:P, 6, t * (D + 1):(t + 1) * (D + 1)], oT[:, t * P:(t + 1) * P],
                                        ident[0:D + 1, 0:D + 1])
                last.then_inc(s_ot, 1)

            rows(0)
            for c in range(NC):
                if c >= 2:
                    pe.wait_ge(s_oT, c - 1)
                for s in range(RING):
                    product(c, s, s, s == 0, False)
                if c + 1 < NC:
                    rows(c + 1)
                if c > 0:
                    transposes(c - 1)
                with pe.Fori(1, NT // RING - 1) as i:
                    for s in range(RING):
                        product(c, i * RING + s, s, False, False)
                for s in range(RING):
                    product(c, NT - RING + s, s, False, s == RING - 1)
            transposes(NC - 1)

    s_n = sem(tag + "normalise_chain")
    with nc.Block() as block:
        @block.vector
        def _(dve):
            v = nc.vector
            link = Chain(dve, s_n)
            link(v.tensor_scalar(m_max, o_all[:, :, D], 1e-16, None, ALU.add))
            link(v.reciprocal(r1, m_max))
            link(v.tensor_tensor(h_in, h_in, b["over_features"](r1), ALU.mult))
            link(v.tensor_tensor(h_in, h_in, b["over_tiles"](b["bias"]), ALU.add))
            if b["relu"]:
                link(v.tensor_scalar(h_in, h_in, 0.0, None, ALU.max))




def add_residual(nc, s_res, x_sb, z, width=D):
    with nc.Block() as block:
        @block.vector
        def _(dve):
            nc.vector.tensor_tensor(x_sb[:, :, :], x_sb[:, :, :], z[:, :, 0:width], ALU.add).then_inc(s_res, 1)
            dve.wait_ge(s_res, 1)


def store(nc, sem, out, x_sb):
    s_out = sem("out_stored")
    with nc.Block() as block:
        @block.sync
        def _(sp):
            sp.dma_start(out, x_sb[:, :, :]).then_inc(s_out, 16)
            sp.wait_ge(s_out, 16)


def kernel(**inputs):
    import numpy as np
    import concourse.bacc as bacc
    from concourse.bass_utils import run_bass_kernel_spmd

    a = {k: np.asarray(v) for k, v in inputs.items()}

    def edges(v, pad):
        return np.concatenate([v, np.full(G * GE - E, pad, v.dtype)])

    def tiles(v, pad):
        return np.ascontiguousarray(edges(v, pad).reshape(G * GT, ET).T)

    groups = np.full((2 * 128, GE), PAD_DST, a["dst"].dtype)
    groups[:G] = edges(a["dst"], PAD_DST).reshape(G, GE)
    mats = [a["L0_gnn_W1l"].T, a["L0_gnn_W1r"].T, a["L0_gnn_W2l"].T, a["L0_gnn_W2r"].T,
            a["L2_gnn_W1"], a["L2_gnn_W2"], a["L2_gnn_W3"],
            a["L3_gnn_W_self1"].T, a["L3_gnn_W_neigh1"].T, a["L3_gnn_W_self2"].T, a["L3_gnn_W_neigh2"].T]
    vecs = [a[k] for k in ("L0_gnn_b1l", "L0_gnn_b2l", "L2_gnn_a1s", "L2_gnn_a2s", "L2_gnn_a3s", "L2_gnn_a1d",
                           "L2_gnn_a2d", "L2_gnn_a3d", "L2_gnn_b1", "L2_gnn_b2", "L2_gnn_b3", "L3_gnn_b1",
                           "L3_gnn_gamma1", "L3_gnn_beta1", "L3_gnn_b2", "L3_gnn_gamma2", "L3_gnn_beta2")]
    arrays = {
        "x": a["x"].reshape(NT, P, D).transpose(1, 0, 2),
        "dst_groups": groups.reshape(2, 128, GE).transpose(1, 0, 2),
        "src_tiles": tiles(a["src"], 0),
        "dst_tiles": tiles(a["dst"], PAD_DST),
        "type_tiles": tiles(a["edge_type_16"], 0),
        "mats": np.stack(mats, axis=1),
        "vecs": np.concatenate(vecs)[None],
        "rel": a["L1_gnn_weight"].transpose(1, 0, 2).reshape(D, R * D),
    }
    arrays = {"in_" + k: np.ascontiguousarray(v) for k, v in arrays.items()}
    nc = bacc.Bacc("TRN2", target_bir_lowering=False, num_devices=1)
    args = [nc.dram_tensor(k, v.shape, mybir.dt.from_np(v.dtype), kind="ExternalInput").ap() for k, v in arrays.items()]
    out = nc.dram_tensor("out", (P, NT, D), FP32, kind="ExternalOutput").ap()
    gnn(nc, *args, out)
    r = run_bass_kernel_spmd(nc, [arrays], core_ids=[0])
    return np.ascontiguousarray(np.asarray(r.results[0]["out"]).reshape(P, NT, D).transpose(1, 0, 2).reshape(N, D))
```

```python
import concourse.bass as bass
from concourse import mybir
from contextlib import ExitStack

FP32 = mybir.dt.float32
FP16 = mybir.dt.float16
BF16 = mybir.dt.bfloat16
I32 = mybir.dt.int32
U32 = mybir.dt.uint32
ALU = mybir.AluOpType
ACT = mybir.ActivationFunctionType
AX = mybir.AxisListType

N = 3125
D = 64
E = 103125
P = 125
NT = N // P
NC = 5
TC = NT // NC
CW = N // NC
ET = 128
GT = 4
GE = ET * GT
G = -(-E // GE)
W = 20
AW = N + W + (N + W) % 2
R = 16
PAD_DST = 1 << 20
MAGIC = 12582912.0
LO_SCALE = 2048.0
LN_EPS = 1e-5

MATS = ["L0_W1l", "L0_W1r", "L0_W2l", "L0_W2r", "G_W1", "G_W2", "G_W3", "S_self1", "S_neigh1", "S_self2", "S_neigh2"]
VECS = ["L0_b1", "L0_b2", "G_as1", "G_as2", "G_as3", "G_ad1", "G_ad2", "G_ad3", "G_b1", "G_b2", "G_b3",
        "S_b1", "S_gamma1", "S_beta1", "S_b2", "S_gamma2", "S_beta2"]
STOP = "L3"


class Chain:

    def __init__(self, eng, sem):
        self.eng, self.sem, self.count = eng, sem, 0

    def __call__(self, ins):
        ins.then_inc(self.sem, 1)
        self.count += 1
        self.eng.wait_ge(self.sem, self.count)
        return ins


def gnn(nc, x_in, dst_groups, src_tiles, dst_tiles, type_tiles, mats_in, vecs_in, rel_in, out):
    ctx = ExitStack()
    with ctx:
        names = set()

        def sem(name):
            assert name not in names, name
            names.add(name)
            return ctx.enter_context(nc.semaphore(name))

        def sb(name, shape, dt, scope=None):
            return (scope or ctx).enter_context(nc.sbuf_tensor(name, shape, dt))

        adj = sb("adj", [P, NT, AW], FP16)
        x_sb = sb("x_sb", [P, NT, D], FP32)
        mats = sb("mats", [128, len(MATS), D], FP32)
        ident = sb("ident", [128, 128], FP32)
        ones = sb("ones", [128, 128], FP32)
        deg = sb("deg", [P, NT], FP32)
        stat = sb("stat", [P, 4, NT], FP32)
        vecs0 = sb("vecs0", [P, 2, D], FP32)
        psum = ctx.enter_context(nc.psum_tensor("psum", [128, 8, 512], FP32))

        def mat(name, rows=D):
            return mats[0:rows, MATS.index(name), :]

        def vec(name):
            return vecs[:, VECS.index(name) - 2, :]

        def vec0(name):
            return vecs0[:, VECS.index(name), :]

        def over_tiles(ap2, n=NT):
            return ap2.unsqueeze(1).to_broadcast([P, n, D])

        def over_features(ap2, n=NT, d=D):
            return ap2.unsqueeze(2).to_broadcast([P, n, d])

        edge_scope = ExitStack()
        base_row = sb("base_row", [1, 2 * 128], I32, edge_scope)
        basef_row = sb("basef_row", [1, 2 * 128], FP32, edge_scope)
        d_tab = sb("d_tab", [128, G * GT], FP32, edge_scope)
        src_tab = sb("src_tab", [128, (G + 2) * GT], mybir.dt.int16, edge_scope)
        type_tab = sb("type_tab", [128, G * GT], FP16, edge_scope)
        npass = sb("npass", [128, 1], I32, edge_scope)
        pass_off = sb("pass_off", [128, 1], FP32, edge_scope)

        build_scope = ExitStack()
        lo_tab = sb("lo_tab", [128, G * GT], FP32, build_scope)
        hi_tab = sb("hi_tab", [128, G * GT], FP32, build_scope)
        c_tab = sb("c_tab", [128, G * GT], FP32, build_scope)
        iota_i = sb("iota_i", [128, W * NT], I32, build_scope)
        iota_h = sb("iota_h", [128, W * NT], FP16, build_scope)

        prep_scope = ExitStack()
        dg_i = sb("dg_i", [128, 2, GE], I32, prep_scope)
        dg = dg_i[:, :, :].bitcast(FP32)
        dv = sb("dv", [128, 2, GE], FP32, prep_scope)
        ti = sb("ti", [128, 3, G * GT], I32, prep_scope)
        tf = ti[:, :, :].bitcast(FP32)
        gstat = sb("gstat", [128, 4, 2], FP32, prep_scope)
        diag = sb("diag", [128, 2, 128], FP32, prep_scope)

        s_dg, s_ti, s_x, s_mats, s_mats2, s_vecs = (sem(n) for n in (
            "dst_groups_in", "edge_tiles_in", "x_in_done", "mats_in_done", "mats_twice_done", "vecs_in_done"))
        s_zeroed, s_zeroed2 = sem("adj_zeroed_by_pool"), sem("adj_zeroed_by_act")
        adj_words = adj[:, :, :].bitcast(FP32).rearrange("p t n -> p (t n)")
        zero_cut = adj_words.shape[1] // 2
        s_iota, s_ident, s_ident2 = sem("iota_ready"), sem("ident_zeroed"), sem("ident_ready")
        s_chain, s_diag, s_basebc, s_span, s_spanall = (sem(n) for n in (
            "prep_chain", "diag_ready", "base_broadcast", "span_ready", "span_over_partitions"))

        block = nc.Block()
        with block as block:
            @block.sync
            def _(sp):
                sp.dma_start(dg_i[:, :, :], dst_groups).then_inc(s_dg, 16)
                sp.dma_start(ti[:, 1, :], dst_tiles).then_inc(s_ti, 16)
                sp.dma_start(ti[:, 0, :], src_tiles).then_inc(s_ti, 16)
                sp.dma_start(ti[:, 2, :], type_tiles).then_inc(s_ti, 16)
                sp.dma_start(x_sb[:, :, :], x_in).then_inc(s_x, 16)
                sp.dma_start(mats[0:D, :, :], mats_in).then_inc(s_mats, 16)
                sp.dma_start(mats[D:2 * D, :, :], mats_in).then_inc(s_mats2, 16)
                sp.dma_start(vecs0[:, :, :], vecs_in[:, 0:2 * D].to_broadcast([P, 2 * D])).then_inc(s_vecs, 16)
                for s in (s_mats, s_mats2, s_vecs, s_x):
                    sp.wait_ge(s, 16)

            @block.gpsimd
            def _(pool):
                pool.iota(iota_i[:, :], pattern=[[1, W * NT]], base=0, channel_multiplier=0).then_inc(s_iota, 1)
                pool.memset(ident[:, :], 0.0).then_inc(s_ident, 1)
                pool.memset(ones[:, :], 1.0).then_inc(s_ident2, 1)
                pool.memset(adj_words[:, 0:zero_cut], 0.0).then_inc(s_zeroed, 1)
                pool.wait_ge(s_zeroed, 1)
                pool.wait_ge(s_ident, 1)
                pool.affine_select(out=ident[:, :], in_=ident[:, :], compare_op=ALU.not_equal, fill=1.0, base=0,
                                   pattern=[[-1, 128]], channel_multiplier=1).then_inc(s_ident2, 1)
                pool.wait_ge(s_span, 1)
                pool.partition_all_reduce(gstat[:, 3, 1:2], gstat[:, 3, 0:1], 128,
                                          bass.bass_isa.ReduceOp.max).then_inc(s_spanall, 1)

            @block.scalar
            def _(act):
                act.memzero(adj_words[:, zero_cut:]).then_inc(s_zeroed2, 1)
                act.wait_ge(s_zeroed2, 1)

            @block.tensor
            def _(pe):
                pe.wait_ge(s_ident2, 2)
                pe.wait_ge(s_diag, 2)
                pe.matmul(psum[:, 0, 0:256], ones[:, :], diag[:, :, :], start=True, stop=True).then_inc(s_basebc, 1)

            @block.vector
            def _(dve):
                link = Chain(dve, s_chain)
                v = nc.vector
                link(v.memset(pass_off[:, :], 0.0))
                dve.wait_ge(s_iota, 1)
                link(v.tensor_copy(iota_h[:, :], iota_i[:, :]))
                dve.wait_ge(s_dg, 16)
                link(v.tensor_copy(dg[:, :, :], dg_i[:, :, :]))
                link(v.tensor_reduce(gstat[:, 0, :], dg[:, :, :], AX.X, ALU.min))
                dve.wait_ge(s_ident2, 2)
                for k in range(2):
                    v.tensor_scalar(diag[:, k, :], ident[:, :], gstat[:, 0, k:k + 1], None, ALU.mult).then_inc(s_diag, 1)
                link(v.scalar_tensor_tensor(dv[:, :, :], dg[:, :, :], float(N), dg[:, :, :], ALU.is_lt, ALU.mult))
                link(v.tensor_reduce(gstat[:, 1, :], dv[:, :, :], AX.X, ALU.max))
                link(v.tensor_tensor(gstat[:, 2, :], gstat[:, 1, :], gstat[:, 0, :], ALU.subtract))
                v.tensor_reduce(gstat[:, 3, 0:1], gstat[:, 2, :], AX.X, ALU.max).then_inc(s_span, 1)
                dve.wait_ge(s_ti, 48)
                link(v.tensor_copy(tf[:, :, :], ti[:, :, :]))
                link(v.memset(src_tab[:, G * GT:], 0))
                link(v.tensor_copy(src_tab[:, 0:G * GT], tf[:, 0, :]))
                link(v.tensor_scalar(type_tab[:, :], tf[:, 2, :], float(W), None, ALU.mult))
                link(v.tensor_scalar(hi_tab[:, :], tf[:, 0, :], 1.0 / P, 0.5 / P - 0.5, ALU.mult, ALU.add))
                link(v.tensor_scalar(hi_tab[:, :], hi_tab[:, :], MAGIC, -MAGIC, ALU.add, ALU.add))
                link(v.scalar_tensor_tensor(lo_tab[:, :], hi_tab[:, :], -float(P), tf[:, 0, :], ALU.mult, ALU.add))
                link(v.tensor_scalar(lo_tab[:, :], lo_tab[:, :], -1.0, None, ALU.mult))
                link(v.tensor_scalar(hi_tab[:, :], hi_tab[:, :], float(W), None, ALU.mult))
                dve.wait_ge(s_basebc, 1)
                link(v.tensor_copy(basef_row[:, :], psum[0:1, 0, 0:256]))
                link(v.tensor_tensor(d_tab[:, :].rearrange("p (g t) -> p g t", t=GT),
                                     tf[:, 1, :].rearrange("p (g t) -> p g t", t=GT),
                                     psum[:, 0, 0:G].unsqueeze(2).to_broadcast([128, G, GT]), ALU.subtract))
                dve.wait_ge(s_spanall, 1)
                link(v.tensor_scalar(gstat[:, 2, 0:1], gstat[:, 3, 1:2], 1.0 / W, 0.5 / W - 0.5, ALU.mult, ALU.add))
                link(v.tensor_scalar(gstat[:, 2, 1:2], gstat[:, 2, 0:1], MAGIC, -MAGIC, ALU.add, ALU.add))
                link(v.tensor_scalar(npass[:, :], gstat[:, 2, 1:2], 1.0, None, ALU.add))
        prep_scope.close()

        src_hot = sb("src_hot", [128, 2, GT, 128], BF16, build_scope)
        col_hot = sb("col_hot", [128, 2, GT, W * NT], BF16, build_scope)
        cv = sb("cv", [128, 2, G * GT], FP32, build_scope)
        square = sb("square", [128, 2, GT, 128], FP16, build_scope)
        s_bchain, s_hot, s_sq, s_src, s_outer, s_added = (sem(n) for n in (
            "build_chain", "col_hots_ready", "squares_ready", "src_hots_ready", "outer_done", "window_added"))

        passes = nc.values_load(npass[0:1, 0:1], min_val=1, max_val=N // W + 1)
        with nc.Fori(0, passes):
            with nc.Block() as block:
                @block.vector
                def _(dve):
                    v = nc.vector
                    link = Chain(dve, s_bchain)
                    dw = cv[:, 0, :]
                    inside = cv[:, 1, :]
                    link(v.tensor_scalar(dw, d_tab[:, :], pass_off[:, 0:1], None, ALU.subtract))
                    link(v.tensor_scalar(inside, dw, 0.0, None, ALU.is_ge))
                    link(v.scalar_tensor_tensor(inside, dw, float(W), inside, ALU.is_lt, ALU.mult))
                    link(v.scalar_tensor_tensor(c_tab[:, :], dw, 1.0, hi_tab[:, :], ALU.add, ALU.add))
                    link(v.tensor_tensor(c_tab[:, :], c_tab[:, :], inside, ALU.mult))
                    link(v.tensor_scalar(c_tab[:, :], c_tab[:, :], -1.0, None, ALU.add))
                    link(v.tensor_scalar(base_row[:, :], basef_row[:, :], pass_off[0:1, 0:1], float(N), ALU.add, ALU.min))

                    def one_hots(g, half):
                        for t in range(GT):
                            last = v.tensor_scalar(col_hot[:, half, t, :], iota_h[:, :], c_tab[:, bass.ds(g * GT + t, 1)],
                                                   None, ALU.is_equal)
                        last.then_inc(s_hot, 1)

                    def add_window(g, half):
                        base = dve.value_load(base_row[0:1, bass.ds(g, 1)], min_val=0, max_val=N)
                        dve.wait_ge(s_outer, g + 1)
                        if not (isinstance(g, int) and g == 0):
                            dve.wait_ge(s_added, g)
                        win = adj[:, :, bass.ds(base, W)]
                        v.tensor_tensor(win, win, psum[0:P, half, 0:W * NT].rearrange("p (t w) -> p t w", w=W),
                                        ALU.add).then_inc(s_added, 1)

                    one_hots(0, 0)
                    one_hots(1, 1)
                    add_window(0, 0)
                    with dve.Fori(1, G // 2) as i:
                        g = 2 * i
                        dve.wait_ge(s_outer, g - 1)
                        one_hots(g, 0)
                        add_window(g - 1, 1)
                        one_hots(g + 1, 1)
                        add_window(g, 0)
                    add_window(G - 1, 1)
                    dve.wait_ge(s_added, G)
                    v.tensor_scalar(pass_off[:, :], pass_off[:, :], float(W), None, ALU.add).then_inc(s_bchain, 1)
                    dve.wait_ge(s_bchain, link.count + 1)

                @block.scalar
                def _(act):
                    def one_hots(g, half):
                        for t in range(GT):
                            last = act.activation(square[:, half, t, :], iota_h[:, 0:128], ACT.Square,
                                                  bias=lo_tab[:, bass.ds(g * GT + t, 1)])
                        last.then_inc(s_sq, 1)

                    def relus(g, half):
                        act.wait_ge(s_sq, g + 1)
                        act.activation(src_hot[:, half, :, :], square[:, half, :, :], ACT.Relu, bias=1.0,
                                       scale=-2.0).then_inc(s_src, 1)

                    one_hots(0, 0)
                    relus(0, 0)
                    one_hots(1, 1)
                    with act.Fori(1, G // 2) as i:
                        g = 2 * i
                        act.wait_ge(s_src, g - 1)
                        one_hots(g, 0)
                        act.wait_ge(s_outer, g - 1)
                        relus(g - 1, 1)
                        act.wait_ge(s_src, g)
                        one_hots(g + 1, 1)
                        relus(g, 0)
                    act.wait_ge(s_outer, G - 2)
                    relus(G - 1, 1)

                @block.tensor
                def _(pe):
                    def group(g, half):
                        pe.wait_ge(s_hot, g + 1)
                        pe.wait_ge(s_src, g + 1)
                        for t in range(GT):
                            last = pe.matmul(psum[0:P, half, 0:W * NT], src_hot[:, half, t, 0:P], col_hot[:, half, t, :],
                                             start=(t == 0), stop=(t == GT - 1))
                        last.then_inc(s_outer, 1)

                    group(0, 0)
                    group(1, 1)
                    with pe.Fori(1, G // 2) as i:
                        g = 2 * i
                        pe.wait_ge(s_added, g - 1)
                        group(g, 0)
                        pe.wait_ge(s_added, g)
                        group(g + 1, 1)
            nc.all_engine_barrier(sems_to_clear=None)
            for s in (s_bchain, s_hot, s_sq, s_src, s_outer, s_added):
                nc.sync.sem_clear(s)
            nc.all_engine_barrier()
        build_scope.close()

        def layer_norm_relu(tag, h, tmp, loops=None, load_vecs=False):
            s_c, s_var, s_std = sem(tag + "_ln_chain"), sem(tag + "_ln_var"), sem(tag + "_ln_std")
            with nc.Block() as block:
                if load_vecs:
                    s_vecs1 = sem("all_vecs_in")

                    @block.sync
                    def _(sp):
                        sp.dma_start(vecs[:, :, :], vecs_in[:, 2 * D:].to_broadcast([P, (len(VECS) - 2) * D])).then_inc(s_vecs1, 16)
                        sp.wait_ge(s_vecs1, 16)

                if loops is not None:
                    s_loops = sem(tag + "_self_loops")

                    @block.gpsimd
                    def _(pool):
                        flat = adj[:, :, :].rearrange("p t n -> p (t n)")
                        with pool.Fori(0, NT) as t:
                            own = flat[:, bass.ds(t * (AW + P), P)]
                            pool.tensor_tensor(own, own, ident[0:P, 0:P], loops).then_inc(s_loops, 1)
                        pool.wait_ge(s_loops, NT)

                @block.vector
                def _(dve):
                    v = nc.vector
                    link = Chain(dve, s_c)
                    link(v.tensor_reduce(stat[:, 0, :], x_sb[:, :, :], AX.X, ALU.add))
                    link(v.tensor_scalar(stat[:, 0, :], stat[:, 0, :], 1.0 / D, None, ALU.mult))
                    link(v.tensor_tensor(tmp, x_sb[:, :, :], over_features(stat[:, 0, :]), ALU.subtract))
                    link(v.tensor_tensor(h, tmp, tmp, ALU.mult))
                    link(v.tensor_reduce(stat[:, 1, :], h, AX.X, ALU.add))
                    v.tensor_scalar(stat[:, 1, :], stat[:, 1, :], 1.0 / D, LN_EPS, ALU.mult, ALU.add).then_inc(s_var, 1)
                    dve.wait_ge(s_std, 1)
                    link(v.reciprocal(stat[:, 3, :], stat[:, 2, :]))
                    link(v.scalar_tensor_tensor(h, tmp, 0.0, over_features(stat[:, 3, :]), ALU.max, ALU.mult))

                @block.scalar
                def _(act):
                    act.wait_ge(s_var, 1)
                    act.activation(stat[:, 2, :], stat[:, 1, :], ACT.Sqrt).then_inc(s_std, 1)

        def sage_layer(tag, h, hT, agg, parts, lows, z, bias, w_agg, w_self, mean):
            s_split, s_t, s_tc, s_agg, s_aggc, s_z, s_zc, s_c = (sem(f"{tag}_{n}") for n in (
                "parts_ready", "transposed", "transpose_copied", "aggregated", "aggregate_copied", "projected",
                "projection_read", "sage_chain"))
            blocks = lambda half: psum[:, 2 * half:2 * half + 2, :].rearrange("p a b -> p (a b)")\
                .rearrange("p (t q) -> p t q", q=128)
            with nc.Block() as block:
                @block.vector
                def _(dve):
                    v = nc.vector
                    link = Chain(dve, s_c)
                    if lows is None:
                        v.tensor_copy(parts[:, :, 0:D], h).then_inc(s_c, 1)
                        v.tensor_scalar(z, h, LO_SCALE, None, ALU.mult).then_inc(s_c, 1)
                        link.count = 2
                        dve.wait_ge(s_c, 2)
                        v.scalar_tensor_tensor(parts[:, :, D:2 * D], parts[:, :, 0:D], -LO_SCALE, z,
                                               ALU.mult, ALU.add).then_inc(s_split, 1)
                    else:
                        link(v.tensor_copy(parts[:, :, 0:D], h))
                        link(v.tensor_tensor(z, h, parts[:, :, 0:D], ALU.subtract))
                        link(v.tensor_copy(parts[:, :, D:2 * D], z))
                        v.tensor_tensor(lows, z, parts[:, :, D:2 * D], ALU.subtract).then_inc(s_split, 1)
                    dve.wait_ge(s_split, 1)
                    for c in range(NC):
                        dve.wait_ge(s_z, c + 1)
                        zc = z[:, c * TC:(c + 1) * TC, :]
                        pa = psum[0:P, 4, 0:TC * D].rearrange("p (t d) -> p t d", d=D)
                        ps = psum[0:P, 5, 0:TC * D].rearrange("p (t d) -> p t d", d=D)
                        if mean:
                            link(v.tensor_tensor(zc, pa, over_features(deg[:, c * TC:(c + 1) * TC], TC), ALU.mult))
                            link(v.tensor_tensor(zc, zc, ps, ALU.add))
                            v.tensor_tensor(zc, zc, over_tiles(bias, TC), ALU.add).then_inc(s_zc, 1)
                        else:
                            v.tensor_tensor(zc, pa, over_tiles(bias, TC), ALU.add).then_inc(s_zc, 1)
                    dve.wait_ge(s_zc, NC)

                @block.scalar
                def _(act):
                    for c in range(NC):
                        act.wait_ge(s_agg, c + 1)
                        if c >= 2:
                            act.wait_ge(s_z, c - 1)
                        act.activation(agg[:, c % 2, :].rearrange("p (t q) -> p t q", q=P),
                                       blocks(c % 2)[:, 0:TC, 0:P], ACT.Copy).then_inc(s_aggc, 1)
                        act.wait_ge(s_t, c + 1)
                        act.activation(hT[:, c % 2, :].rearrange("p (t q) -> p t q", q=P),
                                       blocks(3)[0:D, 0:TC, 0:P], ACT.Copy).then_inc(s_tc, 1)

                @block.tensor
                def _(pe):
                    pe.wait_ge(s_split, 1)

                    def spmm(c):
                        if c >= 2:
                            pe.wait_ge(s_aggc, c - 1)
                        o = blocks(c % 2)

                        for k in range(NT):
                            wide = adj[:, k, c * CW:c * CW + 4 * P].rearrange("p (t q) -> p t q", q=P)
                            rest = adj[:, k, c * CW + 4 * P:(c + 1) * CW]
                            for r, o_all, o_low in ((wide, o[:, 0:4, 0:P], o[0:D, 0:4, 0:P]),
                                                    (rest, o[:, 4, 0:P], o[0:D, 4, 0:P])):
                                last = pe.matmul(o_all, parts[:, k, :], r, start=(k == 0),
                                                 stop=(k == NT - 1 and lows is None), skip_group_check=True)
                                if lows is not None:
                                    last = pe.matmul(o_low, lows[:, k, :], r, start=False, stop=(k == NT - 1),
                                                     skip_group_check=True)
                        last.then_inc(s_agg, 1)

                    def transposes(c):
                        if c >= 1:
                            pe.wait_ge(s_tc, c)
                        for t in range(TC):
                            last = pe.transpose(blocks(3)[0:D, t, 0:P], h[:, c * TC + t, :], ident[0:P, 0:P])
                        last.then_inc(s_t, 1)

                    def project(c):
                        pe.wait_ge(s_aggc, c + 1)
                        pe.wait_ge(s_tc, c + 1)
                        if c >= 1:
                            pe.wait_ge(s_zc, c)
                        for t in range(TC):
                            node = slice(t * P, (t + 1) * P)
                            cols = slice(t * D, (t + 1) * D)
                            pe.matmul(psum[0:P, 4, cols], agg[:, c % 2, node], w_agg, start=True, stop=mean)
                            last = pe.matmul(psum[0:P, 5 if mean else 4, cols], hT[:, c % 2, node], w_self,
                                             start=mean, stop=True)
                        last.then_inc(s_z, 1)

                    for c in range(NC + 1):
                        if c < NC:
                            spmm(c)
                            transposes(c)
                        if c >= 1:
                            project(c - 1)

        s_wscale = sem("weights_scaled")
        with nc.Block() as block:
            @block.scalar
            def _(act):
                for name in ("L0_W1l", "L0_W2l", "S_neigh1"):
                    w = mats[D:2 * D, MATS.index(name), :]
                    act.activation(w, w, ACT.Copy, scale=1.0 / LO_SCALE).then_inc(s_wscale, 1)
                act.wait_ge(s_wscale, 3)

        with ExitStack() as scope:
            h = sb("l0_h", [P, NT, D], FP32, scope)
            z = sb("l0_z", [P, NT, D], FP32, scope)
            hT = sb("l0_hT", [D, 2, CW], FP32, scope)
            agg = sb("l0_agg", [128, 2, CW], FP32, scope)
            parts = sb("l0_parts", [P, NT, 2 * D], FP16, scope)
            layer_norm_relu("l0", h[:, :, :], z[:, :, :])
            sage_layer("l0a", h[:, :, :], hT, agg, parts, None, z[:, :, :], vec0("L0_b1"), mat("L0_W1l", 128),
                       mat("L0_W1r"), False)
            s_c, s_ss, s_nrm = sem("l0_norm_chain"), sem("l0_sum_squares"), sem("l0_norm")
            with nc.Block() as block:
                @block.vector
                def _(dve):
                    v = nc.vector
                    link = Chain(dve, s_c)
                    link(v.tensor_scalar(z[:, :, :], z[:, :, :], 0.0, None, ALU.max))
                    link(v.tensor_tensor(h[:, :, :], z[:, :, :], z[:, :, :], ALU.mult))
                    v.tensor_reduce(stat[:, 0, :], h[:, :, :], AX.X, ALU.add).then_inc(s_ss, 1)
                    dve.wait_ge(s_nrm, 1)
                    link(v.tensor_scalar(stat[:, 1, :], stat[:, 1, :], 1e-12, None, ALU.max))
                    link(v.reciprocal(stat[:, 2, :], stat[:, 1, :]))
                    link(v.tensor_tensor(h[:, :, :], z[:, :, :], over_features(stat[:, 2, :]), ALU.mult))

                @block.scalar
                def _(act):
                    act.wait_ge(s_ss, 1)
                    act.activation(stat[:, 1, :], stat[:, 0, :], ACT.Sqrt).then_inc(s_nrm, 1)
            sage_layer("l0b", h[:, :, :], hT, agg, parts, None, z[:, :, :], vec0("L0_b2"), mat("L0_W2l", 128),
                       mat("L0_W2r"), False)
            add_residual(nc, sem("l0_residual"), x_sb, z)
        if STOP == "L0":
            edge_scope.close()
            return store(nc, sem, out, x_sb)

        table = nc.dram_tensor("h_table", [N, D], FP32, kind="Internal").ap()
        with ExitStack() as scope:
            h = sb("l1_h", [P, NT, D], FP32, scope)
            tmp = sb("l1_tmp", [P, NT, D], FP32, scope)
            layer_norm_relu("l1", h[:, :, :], tmp[:, :, :])
            s_hs, s_table = sem("l1_h_scaled"), sem("l1_table_stored")
            cut = 112
            rows = table.rearrange("(t p) d -> p t d", p=P)
            with nc.Block() as block:
                @block.vector
                def _(dve):
                    nc.vector.tensor_scalar(tmp[:, :, :], h[:, :, :], LO_SCALE, None, ALU.mult).then_inc(s_hs, 1)

                @block.sync
                def _(sp):
                    sp.wait_ge(s_hs, 1)
                    sp.dma_start(rows[0:cut], tmp[0:cut, :, :]).then_inc(s_table, 16)
                    sp.dma_start(rows[cut:P], tmp[cut:P, :, :]).then_inc(s_table, 16)
                    sp.wait_ge(s_table, 32)

        with ExitStack() as scope:
            RW = R * W
            aggT = sb("l1_aggT", [D, AW], FP32, scope)
            rel = sb("l1_rel", [2 * D, R, D], FP32, scope)
            idx = sb("l1_idx", [128, 2, GT], U32, scope)
            got = sb("l1_gathered", [128, 2, GT, D], FP32, scope)
            pair = sb("l1_pair", [128, 2, GT, 2 * D], FP16, scope)
            hot = sb("l1_hot", [128, 2, GT, RW], BF16, scope)
            zs = sb("l1_z", [2 * D, R, 2, W], FP32, scope)
            col_tab = sb("l1_col_tab", [128, G * GT], FP32, scope)
            dw_tab = sb("l1_dw_tab", [128, G * GT], FP32, scope)
            ri = zs[:, 0:R // 2, :, :].rearrange("p r a w -> p (r a w)").bitcast(I32)
            rf = sb("l1_iota", [128, RW], FP16, scope)
            s_iw, s_ic, s_rel, s_relc = (sem("l1_" + n) for n in ("iota", "init_chain", "weights_in", "weights_scaled"))
            with nc.Block() as block:
                @block.sync
                def _(sp):
                    sp.dma_start(rel[0:D, :, :], rel_in).then_inc(s_rel, 16)
                    sp.dma_start(rel[D:2 * D, :, :], rel_in).then_inc(s_rel, 16)

                @block.scalar
                def _(act):
                    act.wait_ge(s_rel, 32)
                    act.activation(rel[D:2 * D, :, :], rel[D:2 * D, :, :], ACT.Copy, scale=1.0 / LO_SCALE).then_inc(s_relc, 1)
                    act.wait_ge(s_relc, 1)

                @block.gpsimd
                def _(pool):
                    pool.iota(ri, pattern=[[1, RW]], base=0, channel_multiplier=0).then_inc(s_iw, 1)

                @block.vector
                def _(dve):
                    v = nc.vector
                    link = Chain(dve, s_ic)
                    link(v.memset(aggT[:, :], 0.0))
                    link(v.memset(pass_off[:, :], 0.0))
                    dve.wait_ge(s_iw, 1)
                    link(v.tensor_copy(rf[:, :], ri))
            s_gc, s_ix, s_hot, s_hi, s_pair, s_z, s_zs, s_sum, s_added, s_tick = (sem("l1_" + n) for n in (
                "pass_chain", "indices_ready", "hot_ready", "hi_ready", "pair_ready", "z_in_psum", "z_copied", "summed",
                "window_added", "wait_carrier"))
            s_got = [sem(f"l1_gathered{k}") for k in range(2)]
            with nc.Fori(0, passes):
                with nc.Block() as block:
                    @block.gpsimd
                    def _(pool):
                        def group(g, half):
                            pool.wait_ge(s_ix, g + 1)
                            pool.sem_inc(s_tick, 1)
                            for t in range(GT):
                                pool.indirect_dma_start(
                                    out=got[:, half, t, :], out_offset=None, in_=table[:, :],
                                    in_offset=bass.IndirectOffsetOnAxis(ap=idx[:, half, t:t + 1], axis=0),
                                ).then_inc(s_got[half], 16)

                        group(0, 0)
                        group(1, 1)
                        with pool.Fori(1, G // 2) as i:
                            for half in range(2):
                                pool.wait_ge(s_pair, 2 * i + half - 1)
                                pool.sem_inc(s_tick, 1)
                                group(2 * i + half, half)

                    @block.scalar
                    def _(act):
                        def groups(i, first):
                            for half in range(2):
                                g = 2 * i + half
                                act.wait_ge(s_got[half], 16 * GT * (i + 1))
                                if not first:
                                    act.wait_ge(s_z, g - 1)
                                act.activation(pair[:, half, :, 0:D], got[:, half, :, :], ACT.Copy,
                                               scale=1.0 / LO_SCALE).then_inc(s_hi, 1)
                            for half in range(2):
                                g = 2 * i + half
                                act.wait_ge(s_z, g + 1)
                                if not first:
                                    act.wait_ge(s_sum, i)
                                act.activation(zs[:, :, half, :],
                                               psum[:, half, 0:RW].rearrange("p (r w) -> p r w", w=W), ACT.Copy)\
                                   .then_inc(s_zs, 1)

                        groups(0, True)
                        with act.Fori(1, G // 2) as i:
                            groups(i, False)

                    @block.tensor
                    def _(pe):
                        def groups(i, first):
                            for half in range(2):
                                g = 2 * i + half
                                pe.wait_ge(s_hot, g + 1)
                                pe.wait_ge(s_pair, g + 1)
                                if not first:
                                    pe.wait_ge(s_zs, g - 1)
                                for t in range(GT):
                                    last = pe.matmul(psum[:, half, 0:RW], pair[:, half, t, :], hot[:, half, t, :],
                                                     start=(t == 0), stop=(t == GT - 1))
                                last.then_inc(s_z, 1)
                            pe.wait_ge(s_zs, 2 * i + 2)
                            if not first:
                                pe.wait_ge(s_added, 2 * i)
                            for r in range(R):
                                last = pe.matmul(psum[0:D, 2, 0:2 * W], rel[:, r, :], zs[:, r, :, :], start=(r == 0),
                                                 stop=(r == R - 1))
                            last.then_inc(s_sum, 1)

                        groups(0, True)
                        with pe.Fori(1, G // 2) as i:
                            groups(i, False)

                    @block.vector
                    def _(dve):
                        v = nc.vector
                        link = Chain(dve, s_gc)

                        def indices(g, half):
                            v.tensor_copy(idx[:, half, :], src_tab[:, bass.ds(g * GT, GT)]).then_inc(s_ix, 1)

                        def hots(i, first):
                            for half in range(2):
                                g = 2 * i + half
                                if not first:
                                    dve.wait_ge(s_z, g - 1)
                                for t in range(GT):
                                    last = v.tensor_scalar(hot[:, half, t, :], rf[:, :], col_tab[:, bass.ds(g * GT + t, 1)],
                                                           None, ALU.is_equal)
                                last.then_inc(s_hot, 1)

                        def lows(i):
                            for half in range(2):
                                g = 2 * i + half
                                dve.wait_ge(s_hi, g + 1)
                                v.scalar_tensor_tensor(pair[:, half, :, D:2 * D], pair[:, half, :, 0:D], -LO_SCALE,
                                                       got[:, half, :, :], ALU.mult, ALU.add).then_inc(s_pair, 1)
                                indices(g + 2, half)

                        def add_windows(i, first):
                            for half in range(2):
                                g = 2 * i + half
                                base = dve.value_load(base_row[0:1, bass.ds(g, 1)], min_val=0, max_val=N)
                                dve.wait_ge(s_sum, i + 1)
                                if half or not first:
                                    dve.wait_ge(s_added, g)
                                win = aggT[:, bass.ds(base, W)]
                                v.tensor_tensor(win, win, psum[0:D, 2, half * W:(half + 1) * W], ALU.add).then_inc(s_added, 1)

                        indices(0, 0)
                        indices(1, 1)
                        link(v.tensor_scalar(base_row[:, :], basef_row[:, :], pass_off[0:1, 0:1], float(N), ALU.add, ALU.min))
                        link(v.tensor_scalar(dw_tab[:, :], d_tab[:, :], pass_off[:, 0:1], None, ALU.subtract))
                        link(v.tensor_scalar(col_tab[:, :], dw_tab[:, :], 0.0, None, ALU.is_ge))
                        link(v.scalar_tensor_tensor(col_tab[:, :], dw_tab[:, :], float(W), col_tab[:, :], ALU.is_lt, ALU.mult))
                        link(v.scalar_tensor_tensor(dw_tab[:, :], dw_tab[:, :], 1.0, type_tab[:, :], ALU.add, ALU.add))
                        link(v.tensor_tensor(col_tab[:, :], col_tab[:, :], dw_tab[:, :], ALU.mult))
                        link(v.tensor_scalar(col_tab[:, :], col_tab[:, :], -1.0, None, ALU.add))
                        hots(0, True)
                        lows(0)
                        hots(1, False)
                        add_windows(0, True)
                        lows(1)
                        with dve.Fori(2, G // 2) as i:
                            hots(i, False)
                            add_windows(i - 1, False)
                            lows(i)
                        add_windows(G // 2 - 1, False)
                        link(v.tensor_scalar(pass_off[:, :], pass_off[:, :], float(W), None, ALU.add))
                        dve.wait_ge(s_added, G)
                nc.all_engine_barrier()
                for s in (s_gc, s_ix, s_hot, s_hi, s_pair, s_z, s_zs, s_sum, s_added, s_tick, *s_got):
                    nc.sync.sem_clear(s)
                nc.all_engine_barrier()
            s_t, s_x = sem("l1_agg_transposed"), sem("l1_x_added")
            with nc.Block() as block:
                @block.tensor
                def _(pe):
                    for c in range(NC):
                        if c >= 2:
                            pe.wait_ge(s_x, c - 1)
                        for t in range(TC):
                            node = c * CW + t * P
                            last = pe.transpose(psum[0:P, c % 2, t * D:(t + 1) * D], aggT[:, node:node + P], ident[0:D, 0:D])
                        last.then_inc(s_t, 1)

                @block.vector
                def _(dve):
                    for c in range(NC):
                        dve.wait_ge(s_t, c + 1)
                        tiles = slice(c * TC, (c + 1) * TC)
                        part = psum[0:P, c % 2, 0:TC * D].rearrange("p (t d) -> p t d", d=D)
                        nc.vector.tensor_tensor(x_sb[:, tiles, :], x_sb[:, tiles, :], part, ALU.add).then_inc(s_x, 1)
                    dve.wait_ge(s_x, NC)
        edge_scope.close()
        if STOP == "L1":
            return store(nc, sem, out, x_sb)

        vecs = sb("vecs", [P, len(VECS) - 2, D], FP32)
        with ExitStack() as scope:
            RING = TC
            o_all = sb("gat_o", [P, NT, D + 1], FP32, scope)
            hx = sb("gat_hx", [P, NT, D + 1], FP32, scope)
            ring = sb("gat_ring", [P, RING, CW], FP32, scope)
            rrow = sb("gat_rows", [P, 2, 2, CW], FP32, scope)
            shuttle = sb("gat_shuttle", [P, TC, P], FP32, scope)
            diag = shuttle
            oT = shuttle[0:D + 1, :, :].rearrange("p t q -> p (t q)")
            hcur = sb("gat_hcur", [P, RING, D + 1], FP32, scope)
            node = sb("gat_node", [P, 8, NT], FP32, scope)
            ext = sb("gat_ext", [P, 8], FP32, scope)
            ones16 = sb("ones16", [P, 2], FP16, scope)
            h_in = o_all[:, :, 0:D]
            tmp = ring[:, :, :].rearrange("p a b -> p (a b)")[:, 0:NT * D].rearrange("p (t d) -> p t d", d=D)
            layer_norm_relu("l2", h_in, tmp, ALU.add, load_vecs=True)
            gat_sems = {}

            def gat_sem(name):
                if name not in gat_sems:
                    gat_sems[name] = sem(name)
                return gat_sems[name]

            for layer in range(3):
                if layer > 0:
                    for s in gat_sems.values():
                        nc.sync.sem_clear(s)
                    nc.all_engine_barrier()
                gat_layer(nc, gat_sem, dict(
                    adj=adj, psum=psum, ident=ident, ones=ones, o_all=o_all, hx=hx, ring=ring, rrow=rrow, oT=oT, hcur=hcur,
                    node=node, ext=ext, diag=diag, w=mat(f"G_W{layer + 1}"), a_src=vec(f"G_as{layer + 1}"),
                    a_dst=vec(f"G_ad{layer + 1}"), bias=vec(f"G_b{layer + 1}"), tmp=tmp, over_tiles=over_tiles,
                    over_features=over_features, relu=(layer < 2), deg=deg if layer == 0 else None, ones16=ones16))
            add_residual(nc, sem("l2_residual"), x_sb, o_all, D)
        if STOP == "L2":
            return store(nc, sem, out, x_sb)

        with ExitStack() as scope:
            h = sb("l3_h", [P, NT, D], FP32, scope)
            z = sb("l3_z", [P, NT, D], FP32, scope)
            hT = sb("l3_hT", [D, 2, CW], FP32, scope)
            agg = sb("l3_agg", [128, 2, CW], FP32, scope)
            bn = sb("l3_bn", [P, 3, D], FP32, scope)

            def batch_norm_lrelu(tag, gamma, beta):
                s_c, s_sum, s_sq, s_sumsq, s_var, s_std = (sem(f"{tag}_{n}") for n in (
                    "bn_chain", "bn_sum", "bn_squares", "bn_sum_squares", "bn_var", "bn_std"))
                with nc.Block() as block:
                    @block.tensor
                    def _(pe):
                        for t in range(NT):
                            last = pe.matmul(psum[0:P, 0, 0:D], ones[0:P, 0:P], z[:, t, :], start=(t == 0), stop=(t == NT - 1))
                        last.then_inc(s_sum, 1)
                        pe.wait_ge(s_sq, 1)
                        for t in range(NT):
                            last = pe.matmul(psum[0:P, 1, 0:D], ones[0:P, 0:P], h[:, t, :], start=(t == 0), stop=(t == NT - 1))
                        last.then_inc(s_sumsq, 1)

                    @block.scalar
                    def _(act):
                        act.wait_ge(s_var, 1)
                        act.activation(bn[:, 2, :], bn[:, 1, :], ACT.Sqrt).then_inc(s_std, 1)

                    @block.vector
                    def _(dve):
                        v = nc.vector
                        link = Chain(dve, s_c)
                        dve.wait_ge(s_sum, 1)
                        link(v.tensor_scalar(bn[:, 0, :], psum[0:P, 0, 0:D], 1.0 / N, None, ALU.mult))
                        link(v.tensor_tensor(z[:, :, :], z[:, :, :], over_tiles(bn[:, 0, :]), ALU.subtract))
                        v.tensor_tensor(h[:, :, :], z[:, :, :], z[:, :, :], ALU.mult).then_inc(s_sq, 1)
                        dve.wait_ge(s_sumsq, 1)
                        v.tensor_scalar(bn[:, 1, :], psum[0:P, 1, 0:D], 1.0 / N, LN_EPS, ALU.mult, ALU.add).then_inc(s_var, 1)
                        dve.wait_ge(s_std, 1)
                        link(v.reciprocal(bn[:, 0, :], bn[:, 2, :]))
                        link(v.tensor_tensor(z[:, :, :], z[:, :, :], over_tiles(bn[:, 0, :]), ALU.mult))
                        link(v.tensor_tensor(z[:, :, :], z[:, :, :], over_tiles(gamma), ALU.mult))
                        link(v.tensor_tensor(z[:, :, :], z[:, :, :], over_tiles(beta), ALU.add))
                        link(v.scalar_tensor_tensor(h[:, :, :], z[:, :, :], 0.01, z[:, :, :], ALU.mult, ALU.max))

            with ExitStack() as half_scope:
                parts = sb("l3_parts", [P, NT, 2 * D], FP16, half_scope)
                layer_norm_relu("l3", h[:, :, :], z[:, :, :], ALU.subtract)
                sage_layer("l3a", h[:, :, :], hT, agg, parts, None, z[:, :, :], vec("S_b1"), mat("S_neigh1", 128),
                           mat("S_self1"), True)
            batch_norm_lrelu("l3a", vec("S_gamma1"), vec("S_beta1"))
            with ExitStack() as half_scope:
                parts = sb("l3_parts3", [P, NT, 2 * D], BF16, half_scope)
                lows = sb("l3_lows", [P, NT, D], BF16, half_scope)
                sage_layer("l3b", h[:, :, :], hT, agg, parts, lows[:, :, :], z[:, :, :], vec("S_b2"), mat("S_neigh2", 128),
                           mat("S_self2"), True)
            batch_norm_lrelu("l3b", vec("S_gamma2"), vec("S_beta2"))
            add_residual(nc, sem("l3_residual"), x_sb, h)
        store(nc, sem, out, x_sb)


def gat_layer(nc, sem, b):
    adj, psum, ident, ones, o_all, hx, ring, rrow, oT, hcur, node, ext = (b[k] for k in (
        "adj", "psum", "ident", "ones", "o_all", "hx", "ring", "rrow", "oT", "hcur", "node", "ext"))
    diag = b["diag"]
    a_s, a_d, a_unit, k_s, m_max, m_log, r1, r2 = (node[:, k, :] for k in range(8))
    h_in = o_all[:, :, 0:D]
    tag = "gat_"
    hT = rrow[0:D, 0, :, :]
    blocks = lambda bank: psum[:, bank:bank + 2, :].rearrange("p a b -> p (a b)").rearrange("p (t q) -> p t q", q=128)
    tiled = lambda row: row.rearrange("p (t q) -> p t q", q=P)
    RING = TC
    mx = ring[:, :, :].rearrange("p a q -> p (a q)")

    s_t, s_tc, s_h, s_hc, s_c, s_ext, s_ext2 = (sem(tag + n) for n in (
        "transposed", "transpose_copied", "h_ready", "h_copied", "node_chain", "extremes", "extremes_all"))
    with nc.Block() as block:
        @block.tensor
        def _(pe):
            def transposes(c):
                if c >= 2:
                    pe.wait_ge(s_tc, c - 1)
                for t in range(TC):
                    last = pe.transpose(blocks(2 * (c % 2))[0:D, t, 0:P], h_in[:, c * TC + t, :], ident[0:P, 0:P])
                last.then_inc(s_t, 1)

            transposes(0)
            for c in range(NC):
                if c + 1 < NC:
                    transposes(c + 1)
                pe.wait_ge(s_tc, c + 1)
                if c >= 2:
                    pe.wait_ge(s_hc, c - 1)
                for t in range(TC):
                    last = pe.matmul(psum[0:P, 4 + c % 2, t * D:(t + 1) * D], hT[:, c % 2, t * P:(t + 1) * P], b["w"],
                                     start=True, stop=True)
                last.then_inc(s_h, 1)

        @block.scalar
        def _(act):
            for c in range(NC):
                act.wait_ge(s_t, c + 1)
                if c >= 2:
                    act.wait_ge(s_h, c - 1)
                act.activation(tiled(hT[:, c % 2, :]), blocks(2 * (c % 2))[0:D, 0:TC, 0:P], ACT.Copy).then_inc(s_tc, 1)

        @block.gpsimd
        def _(pool):
            pool.wait_ge(s_ext, 1)
            pool.partition_all_reduce(ext[0:P, 2:4], ext[0:P, 0:2], P, bass.bass_isa.ReduceOp.max).then_inc(s_ext2, 1)

        @block.vector
        def _(dve):
            v = nc.vector
            link = Chain(dve, s_c)
            link(v.memset(hx[:, :, D:D + 1], 1.0))
            for c in range(NC):
                dve.wait_ge(s_h, c + 1)
                v.tensor_copy(hx[:, c * TC:(c + 1) * TC, 0:D],
                              psum[0:P, 4 + c % 2, 0:TC * D].rearrange("p (t d) -> p t d", d=D)).then_inc(s_hc, 1)
            dve.wait_ge(s_hc, NC)
            link(v.tensor_tensor(b["tmp"], hx[:, :, 0:D], b["over_tiles"](b["a_src"]), ALU.mult))
            link(v.tensor_reduce(a_s, b["tmp"], AX.X, ALU.add))
            link(v.tensor_reduce(ext[:, 0:1], a_s, AX.X, ALU.max))
            link(v.tensor_scalar(k_s, a_s, -1.0, None, ALU.mult))
            v.tensor_reduce(ext[:, 1:2], k_s, AX.X, ALU.max).then_inc(s_ext, 1)
            link(v.tensor_tensor(b["tmp"], hx[:, :, 0:D], b["over_tiles"](b["a_dst"]), ALU.mult))
            link(v.tensor_reduce(a_d, b["tmp"], AX.X, ALU.add))
            dve.wait_ge(s_ext2, 1)
            link(v.tensor_tensor(ext[:, 4:5], ext[:, 2:3], ext[:, 3:4], ALU.add))
            link(v.tensor_scalar(ext[:, 4:5], ext[:, 4:5], 1e-30, 2.0, ALU.max, ALU.mult))
            link(v.reciprocal(ext[:, 5:6], ext[:, 4:5]))
            link(v.tensor_scalar(a_unit, a_s, ext[:, 3:4], ext[:, 5:6], ALU.add, ALU.mult))
            link(v.tensor_scalar(a_unit, a_unit, 0.5, None, ALU.add))
            link(v.tensor_scalar(k_s, a_s, -0.8, None, ALU.mult))

    s_m, s_mt, s_mr, s_mc, s_one, s_deg = (sem(tag + n) for n in (
        "max_step", "max_transposed", "max_reduced", "max_chain", "ones16", "degrees_summed"))
    with nc.Block() as block:
        @block.vector
        def _(dve):
            v = nc.vector
            v.tensor_scalar(mx, adj[:, 0, 0:N], a_unit[:, 0:1], None, ALU.min).then_inc(s_m, 1)
            with dve.Fori(1, NT) as k:
                dve.wait_ge(s_m, k)
                v.scalar_tensor_tensor(mx, adj[:, bass.ds(k, 1), 0:N].rearrange("p a q -> p (a q)"),
                                       a_unit[:, bass.ds(k, 1)], mx, ALU.min, ALU.max).then_inc(s_m, 1)
            for c in range(NC):
                dve.wait_ge(s_mt, c + 1)
                v.tensor_reduce(m_max[:, c * TC:(c + 1) * TC], blocks(2 * (c % 2))[0:P, 0:TC, 0:P], AX.X,
                                ALU.max).then_inc(s_mr, 1)
            dve.wait_ge(s_mr, NC)
            link = Chain(dve, s_mc)
            link(v.tensor_scalar(m_max, m_max, -0.5, ext[:, 4:5], ALU.add, ALU.mult))
            if b["deg"] is not None:
                dve.wait_ge(s_deg, 1)
                link(v.tensor_scalar(b["deg"][:, :], psum[0:P, 7, 0:NT], -1.0, 1.0, ALU.add, ALU.max))
                link(v.reciprocal(b["deg"][:, :], b["deg"][:, :]))
            link(v.scalar_tensor_tensor(r2, m_max, ext[:, 3:4], a_d, ALU.subtract, ALU.add))
            link(v.scalar_tensor_tensor(m_log, r2, 0.2, r2, ALU.mult, ALU.max))
            link(v.tensor_tensor(r1, a_d, m_log, ALU.subtract))
            link(v.scalar_tensor_tensor(r2, a_d, 0.2, m_log, ALU.mult, ALU.subtract))

        if b["deg"] is not None:
            @block.gpsimd
            def _(pool):
                pool.memset(b["ones16"][:, :], 1.0).then_inc(s_one, 1)

        @block.tensor
        def _(pe):
            if b["deg"] is not None:
                pe.wait_ge(s_one, 1)

                def degrees(k, first, final):
                    for t in range(NT):
                        last = pe.matmul(psum[0:P, 7, t:t + 1], adj[:, bass.ds(k, 1), t * P:(t + 1) * P]
                                         .rearrange("p a q -> p (a q)"), b["ones16"][:, 0:1], start=(first and t == 0),
                                         stop=(final and t == NT - 1), skip_group_check=True)
                    return last

                degrees(0, True, False)
                with pe.Fori(1, NT - 1) as k:
                    degrees(k, False, False)
                degrees(NT - 1, False, True).then_inc(s_deg, 1)
            for c in range(NC):
                pe.wait_ge(s_m, NT)
                if c >= 2:
                    pe.wait_ge(s_mr, c - 1)
                for t in range(TC):
                    last = pe.transpose(blocks(2 * (c % 2))[0:P, t, 0:P], ring[:, c, t * P:(t + 1) * P], ident[0:P, 0:P])
                last.then_inc(s_mt, 1)

    s_dg, s_rp, s_rr, s_pre, s_exp, s_w, s_mm, s_hcur, s_oT, s_ot, s_oc = (sem(tag + n) for n in (
        "diag_ready", "rows_in_psum", "rows_ready", "exponent_ready", "exp_ready", "weight_ready", "product_done", "hcur_ready",
        "sums_copied", "sums_transposed", "sums_stored"))
    s_tick = sem(tag + "wait_carrier")
    with nc.Block() as block:
        @block.vector
        def _(dve):
            v = nc.vector

            def exponent(c, k, s):
                n = c * NT + k
                if not (c == 0 and isinstance(k, int)):
                    dve.wait_ge(s_mm, n - RING + 1)
                v.scalar_tensor_tensor(ring[:, s, :], rrow[:, c % 2, 1, :], k_s[:, bass.ds(k, 1)], rrow[:, c % 2, 0, :],
                                       ALU.add, ALU.max).then_inc(s_pre, 1)

            def weight(c, k, s):
                n = c * NT + k
                dve.wait_ge(s_exp, n + 1)
                v.scalar_tensor_tensor(ring[:, s, :], ring[:, s, :], 2.0, adj[:, bass.ds(k, 1), c * CW:(c + 1) * CW]
                                       .rearrange("p a q -> p (a q)"), ALU.min, ALU.mult).then_inc(s_w, 1)

            for c in range(NC):
                dve.wait_ge(s_rr, 2 * (c + 1))
                for s in range(RING):
                    exponent(c, s, s)
                    if s >= 2:
                        weight(c, s - 2, s - 2)
                    elif c > 0:
                        weight(c - 1, NT - 2 + s, RING - 2 + s)
                with dve.Fori(1, NT // RING) as i:
                    for s in range(RING):
                        exponent(c, i * RING + s, s)
                        weight(c, i * RING + s - 2, (s - 2) % RING)
            weight(NC - 1, NT - 2, RING - 2)
            weight(NC - 1, NT - 1, RING - 1)

        @block.gpsimd
        def _(pool):
            def copy(c, k, s):
                n = c * NT + k
                if not (c == 0 and isinstance(k, int)):
                    pool.wait_ge(s_mm, n - RING + 1)
                    pool.sem_inc(s_tick, 1)
                pool.tensor_copy(hcur[:, s, :], hx[:, bass.ds(k, 1), :].rearrange("p a d -> p (a d)")).then_inc(s_hcur, 1)

            def diagonals(c):
                for k, r in enumerate((r1, r2)):
                    if c > 0 or k > 0:
                        pool.wait_ge(s_rp, 2 * c + k)
                    if c >= 3 and k == 0:
                        pool.wait_ge(s_ot, c - 2)
                    pool.tensor_tensor(diag[:, :, :], ident[0:P, 0:P].unsqueeze(1).to_broadcast([P, TC, P]),
                                       r[:, c * TC:(c + 1) * TC].unsqueeze(2).to_broadcast([P, TC, P]),
                                       ALU.mult).then_inc(s_dg, 1)

            diagonals(0)
            for c in range(NC):
                for s in range(RING):
                    copy(c, s, s)
                if c + 1 < NC:
                    diagonals(c + 1)
                with pool.Fori(1, NT // RING) as i:
                    for s in range(RING):
                        copy(c, i * RING + s, s)

        @block.scalar
        def _(act):
            def rows(c):
                for k in range(2):
                    act.wait_ge(s_rp, 2 * c + k + 1)
                    if c >= 2:
                        act.wait_ge(s_pre, (c - 1) * NT)
                    act.activation(tiled(rrow[:, c % 2, k, :]), blocks(4)[0:P, 0:TC, 0:P], ACT.Copy).then_inc(s_rr, 1)

            def exp(c, k, s):
                act.wait_ge(s_pre, c * NT + k + 1)
                act.activation(ring[:, s, :], ring[:, s, :], ACT.Exp, bias=a_s[:, bass.ds(k, 1)]).then_inc(s_exp, 1)

            def sums(c):
                act.wait_ge(s_mm, (c + 1) * NT)
                if c > 0:
                    act.wait_ge(s_ot, c)
                act.activation(tiled(oT[:, :]), blocks(2 * (c % 2))[0:D + 1, 0:TC, 0:P], ACT.Copy).then_inc(s_oT, 1)
                act.wait_ge(s_ot, c + 1)
                act.activation(o_all[:, c * TC:(c + 1) * TC, :],
                               psum[0:P, 6, 0:TC * (D + 1)].rearrange("p (t d) -> p t d", d=D + 1), ACT.Copy).then_inc(s_oc, 1)

            rows(0)
            for c in range(NC):
                for s in range(RING):
                    exp(c, s, s)
                if c + 1 < NC:
                    rows(c + 1)
                if c > 0:
                    sums(c - 1)
                with act.Fori(1, NT // RING) as i:
                    for s in range(RING):
                        exp(c, i * RING + s, s)
            sums(NC - 1)

        @block.tensor
        def _(pe):
            def rows(c):
                for k in range(2):
                    if c > 0 or k > 0:
                        pe.wait_ge(s_rr, 2 * c + k)
                    pe.wait_ge(s_dg, 2 * c + k + 1)
                    for t in range(TC):
                        last = pe.matmul(blocks(4)[0:P, t, 0:P], ones[0:P, 0:P], diag[:, t, :], start=True, stop=True)
                    last.then_inc(s_rp, 1)

            def product(c, k, s, first, final):
                n = c * NT + k
                pe.wait_ge(s_w, n + 1)
                pe.wait_ge(s_hcur, n + 1)
                o = blocks(2 * (c % 2))
                pe.matmul(o[0:D + 1, 0:4, 0:P], hcur[:, s, :], tiled(ring[:, s, 0:4 * P]), start=first, stop=final,
                          skip_group_check=True)
                pe.matmul(o[0:D + 1, 4, 0:P], hcur[:, s, :], ring[:, s, 4 * P:], start=first, stop=final,
                          skip_group_check=True).then_inc(s_mm, 1)

            def transposes(c):
                pe.wait_ge(s_oT, c + 1)
                if c > 0:
                    pe.wait_ge(s_oc, c)
                for t in range(TC):
                    last = pe.transpose(psum[0:P, 6, t * (D + 1):(t + 1) * (D + 1)], oT[:, t * P:(t + 1) * P],
                                        ident[0:D + 1, 0:D + 1])
                last.then_inc(s_ot, 1)

            rows(0)
            for c in range(NC):
                if c >= 2:
                    pe.wait_ge(s_oT, c - 1)
                for s in range(RING):
                    product(c, s, s, s == 0, False)
                if c + 1 < NC:
                    rows(c + 1)
                if c > 0:
                    transposes(c - 1)
                with pe.Fori(1, NT // RING - 1) as i:
                    for s in range(RING):
                        product(c, i * RING + s, s, False, False)
                for s in range(RING):
                    product(c, NT - RING + s, s, False, s == RING - 1)
            transposes(NC - 1)

    s_n = sem(tag + "normalise_chain")
    with nc.Block() as block:
        @block.vector
        def _(dve):
            v = nc.vector
            link = Chain(dve, s_n)
            link(v.tensor_scalar(m_max, o_all[:, :, D], 1e-16, None, ALU.add))
            link(v.reciprocal(r1, m_max))
            link(v.tensor_tensor(h_in, h_in, b["over_features"](r1), ALU.mult))
            link(v.tensor_tensor(h_in, h_in, b["over_tiles"](b["bias"]), ALU.add))
            if b["relu"]:
                link(v.tensor_scalar(h_in, h_in, 0.0, None, ALU.max))




def add_residual(nc, s_res, x_sb, z, width=D):
    with nc.Block() as block:
        @block.vector
        def _(dve):
            nc.vector.tensor_tensor(x_sb[:, :, :], x_sb[:, :, :], z[:, :, 0:width], ALU.add).then_inc(s_res, 1)
            dve.wait_ge(s_res, 1)


def store(nc, sem, out, x_sb):
    s_out = sem("out_stored")
    with nc.Block() as block:
        @block.sync
        def _(sp):
            sp.dma_start(out, x_sb[:, :, :]).then_inc(s_out, 16)
            sp.wait_ge(s_out, 16)


def kernel(**inputs):
    import numpy as np
    import concourse.bacc as bacc
    from concourse.bass_utils import run_bass_kernel_spmd

    a = {k: np.asarray(v) for k, v in inputs.items()}

    def edges(v, pad):
        return np.concatenate([v, np.full(G * GE - E, pad, v.dtype)])

    def tiles(v, pad):
        return np.ascontiguousarray(edges(v, pad).reshape(G * GT, ET).T)

    groups = np.full((2 * 128, GE), PAD_DST, a["dst"].dtype)
    groups[:G] = edges(a["dst"], PAD_DST).reshape(G, GE)
    mats = [a["L0_gnn_W1l"].T, a["L0_gnn_W1r"].T, a["L0_gnn_W2l"].T, a["L0_gnn_W2r"].T,
            a["L2_gnn_W1"], a["L2_gnn_W2"], a["L2_gnn_W3"],
            a["L3_gnn_W_self1"].T, a["L3_gnn_W_neigh1"].T, a["L3_gnn_W_self2"].T, a["L3_gnn_W_neigh2"].T]
    vecs = [a[k] for k in ("L0_gnn_b1l", "L0_gnn_b2l", "L2_gnn_a1s", "L2_gnn_a2s", "L2_gnn_a3s", "L2_gnn_a1d",
                           "L2_gnn_a2d", "L2_gnn_a3d", "L2_gnn_b1", "L2_gnn_b2", "L2_gnn_b3", "L3_gnn_b1",
                           "L3_gnn_gamma1", "L3_gnn_beta1", "L3_gnn_b2", "L3_gnn_gamma2", "L3_gnn_beta2")]
    arrays = {
        "x": a["x"].reshape(NT, P, D).transpose(1, 0, 2),
        "dst_groups": groups.reshape(2, 128, GE).transpose(1, 0, 2),
        "src_tiles": tiles(a["src"], 0),
        "dst_tiles": tiles(a["dst"], PAD_DST),
        "type_tiles": tiles(a["edge_type_16"], 0),
        "mats": np.stack(mats, axis=1),
        "vecs": np.concatenate(vecs)[None],
        "rel": a["L1_gnn_weight"].transpose(1, 0, 2).reshape(D, R * D),
    }
    arrays = {"in_" + k: np.ascontiguousarray(v) for k, v in arrays.items()}
    nc = bacc.Bacc("TRN2", target_bir_lowering=False, num_devices=1)
    args = [nc.dram_tensor(k, v.shape, mybir.dt.from_np(v.dtype), kind="ExternalInput").ap() for k, v in arrays.items()]
    out = nc.dram_tensor("out", (P, NT, D), FP32, kind="ExternalOutput").ap()
    gnn(nc, *args, out)
    r = run_bass_kernel_spmd(nc, [arrays], core_ids=[0])
    return np.ascontiguousarray(np.asarray(r.results[0]["out"]).reshape(P, NT, D).transpose(1, 0, 2).reshape(N, D))
```

```python
import concourse.bass as bass
from concourse import mybir
from contextlib import ExitStack

FP32 = mybir.dt.float32
FP16 = mybir.dt.float16
BF16 = mybir.dt.bfloat16
I32 = mybir.dt.int32
U32 = mybir.dt.uint32
ALU = mybir.AluOpType
ACT = mybir.ActivationFunctionType
AX = mybir.AxisListType

N = 3125
D = 64
E = 103125
P = 125
NT = N // P
NC = 5
TC = NT // NC
CW = N // NC
ET = 128
GT = 4
GE = ET * GT
ACT_TILES = 2
G = -(-E // GE)
PAIRS = G // 2
assert G % 4 == 2
W = 20
AW = N + W + (N + W) % 2
R = 16
KEY_BASE = 1024
SELECTS = 5
CUTS = (5, 12, 18)
PAD_DST = 1 << 20
MAGIC = 12582912.0
LO_SCALE = 2048.0
LN_EPS = 1e-5
RING = TC
POOL_SLOTS = [1, 3]

MATS = ["L0_W1l", "L0_W1r", "L0_W2l", "L0_W2r", "G_W1", "G_W2", "G_W3", "S_self1", "S_neigh1", "S_self2", "S_neigh2"]
VECS = ["L0_b1", "L0_b2", "G_as1", "G_as2", "G_as3", "G_ad1", "G_ad2", "G_ad3", "G_b1", "G_b2", "G_b3",
        "S_b1", "S_gamma1", "S_beta1", "S_b2", "S_gamma2", "S_beta2"]


class Chain:

    def __init__(self, eng, sem):
        self.eng, self.sem, self.count = eng, sem, 0

    def __call__(self, ins):
        ins.then_inc(self.sem, 1)
        self.count += 1
        self.eng.wait_ge(self.sem, self.count)
        return ins


def gnn(nc, x_in, dst_groups, src_groups, src_tiles, dst_tiles, type_tiles, mats_in, vecs_in, rel_in, out):
    ctx = ExitStack()
    with ctx:
        names = set()

        def sem(name, scope=None):
            assert name not in names, name
            names.add(name)
            return (scope or ctx).enter_context(nc.semaphore(name))

        def sb(name, shape, dt, scope=None):
            return (scope or ctx).enter_context(nc.sbuf_tensor(name, shape, dt))


        adj = sb("adj", [P, NT, AW], FP16)
        x_sb = sb("x_sb", [P, NT, D], FP32)
        mats = sb("mats", [128, len(MATS), D], FP32)
        ident = sb("ident", [128, 128], FP32)
        ones = sb("ones", [128, 128], FP32)
        deg = sb("deg", [P, NT], FP32)
        stat = sb("stat", [P, 4, NT], FP32)
        vecs0 = sb("vecs0", [P, 2, D], FP32)
        psum = ctx.enter_context(nc.psum_tensor("psum", [128, 8, 512], FP32))

        def mat(name, rows=D):
            return mats[0:rows, MATS.index(name), :]

        def vec(name):
            return vecs[:, VECS.index(name) - 2, :]

        def vec0(name):
            return vecs0[:, VECS.index(name), :]

        def over_tiles(ap2, n=NT):
            return ap2.unsqueeze(1).to_broadcast([P, n, D])

        def over_features(ap2, n=NT, d=D):
            return ap2.unsqueeze(2).to_broadcast([P, n, d])

        edge_scope = ExitStack()
        base_row = sb("base_row", [1, G], I32, edge_scope)
        basef_row = sb("basef_row", [1, G], FP32, edge_scope)
        select = sb("select", [128, SELECTS, GE], FP16, edge_scope)
        d_tab = select[:, :, :].rearrange("p s e -> p (s e)").bitcast(FP32)[:, 0:G * GT]
        type_tab = select[:, :, :].rearrange("p s e -> p (s e)")[:, 2 * G * GT:3 * G * GT]
        src_tab = sb("src_tab", [128, (G + 4) * GT], mybir.dt.int16, edge_scope)
        node_key = sb("node_key", [P, NT], FP32, edge_scope)
        key_table = nc.dram_tensor("key_table", [2 * 128, GE], FP16, kind="Internal").ap()
        npass = sb("npass", [128, 1], I32, edge_scope)
        pass_off = sb("pass_off", [128, 1], FP32, edge_scope)

        build_scope = ExitStack()
        lo_tab = sb("lo_tab", [128, G * GT], FP32, build_scope)
        hi_tab = sb("hi_tab", [128, G * GT], FP32, build_scope)
        c_tab = sb("c_tab", [128, G * GT], FP32, build_scope)
        iota_i = sb("iota_i", [128, W * NT], I32, build_scope)
        iota_neg = sb("iota_neg", [128, 128], FP16, build_scope)
        iota_h = sb("iota_h", [128, W * NT], FP16, build_scope)

        prep_scope = ExitStack()
        dg_i = sb("dg_i", [128, 2, GE], I32, prep_scope)
        dg = dg_i[:, :, :].bitcast(FP32)
        dv = sb("dv", [128, 2, GE], FP32, prep_scope)
        ti = sb("ti", [128, 3, G * GT], I32, prep_scope)
        tf = ti[:, :, :].bitcast(FP32)
        sg_i = sb("sg_i", [128, 2, GE], I32, prep_scope)
        key_i = sg_i[:, 0, :].bitcast(mybir.dt.int16).rearrange("p (k e) -> p k e", e=GE)
        node_i = stat[:, 0, :].bitcast(I32)
        node_h = stat[:, 1, :].bitcast(mybir.dt.int16)[:, 0:NT]
        gstat = sb("gstat", [128, 4, 2], FP32, prep_scope)
        diag = c_tab[:, 0:2 * 128].rearrange("p (k q) -> p k q", q=128)

        s_sg, s_key, s_keys, s_nodes = (sem(n) for n in ("src_groups_in", "keys_ready", "keys_stored", "node_iota"))
        s_dg, s_ti, s_x, s_mats, s_mats2, s_vecs = (sem(n) for n in (
            "dst_groups_in", "edge_tiles_in", "x_in_done", "mats_in_done", "mats_twice_done", "vecs_in_done"))
        s_zeroed, s_zeroed2 = sem("adj_zeroed_by_pool"), sem("adj_zeroed_by_act")
        adj_words = adj[:, :, :].bitcast(FP32).rearrange("p t n -> p (t n)")
        zero_cut = adj_words.shape[1] // 2
        s_iota, s_ident, s_ident2 = sem("iota_ready"), sem("ident_zeroed"), sem("ident_ready")
        s_chain, s_diag, s_basebc, s_span, s_spanall = (sem(n) for n in (
            "prep_chain", "diag_ready", "base_broadcast", "span_ready", "span_over_partitions"))

        block = nc.Block()
        with block as block:
            @block.sync
            def _(sp):
                sp.dma_start(dg_i[:, :, :], dst_groups).then_inc(s_dg, 16)
                sp.dma_start(sg_i[:, :, :], src_groups).then_inc(s_sg, 16)
                sp.dma_start(ti[:, 1, :], dst_tiles).then_inc(s_ti, 16)
                sp.dma_start(ti[:, 0, :], src_tiles).then_inc(s_ti, 16)
                sp.dma_start(ti[:, 2, :], type_tiles).then_inc(s_ti, 16)
                sp.dma_start(x_sb[:, :, :], x_in).then_inc(s_x, 16)
                sp.dma_start(mats[0:D, :, :], mats_in).then_inc(s_mats, 16)
                sp.dma_start(mats[D:2 * D, :, :], mats_in).then_inc(s_mats2, 16)
                sp.dma_start(vecs0[:, :, :], vecs_in[:, 0:2 * D].to_broadcast([P, 2 * D])).then_inc(s_vecs, 16)
                sp.wait_ge(s_key, 1)
                sp.dma_start(key_table.rearrange("(k g) e -> g k e", g=128), key_i.bitcast(FP16)).then_inc(s_keys, 16)
                for s in (s_mats, s_mats2, s_vecs, s_x, s_keys):
                    sp.wait_ge(s, 16)

            @block.gpsimd
            def _(pool):
                pool.iota(iota_i[:, :], pattern=[[1, W * NT]], base=0, channel_multiplier=0).then_inc(s_iota, 1)
                pool.iota(node_i, pattern=[[P, NT]], base=KEY_BASE, channel_multiplier=1).then_inc(s_nodes, 1)
                pool.memset(ident[:, :], 0.0).then_inc(s_ident, 1)
                pool.memset(ones[:, :], 1.0).then_inc(s_ident2, 1)
                pool.memset(adj_words[:, 0:zero_cut], 0.0).then_inc(s_zeroed, 1)
                pool.wait_ge(s_zeroed, 1)
                pool.wait_ge(s_ident, 1)
                pool.affine_select(out=ident[:, :], in_=ident[:, :], compare_op=ALU.not_equal, fill=1.0, base=0,
                                   pattern=[[-1, 128]], channel_multiplier=1).then_inc(s_ident2, 1)
                pool.wait_ge(s_span, 1)
                pool.partition_all_reduce(gstat[:, 3, 1:2], gstat[:, 3, 0:1], 128,
                                          bass.bass_isa.ReduceOp.max).then_inc(s_spanall, 1)

            @block.scalar
            def _(act):
                act.memzero(adj_words[:, zero_cut:]).then_inc(s_zeroed2, 1)
                act.wait_ge(s_zeroed2, 1)

            @block.tensor
            def _(pe):
                pe.wait_ge(s_ident2, 2)
                pe.wait_ge(s_diag, 2)
                pe.matmul(psum[:, 0, 0:256], ones[:, :], diag[:, :, :], start=True, stop=True).then_inc(s_basebc, 1)

            @block.vector
            def _(dve):
                link = Chain(dve, s_chain)
                v = nc.vector
                link(v.memset(pass_off[:, :], 0.0))
                dve.wait_ge(s_iota, 1)
                link(v.tensor_copy(iota_h[:, :], iota_i[:, :]))
                link(v.tensor_scalar(iota_neg[:, :], iota_h[:, 0:128], -1.0, None, ALU.mult))
                dve.wait_ge(s_dg, 16)
                link(v.tensor_copy(dg[:, :, :], dg_i[:, :, :]))
                link(v.tensor_reduce(gstat[:, 0, :], dg[:, :, :], AX.X, ALU.min))
                dve.wait_ge(s_ident2, 2)
                for k in range(2):
                    v.tensor_scalar(diag[:, k, :], ident[:, :], gstat[:, 0, k:k + 1], None, ALU.mult).then_inc(s_diag, 1)
                link(v.scalar_tensor_tensor(dv[:, :, :], dg[:, :, :], float(N), dg[:, :, :], ALU.is_lt, ALU.mult))
                link(v.tensor_reduce(gstat[:, 1, :], dv[:, :, :], AX.X, ALU.max))
                link(v.tensor_tensor(gstat[:, 2, :], gstat[:, 1, :], gstat[:, 0, :], ALU.subtract))
                v.tensor_reduce(gstat[:, 3, 0:1], gstat[:, 2, :], AX.X, ALU.max).then_inc(s_span, 1)
                dve.wait_ge(s_sg, 16)
                link(v.tensor_copy(dv[:, :, :], sg_i[:, :, :]))
                v.tensor_scalar(key_i, dv[:, :, :], float(KEY_BASE), None, ALU.add).then_inc(s_key, 1)
                dve.wait_ge(s_nodes, 1)
                link(v.tensor_copy(node_key[:, :], node_i))
                link(v.tensor_copy(node_h, node_key[:, :]))
                link(v.tensor_copy(node_key[:, :], node_h.bitcast(FP16)))
                dve.wait_ge(s_ti, 48)
                link(v.tensor_copy(tf[:, :, :], ti[:, :, :]))
                link(v.memset(src_tab[:, G * GT:], 0))
                link(v.tensor_copy(src_tab[:, 0:G * GT], tf[:, 0, :]))
                link(v.tensor_scalar(type_tab, tf[:, 2, :], float(W), None, ALU.mult))
                link(v.tensor_scalar(hi_tab[:, :], tf[:, 0, :], 1.0 / P, 0.5 / P - 0.5, ALU.mult, ALU.add))
                link(v.tensor_scalar(hi_tab[:, :], hi_tab[:, :], MAGIC, -MAGIC, ALU.add, ALU.add))
                link(v.scalar_tensor_tensor(lo_tab[:, :], hi_tab[:, :], -float(P), tf[:, 0, :], ALU.mult, ALU.add))
                link(v.tensor_scalar(lo_tab[:, :], lo_tab[:, :], -1.0, None, ALU.mult))
                link(v.tensor_scalar(hi_tab[:, :], hi_tab[:, :], float(W), None, ALU.mult))
                dve.wait_ge(s_basebc, 1)
                link(v.tensor_copy(basef_row[:, :], psum[0:1, 0, 0:G]))
                link(v.tensor_tensor(d_tab.rearrange("p (g t) -> p g t", t=GT),
                                     tf[:, 1, :].rearrange("p (g t) -> p g t", t=GT),
                                     psum[:, 0, 0:G].unsqueeze(2).to_broadcast([128, G, GT]), ALU.subtract))
                dve.wait_ge(s_spanall, 1)
                link(v.tensor_scalar(gstat[:, 2, 0:1], gstat[:, 3, 1:2], 1.0 / W, 0.5 / W - 0.5, ALU.mult, ALU.add))
                link(v.tensor_scalar(gstat[:, 2, 1:2], gstat[:, 2, 0:1], MAGIC, -MAGIC, ALU.add, ALU.add))
                link(v.tensor_scalar(npass[:, :], gstat[:, 2, 1:2], 1.0, None, ALU.add))
        prep_scope.close()

        src_hot = sb("src_hot", [128, 2, GT, 128], BF16, build_scope)
        col_hot = sb("col_hot", [128, 2, GT, W * NT], BF16, build_scope)
        cv = sb("cv", [128, 2, G * GT], FP32, build_scope)
        window = sb("window", [P, 2, W * NT], FP16, build_scope)
        square = sb("square", [128, 2, ACT_TILES, 128], FP16, build_scope)
        s_bchain, s_hot, s_sq, s_src, s_outer, s_window, s_added = (sem(n, build_scope) for n in (
            "build_chain", "col_hots_ready", "squares_ready", "src_hots_ready", "outer_done", "window_copied", "window_added"))

        passes = nc.values_load(npass[0:1, 0:1], min_val=1, max_val=N // W + 1)
        with nc.Fori(0, passes):
            with nc.Block() as block:
                @block.vector
                def _(dve):
                    v = nc.vector
                    link = Chain(dve, s_bchain)
                    dw = cv[:, 0, :]
                    inside = cv[:, 1, :]
                    link(v.tensor_scalar(dw, d_tab, pass_off[:, 0:1], None, ALU.subtract))
                    link(v.tensor_scalar(inside, dw, 0.0, None, ALU.is_ge))
                    link(v.scalar_tensor_tensor(inside, dw, float(W), inside, ALU.is_lt, ALU.mult))
                    link(v.scalar_tensor_tensor(c_tab[:, :], dw, 1.0, hi_tab[:, :], ALU.add, ALU.add))
                    link(v.tensor_tensor(c_tab[:, :], c_tab[:, :], inside, ALU.mult))
                    link(v.tensor_scalar(c_tab[:, :], c_tab[:, :], -1.0, None, ALU.add))
                    link(v.tensor_scalar(base_row[:, :], basef_row[:, :], pass_off[0:1, 0:1], float(N), ALU.add, ALU.min))

                    def one_hots(g, half):
                        for t in range(GT):
                            last = v.tensor_scalar(col_hot[:, half, t, :], iota_h[:, :], c_tab[:, bass.ds(g * GT + t, 1)],
                                                   None, ALU.is_equal)
                        for t in range(ACT_TILES, GT):
                            last = v.tensor_scalar(src_hot[:, half, t, :], iota_neg[:, :], lo_tab[:, bass.ds(g * GT + t, 1)],
                                                   None, ALU.is_equal)
                        last.then_inc(s_hot, 1)

                    one_hots(0, 0)
                    one_hots(1, 1)
                    with dve.Fori(1, G // 2) as i:
                        for half in range(2):
                            dve.wait_ge(s_outer, 2 * i + half - 1)
                            one_hots(2 * i + half, half)
                    v.tensor_scalar(pass_off[:, :], pass_off[:, :], float(W), None, ALU.add).then_inc(s_bchain, 1)
                    dve.wait_ge(s_bchain, link.count + 1)

                @block.gpsimd
                def _(pool):
                    def add_window(g, half):
                        base = pool.value_load(base_row[0:1, bass.ds(g, 1)], min_val=0, max_val=N)
                        pool.wait_ge(s_window, g + 1)
                        if not (isinstance(g, int) and g == 0):
                            pool.wait_ge(s_added, g)
                        win = adj[:, :, bass.ds(base, W)]
                        pool.tensor_tensor(win, win, window[:, half, :].rearrange("p (t w) -> p t w", w=W), ALU.add).then_inc(s_added, 1)

                    pool.wait_ge(s_bchain, 7)
                    add_window(0, 0)
                    add_window(1, 1)
                    with pool.Fori(1, G // 2) as i:
                        for half in range(2):
                            add_window(2 * i + half, half)
                    pool.wait_ge(s_added, G)

                @block.scalar
                def _(act):
                    def one_hots(g, half):
                        for t in range(ACT_TILES):
                            last = act.activation(square[:, half, t, :], iota_h[:, 0:128], ACT.Square,
                                                  bias=lo_tab[:, bass.ds(g * GT + t, 1)])
                        last.then_inc(s_sq, 1)

                    def relus(g, half):
                        act.wait_ge(s_sq, g + 1)
                        act.activation(src_hot[:, half, 0:ACT_TILES, :], square[:, half, :, :], ACT.Relu, bias=1.0,
                                       scale=-2.0).then_inc(s_src, 1)

                    def copy_window(g, half, first):
                        act.wait_ge(s_outer, g + 1)
                        if not first:
                            act.wait_ge(s_added, g - 1)
                        act.activation(window[:, half, :], psum[0:P, half, 0:W * NT], ACT.Copy).then_inc(s_window, 1)

                    one_hots(0, 0)
                    relus(0, 0)
                    one_hots(1, 1)
                    relus(1, 1)

                    def groups(i, first):
                        for half in range(2):
                            g = 2 * i + half
                            act.wait_ge(s_src, g - 1)
                            one_hots(g, half)
                            copy_window(g - 2, half, first)
                            relus(g, half)

                    groups(1, True)
                    with act.Fori(2, G // 2) as i:
                        groups(i, False)
                    copy_window(G - 2, 0, False)
                    copy_window(G - 1, 1, False)

                @block.tensor
                def _(pe):
                    def group(g, half):
                        pe.wait_ge(s_hot, g + 1)
                        pe.wait_ge(s_src, g + 1)
                        for t in range(GT):
                            last = pe.matmul(psum[0:P, half, 0:W * NT], src_hot[:, half, t, 0:P], col_hot[:, half, t, :],
                                             start=(t == 0), stop=(t == GT - 1))
                        last.then_inc(s_outer, 1)

                    group(0, 0)
                    group(1, 1)
                    with pe.Fori(1, G // 2) as i:
                        g = 2 * i
                        pe.wait_ge(s_window, g - 1)
                        group(g, 0)
                        pe.wait_ge(s_window, g)
                        group(g + 1, 1)
            nc.all_engine_barrier(sems_to_clear=None)
            for s in (s_bchain, s_hot, s_sq, s_src, s_outer, s_window, s_added):
                nc.sync.sem_clear(s)
            nc.all_engine_barrier()
        build_scope.close()

        def layer_norm_relu(tag, h, tmp, loops=None, dmas=()):
            s_c, s_var, s_std = sem(tag + "_ln_chain"), sem(tag + "_ln_var"), sem(tag + "_ln_std")
            with nc.Block() as block:
                if dmas:
                    s_moved = sem(tag + "_moved")

                    @block.sync
                    def _(sp):
                        for to, origin in dmas:
                            sp.dma_start(to, origin).then_inc(s_moved, 16)
                        sp.wait_ge(s_moved, 16 * len(dmas))

                if loops is not None:
                    s_loops = sem(tag + "_self_loops")

                    @block.gpsimd
                    def _(pool):
                        flat = adj[:, :, :].rearrange("p t n -> p (t n)")
                        with pool.Fori(0, NT) as t:
                            own = flat[:, bass.ds(t * (AW + P), P)]
                            pool.tensor_tensor(own, own, ident[0:P, 0:P], loops).then_inc(s_loops, 1)
                        pool.wait_ge(s_loops, NT)

                @block.vector
                def _(dve):
                    v = nc.vector
                    link = Chain(dve, s_c)
                    link(v.tensor_reduce(stat[:, 0, :], x_sb[:, :, :], AX.X, ALU.add))
                    link(v.tensor_scalar(stat[:, 0, :], stat[:, 0, :], 1.0 / D, None, ALU.mult))
                    link(v.tensor_tensor(tmp, x_sb[:, :, :], over_features(stat[:, 0, :]), ALU.subtract))
                    link(v.tensor_tensor(h, tmp, tmp, ALU.mult))
                    link(v.tensor_reduce(stat[:, 1, :], h, AX.X, ALU.add))
                    v.tensor_scalar(stat[:, 1, :], stat[:, 1, :], 1.0 / D, LN_EPS, ALU.mult, ALU.add).then_inc(s_var, 1)
                    dve.wait_ge(s_std, 1)
                    link(v.reciprocal(stat[:, 3, :], stat[:, 2, :]))
                    link(v.scalar_tensor_tensor(h, tmp, 0.0, over_features(stat[:, 3, :]), ALU.max, ALU.mult))

                @block.scalar
                def _(act):
                    act.wait_ge(s_var, 1)
                    act.activation(stat[:, 2, :], stat[:, 1, :], ACT.Sqrt).then_inc(s_std, 1)

        def sage_layer(tag, h, hT, agg, parts, scale, z, bias, w_agg, w_self, mean, after_chunk=None, column_sums=False):
            s_scaled, s_high, s_split, s_t, s_tc, s_agg, s_aggc, s_z, s_zc, s_c = (sem(f"{tag}_{n}") for n in (
                "features_scaled", "high_parts_ready", "parts_ready", "transposed", "transpose_copied", "aggregated", "aggregate_copied", "projected",
                "projection_read", "sage_chain"))
            blocks = lambda half: psum[:, 2 * half:2 * half + 2, :].rearrange("p a b -> p (a b)")\
                .rearrange("p (t q) -> p t q", q=128)
            with nc.Block() as block:
                @block.vector
                def _(dve):
                    v = nc.vector
                    link = Chain(dve, s_c)
                    for c in range(NC):
                        tiles = slice(c * TC, (c + 1) * TC)
                        if scale is None:
                            link(v.tensor_scalar(z[:, tiles, :], h[:, tiles, :], LO_SCALE, None, ALU.mult))
                        else:
                            v.scalar_tensor_tensor(z[:, tiles, :], h[:, tiles, :], LO_SCALE, over_tiles(scale, TC),
                                                   ALU.mult, ALU.mult).then_inc(s_scaled, 1)
                            dve.wait_ge(s_scaled, c + 1)
                        dve.wait_ge(s_high, c + 1)
                        v.scalar_tensor_tensor(parts[:, tiles, D:2 * D], parts[:, tiles, 0:D], -LO_SCALE, z[:, tiles, :],
                                               ALU.mult, ALU.add).then_inc(s_split, 1)
                    dve.wait_ge(s_split, NC)
                    for c in range(NC):
                        dve.wait_ge(s_z, c + 1)
                        zc = z[:, c * TC:(c + 1) * TC, :]
                        pa = psum[0:P, 4, 0:TC * D].rearrange("p (t d) -> p t d", d=D)
                        ps = psum[0:P, 5, 0:TC * D].rearrange("p (t d) -> p t d", d=D)
                        if mean:
                            link(v.tensor_tensor(zc, pa, over_features(deg[:, c * TC:(c + 1) * TC], TC), ALU.mult))
                            link(v.tensor_tensor(zc, zc, ps, ALU.add))
                            v.tensor_tensor(zc, zc, over_tiles(bias, TC), ALU.add).then_inc(s_zc, 1)
                        else:
                            v.tensor_tensor(zc, pa, over_tiles(bias, TC), ALU.add).then_inc(s_zc, 1)
                        if after_chunk is not None:
                            dve.wait_ge(s_zc, c + 1)
                            after_chunk(link, slice(c * TC, (c + 1) * TC))
                    dve.wait_ge(s_zc, NC)

                @block.scalar
                def _(act):
                    for c in range(NC):
                        tiles = slice(c * TC, (c + 1) * TC)
                        if scale is None:
                            act.activation(parts[:, tiles, 0:D], h[:, tiles, :], ACT.Copy).then_inc(s_high, 1)
                        else:
                            act.wait_ge(s_scaled, c + 1)
                            act.activation(parts[:, tiles, 0:D], z[:, tiles, :], ACT.Copy,
                                           scale=1.0 / LO_SCALE).then_inc(s_high, 1)
                    for c in range(NC):
                        act.wait_ge(s_agg, c + 1)
                        if c >= 2:
                            act.wait_ge(s_z, c - 1)
                        act.activation(agg[:, c % 2, :].rearrange("p (t q) -> p t q", q=P),
                                       blocks(c % 2)[:, 0:TC, 0:P], ACT.Copy).then_inc(s_aggc, 1)
                        act.wait_ge(s_t, c + 1)
                        act.activation(hT[:, c % 2, :].rearrange("p (t q) -> p t q", q=P),
                                       blocks(3)[0:D, 0:TC, 0:P], ACT.Copy).then_inc(s_tc, 1)

                @block.tensor
                def _(pe):
                    def spmm(c):
                        if c >= 2:
                            pe.wait_ge(s_aggc, c - 1)
                        o = blocks(c % 2)

                        for k in range(NT):
                            if c == 0 and k % TC == 0:
                                pe.wait_ge(s_split, k // TC + 1)
                            wide = adj[:, k, c * CW:c * CW + 4 * P].rearrange("p (t q) -> p t q", q=P)
                            rest = adj[:, k, c * CW + 4 * P:(c + 1) * CW]
                            for r, sums in ((wide, o[:, 0:4, 0:P]), (rest, o[:, 4, 0:P])):
                                last = pe.matmul(sums, parts[:, k, :], r, start=(k == 0), stop=(k == NT - 1),
                                                 skip_group_check=True)
                        last.then_inc(s_agg, 1)

                    def transposes(c):
                        if c >= 1:
                            pe.wait_ge(s_tc, c)
                        for t in range(TC):
                            last = pe.transpose(blocks(3)[0:D, t, 0:P], h[:, c * TC + t, :], ident[0:P, 0:P])
                        last.then_inc(s_t, 1)

                    def project(c):
                        pe.wait_ge(s_aggc, c + 1)
                        pe.wait_ge(s_tc, c + 1)
                        if c >= 1:
                            pe.wait_ge(s_zc, c)
                        for t in range(TC):
                            node = slice(t * P, (t + 1) * P)
                            cols = slice(t * D, (t + 1) * D)
                            pe.matmul(psum[0:P, 4, cols], agg[:, c % 2, node], w_agg, start=True, stop=mean)
                            last = pe.matmul(psum[0:P, 5 if mean else 4, cols], hT[:, c % 2, node], w_self,
                                             start=mean, stop=True)
                        last.then_inc(s_z, 1)

                    def sums_over_nodes(c):
                        pe.wait_ge(s_zc, c + 1)
                        bank, place = (5, c) if c < 3 else (4, c - 3)
                        at = TC * D + place * D
                        for t in range(TC):
                            pe.matmul(psum[0:P, bank, at:at + D], ones[0:P, 0:P], z[:, c * TC + t, :], start=(t == 0),
                                      stop=(t == TC - 1))

                    for c in range(NC + 1):
                        if c < NC:
                            spmm(c)
                            transposes(c)
                        if c >= 2 and column_sums:
                            sums_over_nodes(c - 2)
                        if c >= 1:
                            project(c - 1)
                    if column_sums:
                        sums_over_nodes(NC - 1)

        s_wscale = sem("weights_scaled")
        with nc.Block() as block:
            @block.scalar
            def _(act):
                for name in ("L0_W1l", "L0_W2l", "S_neigh1"):
                    w = mats[D:2 * D, MATS.index(name), :]
                    act.activation(w, w, ACT.Copy, scale=1.0 / LO_SCALE).then_inc(s_wscale, 1)
                act.wait_ge(s_wscale, 3)

        with ExitStack() as scope:
            h = sb("l0_h", [P, NT, D], FP32, scope)
            z = sb("l0_z", [P, NT, D], FP32, scope)
            hT = sb("l0_hT", [D, 2, CW], FP32, scope)
            agg = sb("l0_agg", [128, 2, CW], FP32, scope)
            parts = sb("l0_parts", [P, NT, 2 * D], FP16, scope)
            layer_norm_relu("l0", h[:, :, :], z[:, :, :])

            def relu_and_squares(link, tiles):
                v, zc, hc = nc.vector, z[:, tiles, :], h[:, tiles, :]
                link(v.tensor_scalar(zc, zc, 0.0, None, ALU.max))
                link(v.tensor_tensor(hc, zc, zc, ALU.mult))
                link(v.tensor_reduce(stat[:, 0, tiles], hc, AX.X, ALU.add))

            sage_layer("l0a", h[:, :, :], hT, agg, parts, None, z[:, :, :], vec0("L0_b1"), mat("L0_W1l", 128),
                       mat("L0_W1r"), False, after_chunk=relu_and_squares)
            s_c, s_nrm = sem("l0_norm_chain"), sem("l0_norm")
            with nc.Block() as block:
                @block.vector
                def _(dve):
                    v = nc.vector
                    link = Chain(dve, s_c)
                    dve.wait_ge(s_nrm, 1)
                    link(v.tensor_scalar(stat[:, 1, :], stat[:, 1, :], 1e-12, None, ALU.max))
                    link(v.reciprocal(stat[:, 2, :], stat[:, 1, :]))
                    link(v.tensor_tensor(h[:, :, :], z[:, :, :], over_features(stat[:, 2, :]), ALU.mult))

                @block.scalar
                def _(act):
                    act.activation(stat[:, 1, :], stat[:, 0, :], ACT.Sqrt).then_inc(s_nrm, 1)
            sage_layer("l0b", h[:, :, :], hT, agg, parts, None, z[:, :, :], vec0("L0_b2"), mat("L0_W2l", 128),
                       mat("L0_W2r"), False)
            add_residual(nc, sem("l0_residual"), x_sb, z)

        x_saved = nc.dram_tensor("x_saved", [P, NT * D], FP32, kind="Internal").ap()
        x_flat = x_sb[:, :, :].rearrange("p t d -> p (t d)")
        h_parts = x_flat.bitcast(FP16).rearrange("p (t d) -> p t d", d=2 * D)
        select_flat = select[:, :, :].rearrange("p s e -> p (s e)")[:, 0:3 * G * GT]
        edge_saved = nc.dram_tensor("edge_saved", [128, 3 * G * GT], FP16, kind="Internal").ap()
        table = nc.dram_tensor("h_table", [N, D], FP32, kind="Internal").ap()
        with ExitStack() as scope:
            h = sb("l1_h", [P, NT, D], FP32, scope)
            tmp = sb("l1_tmp", [P, NT, D], FP32, scope)
            layer_norm_relu("l1", h[:, :, :], tmp[:, :, :], dmas=[(x_saved, x_flat), (edge_saved, select_flat)])
            s_hs, s_table, s_hp, s_lp = (sem("l1_" + n) for n in ("h_scaled", "table_stored", "high_parts", "low_parts"))
            cut = 112
            rows = table.rearrange("(t p) d -> p t d", p=P)
            with nc.Block() as block:
                @block.vector
                def _(dve):
                    nc.vector.tensor_scalar(tmp[:, :, :], h[:, :, :], LO_SCALE, None, ALU.mult).then_inc(s_hs, 1)
                    dve.wait_ge(s_hp, 1)
                    dve.wait_ge(s_hs, 1)
                    nc.vector.scalar_tensor_tensor(h_parts[:, :, D:2 * D], h_parts[:, :, 0:D], -LO_SCALE, tmp[:, :, :],
                                                   ALU.mult, ALU.add).then_inc(s_lp, 1)
                    dve.wait_ge(s_lp, 1)

                @block.scalar
                def _(act):
                    act.activation(h_parts[:, :, 0:D], h[:, :, :], ACT.Copy).then_inc(s_hp, 1)

                @block.sync
                def _(sp):
                    sp.wait_ge(s_hs, 1)
                    sp.dma_start(rows[0:cut], tmp[0:cut, :, :]).then_inc(s_table, 16)
                    sp.dma_start(rows[cut:P], tmp[cut:P, :, :]).then_inc(s_table, 16)
                    sp.wait_ge(s_table, 32)

        with ExitStack() as scope:
            RW = R * W
            aggT = sb("l1_aggT", [D, AW], FP32, scope)
            rel = sb("l1_rel", [2 * D, R, D], FP32, scope)
            idx = sb("l1_idx", [128, 3, GT], U32, scope)
            got = sb("l1_gathered", [128, 3, GT, D], FP32, scope)
            key_row = sb("l1_key_row", [P, 2, GE], FP16, scope)
            pair = sb("l1_pair", [128, 2, GT, 2 * D], FP16, scope)
            hot = sb("l1_hot", [128, 2, GT, RW], BF16, scope)
            zs = sb("l1_z", [2 * D, R, 2, W], FP32, scope)
            col_tab = sb("l1_col_tab", [128, G * GT], FP32, scope)
            dw_tab = hot[:, :, :, :].rearrange("p a t w -> p (a t w)").bitcast(FP32)[:, 0:G * GT]
            ri = zs[:, 0:R // 2, :, :].rearrange("p r a w -> p (r a w)").bitcast(I32)
            rf = sb("l1_iota", [128, RW], FP16, scope)
            s_iw, s_ic, s_rel, s_relc, s_az, s_pz = (sem("l1_" + n) for n in (
                "iota", "init_chain", "weights_in", "weights_scaled", "zeroed_by_act", "zeroed_by_pool"))
            with nc.Block() as block:
                @block.sync
                def _(sp):
                    sp.dma_start(rel[0:D, :, :], rel_in).then_inc(s_rel, 16)
                    sp.dma_start(rel[D:2 * D, :, :], rel_in).then_inc(s_rel, 16)

                @block.scalar
                def _(act):
                    act.memzero(aggT[:, AW // 3:2 * (AW // 3)]).then_inc(s_az, 1)
                    act.wait_ge(s_az, 1)
                    act.wait_ge(s_rel, 32)
                    act.activation(rel[D:2 * D, :, :], rel[D:2 * D, :, :], ACT.Copy, scale=1.0 / LO_SCALE).then_inc(s_relc, 1)
                    act.wait_ge(s_relc, 1)

                @block.gpsimd
                def _(pool):
                    pool.iota(ri, pattern=[[1, RW]], base=0, channel_multiplier=0).then_inc(s_iw, 1)
                    pool.memset(aggT[:, 2 * (AW // 3):], 0.0).then_inc(s_pz, 1)
                    pool.wait_ge(s_pz, 1)

                @block.vector
                def _(dve):
                    v = nc.vector
                    link = Chain(dve, s_ic)
                    link(v.memset(aggT[:, 0:AW // 3], 0.0))
                    link(v.memset(pass_off[:, :], 0.0))
                    dve.wait_ge(s_iw, 1)
                    link(v.tensor_copy(rf[:, :], ri))
            s_gc, s_ix, s_hot, s_hi, s_pair, s_z, s_zs, s_sum, s_added, s_tick = (sem("l1_" + n, scope) for n in (
                "pass_chain", "indices_ready", "hot_ready", "hi_ready", "pair_ready", "z_in_psum", "z_copied", "summed",
                "window_added", "wait_carrier"))
            s_asq, s_ahot, s_tab, s_sel, s_selmm, s_picked, s_ppair = (sem("l1_" + n, scope) for n in (
                "first_squares", "first_hot_ready", "edge_tables_back", "select_ready", "select_used", "rows_picked", "picked_pair_ready"))
            s_got = [sem(f"l1_gathered{k}", scope) for k in range(3)]
            s_key = [sem(f"l1_keys_in{k}", scope) for k in range(2)]
            TURNS = PAIRS // 2
            with nc.Fori(0, passes):
                with nc.Block() as block:
                    @block.sync
                    def _(sp):
                        sp.dma_start(select_flat, edge_saved).then_inc(s_tab, 16)

                        def keys(j, slot):
                            row = key_table[bass.ds(4 * j + 1, 1), :]
                            sp.dma_start(key_row[:, slot, :], row.to_broadcast([P, GE])).then_inc(s_key[slot], 16)

                        keys(1, 1)
                        keys(2, 0)
                        with sp.Fori(2, TURNS // 2 + 1) as q:
                            for j, slot in ((2 * q - 1, 1), (2 * q, 0)):
                                sp.wait_ge(s_sel, NT * (j - 2))
                                keys(j, slot)

                    @block.gpsimd
                    def _(pool):
                        def fetch(m, slot, first):
                            if not first:
                                pool.wait_ge(s_pair, m - 2)
                                pool.sem_inc(s_tick, 1)
                            pool.wait_ge(s_ix, m + 1)
                            pool.sem_inc(s_tick, 1)
                            for t in range(GT):
                                pool.indirect_dma_start(
                                    out=got[:, slot, t, :], out_offset=None, in_=table[:, :],
                                    in_offset=bass.IndirectOffsetOnAxis(ap=idx[:, slot, t:t + 1], axis=0),
                                ).then_inc(s_got[slot], 16)

                        for m in range(5):
                            fetch(m, m % 3, m < 3)
                        with pool.Fori(2, TURNS + 1) as j:
                            for r in range(3):
                                fetch(3 * j - 1 + r, (r + 2) % 3, False)

                    @block.scalar
                    def _(act):
                        def hi(g, half, slot, uses):
                            act.wait_ge(s_got[slot], 16 * GT * uses)
                            if not (isinstance(g, int) and g < 2):
                                act.wait_ge(s_z, g - 1)
                            act.activation(pair[:, half, :, 0:D], got[:, slot, :, :], ACT.Copy,
                                           scale=1.0 / LO_SCALE).then_inc(s_hi, 1)

                        def picked(j):
                            g = 4 * j + 1
                            act.wait_ge(s_picked, j)
                            act.wait_ge(s_z, g - 1)
                            act.activation(pair[:, 1, :, :].rearrange("p t d -> p (t d)"), psum[:, 3, :], ACT.Copy)\
                               .then_inc(s_ppair, 1)

                        def z_out(g, half, i):
                            act.wait_ge(s_z, g + 1)
                            if not (isinstance(i, int) and i == 0):
                                act.wait_ge(s_sum, i)
                            act.activation(zs[:, :, half, :], psum[:, half, 0:RW].rearrange("p (r w) -> p r w", w=W),
                                           ACT.Copy).then_inc(s_zs, 1)

                        def first_hot(g, half):
                            act.wait_ge(s_z, g - 1)
                            tile = hot[:, half, 0, :]
                            act.activation(tile, rf[:, :], ACT.Square, scale=-1.0,
                                           bias=col_tab[:, bass.ds(g * GT, 1)]).then_inc(s_asq, 1)
                            act.wait_ge(s_asq, g - 1)
                            act.activation(tile, tile, ACT.Relu, scale=-2.0, bias=1.0).then_inc(s_ahot, 1)

                        def turn(j, last=False):
                            hi(4 * j - 1, 1, 0, j + 1)
                            z_out(4 * j - 2, 0, 2 * j - 1)
                            hi(4 * j, 0, 1, j + 1)
                            first_hot(4 * j, 0)
                            z_out(4 * j - 1, 1, 2 * j - 1)
                            first_hot(4 * j + 1, 1)
                            z_out(4 * j, 0, 2 * j)
                            if not last:
                                hi(4 * j + 2, 0, 2, j + 1)
                                first_hot(4 * j + 2, 0)
                            picked(j)
                            z_out(4 * j + 1, 1, 2 * j)
                            if not last:
                                first_hot(4 * j + 3, 1)

                        hi(0, 0, 0, 1)
                        hi(1, 1, 1, 1)
                        z_out(0, 0, 0)
                        act.wait_ge(s_gc, 7)
                        hi(2, 0, 2, 1)
                        first_hot(2, 0)
                        z_out(1, 1, 0)
                        first_hot(3, 1)
                        with act.Fori(1, TURNS) as j:
                            turn(j)
                        turn(TURNS, True)

                    @block.tensor
                    def _(pe):
                        def z(g, half, s_ready, count):
                            pe.wait_ge(s_hot, g + 1)
                            if not (isinstance(g, int) and g < 2):
                                pe.wait_ge(s_ahot, g - 1)
                            pe.wait_ge(s_ready, count)
                            if not (isinstance(g, int) and g < 2):
                                pe.wait_ge(s_zs, g - 1)
                            for t in range(GT):
                                last = pe.matmul(psum[:, half, 0:RW], pair[:, half, t, :], hot[:, half, t, :],
                                                 start=(t == 0), stop=(t == GT - 1))
                            last.then_inc(s_z, 1)

                        def outputs(i, first=False):
                            pe.wait_ge(s_zs, 2 * i + 2)
                            if not first:
                                pe.wait_ge(s_added, 2 * i)
                            for r in range(R):
                                last = pe.matmul(psum[0:D, 2, 0:2 * W], rel[:, r, :], zs[:, r, :, :], start=(r == 0),
                                                 stop=(r == R - 1))
                            last.then_inc(s_sum, 1)

                        def pick(j, lo, hi):
                            for k in range(lo, hi):
                                if k == 0 and not isinstance(j, int):
                                    pe.wait_ge(s_ppair, j - 1)
                                pe.wait_ge(s_sel, NT * (j - 1) + k + 1)
                                for t in range(GT):
                                    edge = slice(t * ET, (t + 1) * ET)
                                    last = pe.matmul(psum[:, 3, edge], select[0:P, k % SELECTS, edge], h_parts[:, k, :],
                                                     start=(k == 0 and t == 0), stop=(k == NT - 1 and t == GT - 1),
                                                     skip_group_check=True)
                                last.then_inc(s_selmm, 1)
                            if hi == NT:
                                pe.wait_ge(s_selmm, NT * j)
                                pe.sem_inc(s_picked, 1)

                        def turn(j):
                            pick(j, 0, CUTS[0])
                            outputs(2 * j - 2, isinstance(j, int))
                            z(4 * j - 2, 0, s_pair, 3 * j)
                            pick(j, CUTS[0], CUTS[1])
                            z(4 * j - 1, 1, s_pair, 3 * j + 1)
                            pick(j, CUTS[1], CUTS[2])
                            outputs(2 * j - 1)
                            z(4 * j, 0, s_pair, 3 * j + 2)
                            pick(j, CUTS[2], NT)
                            z(4 * j + 1, 1, s_ppair, j)

                        z(0, 0, s_pair, 1)
                        z(1, 1, s_pair, 2)
                        turn(1)
                        with pe.Fori(2, TURNS + 1) as j:
                            turn(j)
                        outputs(PAIRS - 1)

                    @block.vector
                    def _(dve):
                        v = nc.vector
                        link = Chain(dve, s_gc)

                        def indices(g, slot):
                            v.tensor_copy(idx[:, slot, :], src_tab[:, bass.ds(g * GT, GT)]).then_inc(s_ix, 1)

                        def hots(g, half):
                            if not (isinstance(g, int) and g < 2):
                                dve.wait_ge(s_z, g - 1)
                            for t in range(0 if isinstance(g, int) and g < 2 else 1, GT):
                                last = v.tensor_scalar(hot[:, half, t, :], rf[:, :], col_tab[:, bass.ds(g * GT + t, 1)],
                                                       None, ALU.is_equal)
                            last.then_inc(s_hot, 1)

                        def lows(g, half, m, slot, next_g):
                            dve.wait_ge(s_hi, m + 1)
                            v.scalar_tensor_tensor(pair[:, half, :, D:2 * D], pair[:, half, :, 0:D], -LO_SCALE,
                                                   got[:, slot, :, :], ALU.mult, ALU.add).then_inc(s_pair, 1)
                            indices(next_g, slot)

                        def selects(j, slot, uses, lo, hi):
                            if lo == 0:
                                dve.wait_ge(s_key[slot], 16 * uses)
                            for k in range(lo, hi):
                                if not (isinstance(j, int) and j == 1 and k < SELECTS):
                                    dve.wait_ge(s_selmm, NT * (j - 1) + k + 1 - SELECTS)
                                v.tensor_scalar(select[0:P, k % SELECTS, :], key_row[:, slot, :], node_key[:, k:k + 1],
                                                None, ALU.is_equal).then_inc(s_sel, 1)

                        def window_bases(i):
                            return [dve.value_load(base_row[0:1, bass.ds(2 * i + half, 1)], min_val=0, max_val=N)
                                    for half in range(2)]

                        def add_windows(i, bases, first=False):
                            for half, base in enumerate(bases):
                                g = 2 * i + half
                                dve.wait_ge(s_sum, i + 1)
                                if half or not first:
                                    dve.wait_ge(s_added, g)
                                win = aggT[:, bass.ds(base, W)]
                                v.tensor_tensor(win, win, psum[0:D, 2, half * W:(half + 1) * W], ALU.add).then_inc(s_added, 1)

                        def turn(j, slot, uses, first=False):
                            hots(4 * j - 2, 0)
                            selects(j, slot, uses, 0, CUTS[0])
                            lows(4 * j - 2, 0, 3 * j - 1, 2, 4 * j + 2)
                            hots(4 * j - 1, 1)
                            bases = window_bases(2 * j - 2)
                            selects(j, slot, uses, CUTS[0], CUTS[1])
                            lows(4 * j - 1, 1, 3 * j, 0, 4 * j + 3)
                            add_windows(2 * j - 2, bases, first)
                            hots(4 * j, 0)
                            selects(j, slot, uses, CUTS[1], CUTS[2])
                            lows(4 * j, 0, 3 * j + 1, 1, 4 * j + 4)
                            hots(4 * j + 1, 1)
                            bases = window_bases(2 * j - 1)
                            selects(j, slot, uses, CUTS[2], NT)
                            add_windows(2 * j - 1, bases)

                        for m in range(3):
                            indices(m, m)
                        dve.wait_ge(s_tab, 16)
                        link(v.tensor_scalar(base_row[:, :], basef_row[:, :], pass_off[0:1, 0:1], float(N), ALU.add, ALU.min))
                        link(v.tensor_scalar(dw_tab, d_tab, pass_off[:, 0:1], None, ALU.subtract))
                        link(v.tensor_scalar(col_tab[:, :], dw_tab, 0.0, None, ALU.is_ge))
                        link(v.scalar_tensor_tensor(col_tab[:, :], dw_tab, float(W), col_tab[:, :], ALU.is_lt, ALU.mult))
                        link(v.scalar_tensor_tensor(dw_tab, dw_tab, 1.0, type_tab, ALU.add, ALU.add))
                        link(v.tensor_tensor(col_tab[:, :], col_tab[:, :], dw_tab, ALU.mult))
                        link(v.tensor_scalar(col_tab[:, :], col_tab[:, :], -1.0, None, ALU.add))
                        hots(0, 0)
                        hots(1, 1)
                        lows(0, 0, 0, 0, 3)
                        lows(1, 1, 1, 1, 4)
                        turn(1, 1, 1, True)
                        turn(2, 0, 1)
                        with dve.Fori(2, TURNS // 2 + 1) as q:
                            turn(2 * q - 1, 1, q)
                            turn(2 * q, 0, q)
                        add_windows(PAIRS - 1, window_bases(PAIRS - 1))
                        link(v.tensor_scalar(pass_off[:, :], pass_off[:, :], float(W), None, ALU.add))
                        dve.wait_ge(s_added, G)
                nc.all_engine_barrier()
                nc.gpsimd.dma_reset()
                nc.all_engine_barrier()
                for s in (s_gc, s_ix, s_hot, s_hi, s_pair, s_z, s_zs, s_sum, s_added, s_tick, s_asq, s_ahot, s_tab, s_sel, s_selmm, s_picked,
                          s_ppair, *s_got, *s_key):
                    nc.sync.sem_clear(s)
                nc.all_engine_barrier()
            s_t, s_x, s_xb = sem("l1_agg_transposed"), sem("l1_x_added"), sem("l1_x_back")
            with nc.Block() as block:
                @block.sync
                def _(sp):
                    sp.dma_start(x_flat, x_saved).then_inc(s_xb, 16)

                @block.tensor
                def _(pe):
                    for c in range(NC):
                        if c >= 2:
                            pe.wait_ge(s_x, c - 1)
                        for t in range(TC):
                            node = c * CW + t * P
                            last = pe.transpose(psum[0:P, c % 2, t * D:(t + 1) * D], aggT[:, node:node + P], ident[0:D, 0:D])
                        last.then_inc(s_t, 1)

                @block.vector
                def _(dve):
                    dve.wait_ge(s_xb, 16)
                    for c in range(NC):
                        dve.wait_ge(s_t, c + 1)
                        tiles = slice(c * TC, (c + 1) * TC)
                        part = psum[0:P, c % 2, 0:TC * D].rearrange("p (t d) -> p t d", d=D)
                        nc.vector.tensor_tensor(x_sb[:, tiles, :], x_sb[:, tiles, :], part, ALU.add).then_inc(s_x, 1)
                    dve.wait_ge(s_x, NC)
        edge_scope.close()

        vecs = sb("vecs", [P, len(VECS) - 2, D], FP32)
        with ExitStack() as scope:
            o_all = sb("gat_o", [P, NT, D + 1], FP32, scope)
            hx = sb("gat_hx", [P, NT, D + 1], FP32, scope)
            ring = sb("gat_ring", [P, RING, CW], FP32, scope)
            rrow = sb("gat_rows", [P, 2, 2, CW], FP32, scope)
            oT = sb("gat_oT", [D + 1, CW], FP32, scope)
            row_table = nc.dram_tensor("row_table", [NC, 2 * CW], FP32, kind="Internal").ap()
            rT = sb("gat_rT", [4 * TC, P], FP32, scope)
            node = sb("gat_node", [P, 7, NT], FP32, scope)
            rr = sb("gat_shifts", [P, NC, 2, TC], FP32, scope)
            ext = sb("gat_ext", [P, 8], FP32, scope)
            ones16 = sb("ones16", [P, 2], FP16, scope)
            h_in = o_all[:, :, 0:D]
            tmp = ring[:, :, :].rearrange("p a b -> p (a b)")[:, 0:NT * D].rearrange("p (t d) -> p t d", d=D)
            layer_norm_relu("l2", h_in, tmp, ALU.add, dmas=[
                (x_saved, x_flat), (vecs[:, :, :], vecs_in[:, 2 * D:].to_broadcast([P, (len(VECS) - 2) * D]))])
            s_back = sem("x_back")
            gat_sems = {}

            def gat_sem(name):
                if name not in gat_sems:
                    gat_sems[name] = sem(name)
                return gat_sems[name]

            for layer in range(3):
                if layer > 0:
                    for s in gat_sems.values():
                        nc.sync.sem_clear(s)
                    nc.all_engine_barrier()
                gat_layer(nc, gat_sem, dict(
                    adj=adj, psum=psum, ident=ident, o_all=o_all, hx=hx, ring=ring, rrow=rrow, oT=oT, row_table=row_table,
                    node=node, rr=rr, ext=ext, rT=rT[:, :], mx=x_flat[:, 0:2 * CW], layer=layer,
                    w=mat(f"G_W{layer + 1}"), a_src=vec(f"G_as{layer + 1}"), a_dst=vec(f"G_ad{layer + 1}"), bias=vec(f"G_b{layer + 1}"), tmp=tmp, over_tiles=over_tiles,
                    over_features=over_features, relu=(layer < 2), deg=deg, ones16=ones16))
            with nc.Block() as block:
                @block.sync
                def _(sp):
                    sp.dma_start(x_flat, x_saved).then_inc(s_back, 16)
                    sp.wait_ge(s_back, 16)
            add_residual(nc, sem("l2_residual"), x_sb, o_all, D)

        with ExitStack() as scope:
            h = sb("l3_h", [P, NT, D], FP32, scope)
            z = sb("l3_z", [P, NT, D], FP32, scope)
            hT = sb("l3_hT", [D, 2, CW], FP32, scope)
            agg = sb("l3_agg", [128, 2, CW], FP32, scope)
            bn = sb("l3_bn", [P, 3, D], FP32, scope)
            bound = sb("l3_bound", [P, 2, D], FP32, scope)
            inverse = sb("l3_inverse_bound", [P, D], FP32, scope)
            bound_col = sb("l3_bound_col", [128, 2], FP32, scope)

            def batch_norm_lrelu(tag, gamma, beta, scale_next=False):
                s_c, s_sq, s_sumsq, s_var, s_std = (sem(f"{tag}_{n}") for n in (
                    "bn_chain", "bn_squares", "bn_sum_squares", "bn_var", "bn_std"))
                if scale_next:
                    s_col = sem(f"{tag}_bound_transposed")
                with nc.Block() as block:
                    @block.tensor
                    def _(pe):
                        for t in range(NT):
                            if t % TC == 0:
                                pe.wait_ge(s_sq, t // TC + 1)
                            last = pe.matmul(psum[0:P, 1, 0:D], ones[0:P, 0:P], h[:, t, :], start=(t == 0), stop=(t == NT - 1))
                        last.then_inc(s_sumsq, 1)
                        if scale_next:
                            pe.wait_ge(s_c, 5 + 5)
                            pe.transpose(psum[:, 0, 0:P], bound[:, :, :].rearrange("p k d -> p (k d)"), ident[0:P, 0:P])\
                                .then_inc(s_col, 1)

                    @block.scalar
                    def _(act):
                        act.wait_ge(s_var, 1)
                        act.activation(bn[:, 2, :], bn[:, 1, :], ACT.Sqrt).then_inc(s_std, 1)

                    @block.vector
                    def _(dve):
                        v = nc.vector
                        link = Chain(dve, s_c)
                        for k, (bank, chunks) in enumerate(((5, 3), (4, NC - 3))):
                            chunk_sums = psum[0:P, bank, TC * D:(TC + chunks) * D].rearrange("p (c d) -> p d c", d=D)
                            link(v.tensor_reduce(bn[:, k, :], chunk_sums, AX.X, ALU.add))
                        link(v.tensor_scalar(bn[:, 0, :], bn[:, 0, :], 1.0 / N, None, ALU.mult))
                        link(v.scalar_tensor_tensor(bn[:, 0, :], bn[:, 1, :], 1.0 / N, bn[:, 0, :], ALU.mult, ALU.add))
                        link(v.tensor_tensor(z[:, :, :], z[:, :, :], over_tiles(bn[:, 0, :]), ALU.subtract))
                        for c in range(NC):
                            tiles = slice(c * TC, (c + 1) * TC)
                            v.tensor_tensor(h[:, tiles, :], z[:, tiles, :], z[:, tiles, :], ALU.mult).then_inc(s_sq, 1)
                        if scale_next:
                            b0, b1 = bound[:, 0, :], bound[:, 1, :]
                            link(v.scalar_tensor_tensor(b0, gamma, -1.0, gamma, ALU.mult, ALU.max))
                            link(v.scalar_tensor_tensor(b1, beta, -1.0, beta, ALU.mult, ALU.max))
                            link(v.scalar_tensor_tensor(b0, b0, float(int(N ** 0.5) + 1), b1, ALU.mult, ALU.add))
                            link(v.tensor_scalar(b0, b0, 1e-30, None, ALU.max))
                            link(v.tensor_copy(b1, b0))
                            link(v.reciprocal(inverse[:, :], b0))
                            dve.wait_ge(s_col, 1)
                            link(v.tensor_copy(bound_col[:, 0:1], psum[:, 0, 0:1]))
                            link(v.tensor_scalar(bound_col[:, 1:2], bound_col[:, 0:1], 1.0 / LO_SCALE, None, ALU.mult))
                            w = mats[:, MATS.index("S_neigh2"), :]
                            link(v.tensor_scalar(w[0:D], w[0:D], bound_col[0:D, 0:1], None, ALU.mult))
                            link(v.tensor_scalar(w[D:2 * D], w[D:2 * D], bound_col[D:2 * D, 1:2], None, ALU.mult))
                        dve.wait_ge(s_sumsq, 1)
                        v.tensor_scalar(bn[:, 1, :], psum[0:P, 1, 0:D], 1.0 / N, LN_EPS, ALU.mult, ALU.add).then_inc(s_var, 1)
                        dve.wait_ge(s_std, 1)
                        link(v.reciprocal(bn[:, 0, :], bn[:, 2, :]))
                        link(v.tensor_tensor(bn[:, 0, :], bn[:, 0, :], gamma, ALU.mult))
                        link(v.tensor_tensor(z[:, :, :], z[:, :, :], over_tiles(bn[:, 0, :]), ALU.mult))
                        link(v.tensor_tensor(z[:, :, :], z[:, :, :], over_tiles(beta), ALU.add))
                        link(v.scalar_tensor_tensor(h[:, :, :], z[:, :, :], 0.01, z[:, :, :], ALU.mult, ALU.max))

            parts = sb("l3_parts", [P, NT, 2 * D], FP16, scope)
            layer_norm_relu("l3", h[:, :, :], z[:, :, :], ALU.subtract)
            sage_layer("l3a", h[:, :, :], hT, agg, parts, None, z[:, :, :], vec("S_b1"), mat("S_neigh1", 128),
                       mat("S_self1"), True, column_sums=True)
            batch_norm_lrelu("l3a", vec("S_gamma1"), vec("S_beta1"), scale_next=True)
            sage_layer("l3b", h[:, :, :], hT, agg, parts, inverse[:, :], z[:, :, :], vec("S_b2"), mat("S_neigh2", 128),
                       mat("S_self2"), True, column_sums=True)
            batch_norm_lrelu("l3b", vec("S_gamma2"), vec("S_beta2"))
            add_residual(nc, sem("l3_residual"), x_sb, h)
        store(nc, sem, out, x_sb)


def gat_layer(nc, sem, b):
    adj, psum, ident, o_all, hx, ring, rrow, oT, node, rr, ext, row_table = (b[k] for k in (
        "adj", "psum", "ident", "o_all", "hx", "ring", "rrow", "oT", "node", "rr", "ext", "row_table"))
    a_s, a_d, a_unit, k_s, m_max, m_log, neg_a_s = (node[:, k, :] for k in range(7))
    h_in = o_all[:, :, 0:D]
    tag = "gat_"
    hT = rrow[0:D, 0, :, :]
    blocks = lambda bank: psum[:, bank:bank + 2, :].rearrange("p a b -> p (a b)").rearrange("p (t q) -> p t q", q=128)
    tiled = lambda row: row.rearrange("p (t q) -> p t q", q=P)

    s_t, s_tc, s_h, s_hc, s_c, s_ext, s_ext2 = (sem(tag + n) for n in (
        "transposed", "transpose_copied", "h_ready", "h_copied", "node_chain", "extremes", "extremes_all"))
    with nc.Block() as block:
        @block.tensor
        def _(pe):
            def transposes(c):
                if c >= 2:
                    pe.wait_ge(s_tc, c - 1)
                for t in range(TC):
                    last = pe.transpose(blocks(2 * (c % 2))[0:D, t, 0:P], h_in[:, c * TC + t, :], ident[0:P, 0:P])
                last.then_inc(s_t, 1)

            transposes(0)
            for c in range(NC):
                if c + 1 < NC:
                    transposes(c + 1)
                pe.wait_ge(s_tc, c + 1)
                if c >= 2:
                    pe.wait_ge(s_hc, c - 1)
                for t in range(TC):
                    last = pe.matmul(psum[0:P, 4 + c % 2, t * D:(t + 1) * D], hT[:, c % 2, t * P:(t + 1) * P], b["w"],
                                     start=True, stop=True)
                last.then_inc(s_h, 1)

        @block.scalar
        def _(act):
            for c in range(NC):
                act.wait_ge(s_t, c + 1)
                if c >= 2:
                    act.wait_ge(s_h, c - 1)
                act.activation(tiled(hT[:, c % 2, :]), blocks(2 * (c % 2))[0:D, 0:TC, 0:P], ACT.Copy).then_inc(s_tc, 1)

        @block.gpsimd
        def _(pool):
            pool.wait_ge(s_ext, 1)
            pool.partition_all_reduce(ext[0:P, 2:4], ext[0:P, 0:2], P, bass.bass_isa.ReduceOp.max).then_inc(s_ext2, 1)

        @block.vector
        def _(dve):
            v = nc.vector
            link = Chain(dve, s_c)
            link(v.memset(hx[:, :, D:D + 1], 1.0))
            for c in range(NC):
                tiles = slice(c * TC, (c + 1) * TC)
                hc = hx[:, tiles, 0:D]
                dve.wait_ge(s_h, c + 1)
                v.tensor_copy(hc, psum[0:P, 4 + c % 2, 0:TC * D].rearrange("p (t d) -> p t d", d=D)).then_inc(s_hc, 1)
                dve.wait_ge(s_hc, c + 1)
                link(v.tensor_tensor(b["tmp"][:, tiles, :], hc, b["over_tiles"](b["a_src"], TC), ALU.mult))
                link(v.tensor_reduce(a_s[:, tiles], b["tmp"][:, tiles, :], AX.X, ALU.add))
            link(v.tensor_reduce(ext[:, 0:1], a_s, AX.X, ALU.max))
            link(v.tensor_scalar(k_s, a_s, -1.0, None, ALU.mult))
            v.tensor_reduce(ext[:, 1:2], k_s, AX.X, ALU.max).then_inc(s_ext, 1)
            dve.wait_ge(s_ext2, 1)
            link(v.tensor_tensor(ext[:, 4:5], ext[:, 2:3], ext[:, 3:4], ALU.add))
            link(v.tensor_scalar(ext[:, 4:5], ext[:, 4:5], 1e-30, 2.0, ALU.max, ALU.mult))
            link(v.reciprocal(ext[:, 5:6], ext[:, 4:5]))
            link(v.tensor_scalar(a_unit, a_s, ext[:, 3:4], ext[:, 5:6], ALU.add, ALU.mult))
            link(v.tensor_scalar(a_unit, a_unit, 0.5, None, ALU.add))
            link(v.tensor_scalar(k_s, a_s, -0.8, None, ALU.mult))

    s_ad, s_m, s_mt, s_mr, s_mc, s_one, s_deg, s_rt, s_rtc, s_table = (sem(tag + n) for n in (
        "ad_products", "max_step", "max_transposed", "max_reduced", "max_chain", "ones16", "degrees_summed", "rows_transposed",
        "rows_copied", "row_table_stored"))
    mx = b["mx"]
    rT = b["rT"]

    def max_step(dve, k, out, dst):
        if isinstance(k, int) and k == 0:
            return nc.vector.tensor_scalar(out, adj[:, 0, dst], a_unit[:, 0:1], None, ALU.min)
        return nc.vector.scalar_tensor_tensor(out, adj[:, bass.ds(k, 1), dst].rearrange("p a q -> p (a q)"),
                                              a_unit[:, bass.ds(k, 1)], out, ALU.min, ALU.max)

    def shifts(link, first, count):
        tiles = slice(first * TC, (first + count) * TC)
        m, log, ad = m_max[:, tiles], m_log[:, tiles], a_d[:, tiles]
        v3 = lambda ap: ap.rearrange("p (c t) -> p c t", t=TC)
        r1, r2 = (rr[:, first:first + count, k, :] for k in range(2))
        v = nc.vector
        link(v.tensor_scalar(m, m, -0.5, ext[:, 4:5], ALU.add, ALU.mult))
        link(v.scalar_tensor_tensor(r2, v3(m), ext[:, 3:4], v3(ad), ALU.subtract, ALU.add))
        link(v.scalar_tensor_tensor(v3(log), r2, 0.2, r2, ALU.mult, ALU.max))
        link(v.tensor_tensor(r1, v3(ad), v3(log), ALU.subtract))
        link(v.scalar_tensor_tensor(r2, v3(ad), 0.2, v3(log), ALU.mult, ALU.subtract))

    with nc.Block() as block:
        @block.vector
        def _(dve):
            v = nc.vector
            both = slice(0, 2 * CW)
            max_step(dve, 0, mx, both).then_inc(s_m, 1)
            with dve.Fori(1, NT) as k:
                dve.wait_ge(s_m, k)
                max_step(dve, k, mx, both).then_inc(s_m, 1)
            link = Chain(dve, s_mc)
            dve.wait_ge(s_ad, 1)
            link(v.tensor_reduce(a_d, b["tmp"], AX.X, ALU.add))
            for c in range(2):
                dve.wait_ge(s_mt, c + 1)
                v.tensor_reduce(m_max[:, c * TC:(c + 1) * TC], blocks(2 * c)[0:P, 0:TC, 0:P], AX.X, ALU.max).then_inc(s_mr, 1)
            dve.wait_ge(s_mr, 2)
            shifts(link, 0, 2)
            link(v.tensor_scalar(neg_a_s, a_s, -1.0, None, ALU.mult))
            dve.wait_ge(s_deg, 1)
            deg, part = b["deg"][:, :], psum[0:P, 7, 0:NT]
            if b["layer"] == 0:
                link(v.tensor_scalar(deg, part, -1.0, None, ALU.add))
            else:
                link(v.tensor_tensor(deg, deg, part, ALU.add))
            if b["layer"] == 2:
                link(v.tensor_scalar(deg, deg, 1.0, None, ALU.max))
                link(v.reciprocal(deg, deg))

        @block.gpsimd
        def _(pool):
            if b["layer"] == 0:
                pool.memset(b["ones16"][:, :], 1.0).then_inc(s_one, 1)
            pool.tensor_tensor(b["tmp"], hx[:, :, 0:D], b["over_tiles"](b["a_dst"]), ALU.mult).then_inc(s_ad, 1)

        @block.tensor
        def _(pe):
            if b["layer"] == 0:
                pe.wait_ge(s_one, 1)
            first, last_k = b["layer"] * NT // 3, (b["layer"] + 1) * NT // 3 - 1

            def degrees(k):
                for t in range(NT):
                    last = pe.matmul(psum[0:P, 7, t:t + 1], adj[:, bass.ds(k, 1), t * P:(t + 1) * P]
                                     .rearrange("p a q -> p (a q)"), b["ones16"][:, 0:1],
                                     start=(isinstance(k, int) and k == first and t == 0),
                                     stop=(isinstance(k, int) and k == last_k and t == NT - 1), skip_group_check=True)
                return last

            degrees(first)
            with pe.Fori(first + 1, last_k) as k:
                degrees(k)
            degrees(last_k).then_inc(s_deg, 1)
            pe.wait_ge(s_m, NT)
            for c in range(2):
                for t in range(TC):
                    last = pe.transpose(blocks(2 * c)[0:P, t, 0:P], mx[:, c * CW + t * P:c * CW + (t + 1) * P],
                                        ident[0:P, 0:P])
                last.then_inc(s_mt, 1)
            pe.wait_ge(s_mc, 1 + 5)
            pe.transpose(psum[0:4 * TC, 6, 0:P], rr[:, 0:2, :, :].rearrange("p c k t -> p (c k t)"), ident[0:P, 0:P])\
                .then_inc(s_rt, 1)

        @block.scalar
        def _(act):
            act.wait_ge(s_rt, 1)
            act.activation(rT, psum[0:4 * TC, 6, 0:P], ACT.Copy).then_inc(s_rtc, 1)

        @block.sync
        def _(sp):
            sp.wait_ge(s_rtc, 1)
            sp.dma_start(row_table[0:2, :].rearrange("c (k q) -> (c k) q", q=P), rT).then_inc(s_table, 16)
            sp.wait_ge(s_table, 16)

    s_pre, s_exp, s_w, s_bound, s_wp, s_mm, s_oT, s_ot, s_oc = (sem(tag + n) for n in (
        "exponent_ready", "exp_ready", "weight_ready", "exponent_bounded", "pool_weight_ready", "product_done", "sums_copied",
        "sums_transposed", "sums_stored"))
    s_next, s_nt, s_nr, s_nc, s_nrt, s_nrc, s_nst = (sem(tag + n) for n in (
        "next_max_step", "next_max_transposed", "next_max_reduced", "next_max_chain", "next_rows_transposed",
        "next_rows_copied", "next_row_table_stored"))
    s_rows = [sem(tag + f"rows_in{k}") for k in range(2)]
    LAG = 2

    def pool_slots(c):
        return list(range(RING)) if c + 2 < NC else [1, 3]

    def dve_slots(c):
        return [s for s in range(RING) if s not in pool_slots(c)]

    def turn(slots, c, i, s):
        return sum(len(slots(a)) for a in range(c)) * (NT // RING) + i * len(slots(c)) + slots(c).index(s) + 1

    with nc.Block() as block:
        @block.sync
        def _(sp):
            for c in range(NC):
                if c >= 2:
                    sp.wait_ge(s_nrc, c - 1)
                    sp.dma_start(row_table[c:c + 1, :].rearrange("c (k q) -> (c k) q", q=P), rT[0:2 * TC, :]).then_inc(s_nst, 16)
                    sp.wait_ge(s_nst, 16 * (c - 1))
                    sp.wait_ge(s_pre, (c - 1) * NT)
                sp.dma_start(rrow[:, c % 2, :, :].rearrange("p k q -> p (k q)"), row_table[c:c + 1, :].to_broadcast([P, 2 * CW]))\
                    .then_inc(s_rows[c % 2], 16)

        @block.vector
        def _(dve):
            v = nc.vector
            link = Chain(dve, s_nc)

            def exponent(c, k, s):
                n = c * NT + k
                if not (c == 0 and isinstance(k, int)):
                    dve.wait_ge(s_mm, n - RING + 1)
                v.scalar_tensor_tensor(ring[:, s, :], rrow[:, c % 2, 1, :], k_s[:, bass.ds(k, 1)], rrow[:, c % 2, 0, :],
                                       ALU.add, ALU.max).then_inc(s_pre, 1)

            def weight(c, i, s):
                if s in pool_slots(c):
                    return
                k = i * RING + s
                dve.wait_ge(s_exp, c * NT + k + 1)
                v.scalar_tensor_tensor(ring[:, s, :], ring[:, s, :], 2.0, adj[:, bass.ds(k, 1), c * CW:(c + 1) * CW]
                                       .rearrange("p a q -> p (a q)"), ALU.min, ALU.mult).then_inc(s_w, 1)

            def next_max(c, k):
                if c + 2 >= NC:
                    return
                if not (isinstance(k, int) and k == 0):
                    dve.wait_ge(s_next, c * NT + k)
                elif c > 0:
                    dve.wait_ge(s_next, c * NT)
                half = c % 2
                max_step(dve, k, mx[:, half * CW:(half + 1) * CW], slice((c + 2) * CW, (c + 3) * CW)).then_inc(s_next, 1)

            def turns(c, lo, hi):
                with dve.Fori(lo, hi) as i:
                    for s in range(RING):
                        exponent(c, i * RING + s, s)
                        next_max(c, i * RING + s)
                        if s >= LAG:
                            weight(c, i, s - LAG)
                        else:
                            weight(c, i - 1, s - LAG + RING)

            for c in range(NC):
                dve.wait_ge(s_rows[c % 2], 16 * (c // 2 + 1))
                for s in range(RING):
                    exponent(c, s, s)
                    next_max(c, s)
                    if s >= LAG:
                        weight(c, 0, s - LAG)
                    elif c > 0:
                        weight(c - 1, NT // RING - 1, RING - LAG + s)
                turns(c, 1, 3)
                if 2 <= c + 1 < NC:
                    dve.wait_ge(s_nt, c)
                    v.tensor_reduce(m_max[:, (c + 1) * TC:(c + 2) * TC], blocks(4)[0:P, 0:TC, 0:P], AX.X, ALU.max)\
                        .then_inc(s_nr, 1)
                    dve.wait_ge(s_nr, c)
                    shifts(link, c + 1, 1)
                turns(c, 3, NT // RING)
            for s in range(RING - LAG, RING):
                weight(NC - 1, NT // RING - 1, s)

        @block.gpsimd
        def _(pool):
            for c in range(NC):
                def mask(k, s):
                    pool.wait_ge(s_exp, c * NT + k + 1)
                    pool.tensor_tensor(ring[:, s, :], ring[:, s, :], adj[:, bass.ds(k, 1), c * CW:(c + 1) * CW]
                                       .rearrange("p a q -> p (a q)"), ALU.mult).then_inc(s_wp, 1)

                with pool.Fori(0, NT // RING) as i:
                    for s in pool_slots(c):
                        mask(i * RING + s, s)

        @block.scalar
        def _(act):
            def exp(c, i, s):
                k = i * RING + s
                act.wait_ge(s_pre, c * NT + k + 1)
                if s in pool_slots(c):
                    act.activation(ring[:, s, :], ring[:, s, :], ACT.Relu, scale=-1.0,
                                   bias=neg_a_s[:, bass.ds(k, 1)]).then_inc(s_bound, 1)
                    act.wait_ge(s_bound, turn(pool_slots, c, i, s))
                    act.activation(ring[:, s, :], ring[:, s, :], ACT.Exp, scale=-1.0).then_inc(s_exp, 1)
                else:
                    act.activation(ring[:, s, :], ring[:, s, :], ACT.Exp, bias=a_s[:, bass.ds(k, 1)]).then_inc(s_exp, 1)

            def sums_out(c):
                act.wait_ge(s_mm, (c + 1) * NT)
                act.activation(tiled(oT[:, :]), blocks(2 * (c % 2))[0:D + 1, 0:TC, 0:P], ACT.Copy).then_inc(s_oT, 1)

            def sums_in(c):
                act.wait_ge(s_ot, c + 1)
                act.activation(o_all[:, c * TC:(c + 1) * TC, :],
                               psum[0:P, 6, 0:TC * (D + 1)].rearrange("p (t d) -> p t d", d=D + 1), ACT.Copy).then_inc(s_oc, 1)

            def turns(c, lo, hi):
                with act.Fori(lo, hi) as i:
                    for s in range(RING):
                        exp(c, i, s)

            for c in range(NC):
                for s in range(RING):
                    exp(c, 0, s)
                if c > 0:
                    sums_out(c - 1)
                turns(c, 1, 3)
                if c > 0:
                    sums_in(c - 1)
                for s in range(RING):
                    exp(c, 3, s)
                if 2 <= c + 1 < NC:
                    act.wait_ge(s_nrt, c)
                    if c > 1:
                        act.wait_ge(s_nst, 16 * (c - 1))
                    act.activation(rT[0:2 * TC, :], psum[0:2 * TC, 7, 0:P], ACT.Copy).then_inc(s_nrc, 1)
                for s in range(RING):
                    exp(c, 4, s)
            sums_out(NC - 1)
            sums_in(NC - 1)

        @block.tensor
        def _(pe):
            def product(c, k):
                i, s = divmod(k, RING)
                if s in pool_slots(c):
                    pe.wait_ge(s_wp, turn(pool_slots, c, i, s))
                else:
                    pe.wait_ge(s_w, turn(dve_slots, c, i, s))
                o = blocks(2 * (c % 2))
                for out_part, weights in ((o[0:D + 1, 0:4, 0:P], tiled(ring[:, s, 0:4 * P])),
                                          (o[0:D + 1, 4, 0:P], ring[:, s, 4 * P:])):
                    last = pe.matmul(out_part, hx[:, k, :], weights, start=(k == 0), stop=(k == NT - 1),
                                     skip_group_check=True)
                last.then_inc(s_mm, 1)

            def transposes(c):
                pe.wait_ge(s_oT, c + 1)
                if c > 0:
                    pe.wait_ge(s_oc, c)
                for t in range(TC):
                    last = pe.transpose(psum[0:P, 6, t * (D + 1):(t + 1) * (D + 1)], oT[:, t * P:(t + 1) * P],
                                        ident[0:D + 1, 0:D + 1])
                last.then_inc(s_ot, 1)

            for c in range(NC):
                if c >= 2:
                    pe.wait_ge(s_oT, c - 1)
                for k in range(NT):
                    product(c, k)
                    if 2 <= c + 1 < NC and k == RING - 1:
                        pe.wait_ge(s_next, c * NT)
                        half = (c + 1) % 2
                        for t in range(TC):
                            last = pe.transpose(blocks(4)[0:P, t, 0:P], mx[:, half * CW + t * P:half * CW + (t + 1) * P],
                                                ident[0:P, 0:P])
                        last.then_inc(s_nt, 1)
                    if c > 0 and k == 2 * RING:
                        transposes(c - 1)
                    if 2 <= c + 1 < NC and k == NT - 8:
                        pe.wait_ge(s_nc, 5 * c)
                        pe.transpose(psum[0:2 * TC, 7, 0:P], rr[:, c + 1, :, :].rearrange("p k t -> p (k t)"), ident[0:P, 0:P])\
                            .then_inc(s_nrt, 1)
            transposes(NC - 1)

    s_n = sem(tag + "normalise_chain")
    with nc.Block() as block:
        @block.vector
        def _(dve):
            v = nc.vector
            link = Chain(dve, s_n)
            link(v.tensor_scalar(m_max, o_all[:, :, D], 1e-16, None, ALU.add))
            link(v.reciprocal(m_log, m_max))
            link(v.tensor_tensor(h_in, h_in, b["over_features"](m_log), ALU.mult))
            link(v.tensor_tensor(h_in, h_in, b["over_tiles"](b["bias"]), ALU.add))
            if b["relu"]:
                link(v.tensor_scalar(h_in, h_in, 0.0, None, ALU.max))


def add_residual(nc, s_res, x_sb, z, width=D):
    with nc.Block() as block:
        @block.vector
        def _(dve):
            nc.vector.tensor_tensor(x_sb[:, :, :], x_sb[:, :, :], z[:, :, 0:width], ALU.add).then_inc(s_res, 1)
            dve.wait_ge(s_res, 1)


def store(nc, sem, out, x_sb):
    s_out = sem("out_stored")
    with nc.Block() as block:
        @block.sync
        def _(sp):
            sp.dma_start(out, x_sb[:, :, :]).then_inc(s_out, 16)
            sp.wait_ge(s_out, 16)


def kernel(**inputs):
    import numpy as np
    import concourse.bacc as bacc
    from concourse.bass_utils import run_bass_kernel_spmd

    a = {k: np.asarray(v) for k, v in inputs.items()}

    def edges(v, pad):
        return np.concatenate([v, np.full(G * GE - E, pad, v.dtype)])

    def tiles(v, pad):
        return np.ascontiguousarray(edges(v, pad).reshape(G * GT, ET).T)

    def groups(v, pad):
        rows = np.full((2 * 128, GE), pad, v.dtype)
        rows[:G] = edges(v, pad).reshape(G, GE)
        return rows.reshape(2, 128, GE).transpose(1, 0, 2)

    mats = [a["L0_gnn_W1l"].T, a["L0_gnn_W1r"].T, a["L0_gnn_W2l"].T, a["L0_gnn_W2r"].T,
            a["L2_gnn_W1"], a["L2_gnn_W2"], a["L2_gnn_W3"],
            a["L3_gnn_W_self1"].T, a["L3_gnn_W_neigh1"].T, a["L3_gnn_W_self2"].T, a["L3_gnn_W_neigh2"].T]
    vecs = [a[k] for k in ("L0_gnn_b1l", "L0_gnn_b2l", "L2_gnn_a1s", "L2_gnn_a2s", "L2_gnn_a3s", "L2_gnn_a1d",
                           "L2_gnn_a2d", "L2_gnn_a3d", "L2_gnn_b1", "L2_gnn_b2", "L2_gnn_b3", "L3_gnn_b1",
                           "L3_gnn_gamma1", "L3_gnn_beta1", "L3_gnn_b2", "L3_gnn_gamma2", "L3_gnn_beta2")]
    arrays = {
        "x": a["x"].reshape(NT, P, D).transpose(1, 0, 2),
        "dst_groups": groups(a["dst"], PAD_DST),
        "src_groups": groups(a["src"], 0),
        "src_tiles": tiles(a["src"], 0),
        "dst_tiles": tiles(a["dst"], PAD_DST),
        "type_tiles": tiles(a["edge_type_16"], 0),
        "mats": np.stack(mats, axis=1),
        "vecs": np.concatenate(vecs)[None],
        "rel": a["L1_gnn_weight"].transpose(1, 0, 2).reshape(D, R * D),
    }
    arrays = {"in_" + k: np.ascontiguousarray(v) for k, v in arrays.items()}
    nc = bacc.Bacc("TRN2", target_bir_lowering=False, num_devices=1)
    args = [nc.dram_tensor(k, v.shape, mybir.dt.from_np(v.dtype), kind="ExternalInput").ap() for k, v in arrays.items()]
    out = nc.dram_tensor("out", (P, NT, D), FP32, kind="ExternalOutput").ap()
    gnn(nc, *args, out)
    r = run_bass_kernel_spmd(nc, [arrays], core_ids=[0])
    return np.ascontiguousarray(np.asarray(r.results[0]["out"]).reshape(P, NT, D).transpose(1, 0, 2).reshape(N, D))
```
